# Optimizing a Trainium2 kernel written in Bass

```python
import numpy as np
import jax
import jax.numpy as jnp

def _softmax(x, axis=-1):
    return jax.nn.softmax(x, axis=axis)

def _gelu(x):
    return jax.nn.gelu(x, approximate=True)

def _silu(x):
    return jax.nn.silu(x)

def _sigmoid(x):
    return jax.nn.sigmoid(x)

def _layernorm(x, axis=-1, eps=1e-05):
    m = jnp.mean(x, axis=axis, keepdims=True)
    v = jnp.var(x, axis=axis, keepdims=True)
    return (x - m) / jnp.sqrt(v + eps)

def _scatter_add(tgt, idx, src, axis=0):
    return tgt.at[idx].add(src)

def _segment_sum(src, seg, n):
    return jax.ops.segment_sum(src, seg, n)
kernel_name = 'mk_sandwich_d4_jaxref_r8_61e971'

def setup_inputs(seed: int=0):
    np.random.seed(seed)
    _w = jnp.asarray

    def _L0_attn_setup():
        import jax, jax.numpy as jnp
        import numpy as np
        B, S, D = (2, 256, 128)
        H = 16
        DK = 128
        DV = 128
        EPS = 1e-05
        key = jax.random.key(seed)
        k1, k2, k3, k4 = jax.random.split(key, 4)
        x = jax.random.normal(k1, (B, S, D), dtype=jnp.float32)
        Wq = jax.random.normal(k2, (DK, D), dtype=jnp.float32) * 0.02
        Wk = jax.random.normal(k3, (DK, D), dtype=jnp.float32) * 0.02
        Wv = jax.random.normal(k4, (DV, D), dtype=jnp.float32) * 0.02
        return {'x': x, 'Wq': Wq, 'Wk': Wk, 'Wv': Wv}
    _L0_attn_in = _L0_attn_setup()

    def _L0_ffn_setup():
        import jax, jax.numpy as jnp
        import numpy as np
        DIM = 128

        def _reference_tuple_inner(x, W_r, W_k, W_v, mu_r, mu_k):
            B, T, C = x.shape
            x_prev = jnp.concatenate([jnp.zeros((B, 1, C), x.dtype), x[:, :-1, :]], axis=1)
            xr = mu_r * x + (1.0 - mu_r) * x_prev
            xk = mu_k * x + (1.0 - mu_k) * x_prev
            r = jax.nn.sigmoid(jnp.einsum('btc,dc->btd', xr, W_r))
            k = jnp.einsum('btc,dc->btd', xk, W_k)
            k_act = jnp.square(jax.nn.relu(k))
            out = r * jnp.einsum('btc,dc->btd', k_act, W_v)
            new_state = x[:, -1, :]
            return (out, new_state)
        key = jax.random.key(seed)
        ks = jax.random.split(key, 6)
        B, T, C = (8, 256, DIM)
        x = jax.random.normal(ks[0], (B, T, C), dtype=jnp.float32)
        s = 1.0 / np.sqrt(C)
        W_r = jax.random.uniform(ks[1], (C, C), jnp.float32, -s, s)
        W_k = jax.random.uniform(ks[2], (C, C), jnp.float32, -s, s)
        W_v = jax.random.uniform(ks[3], (C, C), jnp.float32, -s, s)
        mu_r = jax.random.uniform(ks[4], (C,), jnp.float32)
        mu_k = jax.random.uniform(ks[5], (C,), jnp.float32)
        return {'x': x, 'W_r': W_r, 'W_k': W_k, 'W_v': W_v, 'mu_r': mu_r, 'mu_k': mu_k}
    _L0_ffn_in = _L0_ffn_setup()

    def _L1_attn_setup():
        import jax, jax.numpy as jnp
        import numpy as np
        T, N, D, H = (128, 32, 128, 128)
        LR = 0.001

        def _recon(params, z):
            W1, b1, W2, b2 = params
            h = jax.nn.gelu(z @ W1.T + b1, approximate=False)
            return z + h @ W2.T + b2
        key = jax.random.key(seed)
        ks = jax.random.split(key, 6)
        sd = 1.0 / np.sqrt(D)
        sh = 1.0 / np.sqrt(H)
        s4 = 1.0 / np.sqrt(H // 4)
        return {'in_seq': jax.random.normal(ks[0], (T, N, D), jnp.float32), 't_k': jax.random.normal(ks[1], (H, D), jnp.float32) * sd, 't_v': jax.random.normal(ks[2], (H, D), jnp.float32) * sd, 't_q': jax.random.normal(ks[3], (H, D), jnp.float32) * sd, 'W1': jax.random.normal(ks[4], (H // 4, H), jnp.float32) * sh, 'b1': jnp.zeros((H // 4,), jnp.float32), 'W2': jax.random.normal(ks[5], (H, H // 4), jnp.float32) * s4, 'b2': jnp.zeros((H,), jnp.float32)}
    _L1_attn_in = _L1_attn_setup()

    def _L1_ffn_setup():
        import jax, jax.numpy as jnp
        import numpy as np
        D_MODEL = 128
        EXPERT_DIM = 512
        N_EXPERTS = 8
        CAP_FACTOR = 0.5
        key = jax.random.key(seed)
        ks = jax.random.split(key, 7)
        inp = {'input': jax.random.normal(ks[0], (4, 512, D_MODEL), dtype=jnp.float32), 'w_switch': jax.random.normal(ks[1], (D_MODEL, N_EXPERTS), dtype=jnp.float32) * 0.02, 'b_switch': jnp.zeros((N_EXPERTS,), jnp.float32), 'w1': jax.random.normal(ks[2], (N_EXPERTS, D_MODEL, EXPERT_DIM), dtype=jnp.float32) * 0.02, 'b1': jnp.zeros((N_EXPERTS, EXPERT_DIM), jnp.float32), 'w2': jax.random.normal(ks[3], (N_EXPERTS, EXPERT_DIM, D_MODEL), dtype=jnp.float32) * 0.02, 'b2': jnp.zeros((N_EXPERTS, D_MODEL), jnp.float32)}
        return inp
    _L1_ffn_in = _L1_ffn_setup()

    def _L2_attn_setup():
        import jax, jax.numpy as jnp
        import numpy as np
        NUM_HEADS = 16
        EPS = 1e-06
        L2_EPS = 1e-12

        def _l2_normalize(x):
            n = jnp.linalg.norm(x, axis=-1, keepdims=True)
            return x / jnp.maximum(n, L2_EPS)
        key = jax.random.key(seed)
        k1, k2 = jax.random.split(key)
        x = jax.random.normal(k1, (2, 1024, 128), dtype=jnp.float32)
        W_qkv = jax.random.normal(k2, (384, 128), dtype=jnp.float32) * 0.02
        return {'x': x, 'W_qkv': W_qkv}
    _L2_attn_in = _L2_attn_setup()

    def _L2_ffn_setup():
        import jax, jax.numpy as jnp
        import numpy as np
        B, S, D = (4, 512, 128)
        DD = 4 * D
        N_EXPERTS = 8
        CAPACITY = 1.0
        LN_EPS = 1e-05
        key = jax.random.key(seed)
        ks = jax.random.split(key, 8)
        s1 = 1.0 / np.sqrt(D)
        s2 = 1.0 / np.sqrt(DD)
        return {'x': jax.random.normal(ks[0], (B, S, D), jnp.float32), 'gate_w': jax.random.normal(ks[1], (N_EXPERTS, D), jnp.float32) * 0.02, 'ln_w': jnp.ones((D,), jnp.float32), 'ln_b': jnp.zeros((D,), jnp.float32), 'fc1s': jax.random.normal(ks[2], (N_EXPERTS, DD, D), jnp.float32) * s1, 'b1s': jax.random.normal(ks[3], (N_EXPERTS, DD), jnp.float32) * s1, 'fc2s': jax.random.normal(ks[4], (N_EXPERTS, D, DD), jnp.float32) * s2, 'b2s': jax.random.normal(ks[5], (N_EXPERTS, D), jnp.float32) * s2}
    _L2_ffn_in = _L2_ffn_setup()

    def _L3_attn_setup():
        import jax, jax.numpy as jnp
        import numpy as np
        B, T, D = (4, 256, 128)
        NHEAD = 16
        HEAD_DIM = D // NHEAD

        def _rope_cache(seq_len, dim):
            inv_freq = 1.0 / 10000.0 ** (jnp.arange(0, dim, 2, dtype=jnp.float32) / dim)
            t = jnp.arange(seq_len, dtype=jnp.float32)
            freqs = jnp.outer(t, inv_freq)
            return (jnp.cos(freqs), jnp.sin(freqs))

        def _apply_rope(x, cos, sin):
            d2 = x.shape[-1] // 2
            x1, x2 = (x[..., :d2], x[..., d2:])
            cos = cos[None, None]
            sin = sin[None, None]
            return jnp.concatenate([x1 * cos - x2 * sin, x2 * cos + x1 * sin], axis=-1)
        key = jax.random.key(seed)
        ks = jax.random.split(key, 5)
        s = 1.0 / np.sqrt(D)
        x = jax.random.normal(ks[0], (B, T, D), dtype=jnp.float32)
        Wqkv = jax.random.uniform(ks[1], (3 * D, D), jnp.float32, -s, s)
        bqkv = jax.random.uniform(ks[2], (3 * D,), jnp.float32, -s, s)
        Wout = jax.random.uniform(ks[3], (D, D), jnp.float32, -s, s)
        bout = jax.random.uniform(ks[4], (D,), jnp.float32, -s, s)
        return {'x': x, 'Wqkv': Wqkv, 'bqkv': bqkv, 'Wout': Wout, 'bout': bout}
    _L3_attn_in = _L3_attn_setup()

    def _L3_ffn_setup():
        import jax, jax.numpy as jnp
        import numpy as np
        B, S, D, F, E = (4, 256, 128, 512, 4)
        key = jax.random.key(seed)
        ks = jax.random.split(key, 8)
        sd = 1.0 / np.sqrt(D)
        sf = 1.0 / np.sqrt(F)
        return {'x': jax.random.normal(ks[0], (B, S, D), dtype=jnp.float32), 'W1': jax.random.uniform(ks[1], (E, D, F), jnp.float32, -sd, sd), 'b1': jax.random.uniform(ks[2], (E, F), jnp.float32, -sd, sd), 'W2': jax.random.uniform(ks[3], (E, F, D), jnp.float32, -sf, sf), 'b2': jax.random.uniform(ks[4], (E, D), jnp.float32, -sf, sf), 'Wu': jax.random.uniform(ks[5], (D, 1), jnp.float32, -sd, sd), 'bu': jax.random.uniform(ks[6], (1,), jnp.float32, -sd, sd)}
    _L3_ffn_in = _L3_ffn_setup()
    _d = {'L0_attn_x': _L0_attn_in['x'], 'L0_attn_Wq': _L0_attn_in['Wq'], 'L0_attn_Wk': _L0_attn_in['Wk'], 'L0_attn_Wv': _L0_attn_in['Wv'], 'L0_ffn_W_r': _L0_ffn_in['W_r'], 'L0_ffn_W_k': _L0_ffn_in['W_k'], 'L0_ffn_W_v': _L0_ffn_in['W_v'], 'L0_ffn_mu_r': _L0_ffn_in['mu_r'], 'L0_ffn_mu_k': _L0_ffn_in['mu_k'], 'L1_attn_t_k': _L1_attn_in['t_k'], 'L1_attn_t_v': _L1_attn_in['t_v'], 'L1_attn_t_q': _L1_attn_in['t_q'], 'L1_attn_W1': _L1_attn_in['W1'], 'L1_attn_b1': _L1_attn_in['b1'], 'L1_attn_W2': _L1_attn_in['W2'], 'L1_attn_b2': _L1_attn_in['b2'], 'L1_ffn_w_switch': _L1_ffn_in['w_switch'], 'L1_ffn_b_switch': _L1_ffn_in['b_switch'], 'L1_ffn_w1': _L1_ffn_in['w1'], 'L1_ffn_b1': _L1_ffn_in['b1'], 'L1_ffn_w2': _L1_ffn_in['w2'], 'L1_ffn_b2': _L1_ffn_in['b2'], 'L2_attn_W_qkv': _L2_attn_in['W_qkv'], 'L2_ffn_gate_w': _L2_ffn_in['gate_w'], 'L2_ffn_ln_w': _L2_ffn_in['ln_w'], 'L2_ffn_ln_b': _L2_ffn_in['ln_b'], 'L2_ffn_fc1s': _L2_ffn_in['fc1s'], 'L2_ffn_b1s': _L2_ffn_in['b1s'], 'L2_ffn_fc2s': _L2_ffn_in['fc2s'], 'L2_ffn_b2s': _L2_ffn_in['b2s'], 'L3_attn_Wqkv': _L3_attn_in['Wqkv'], 'L3_attn_bqkv': _L3_attn_in['bqkv'], 'L3_attn_Wout': _L3_attn_in['Wout'], 'L3_attn_bout': _L3_attn_in['bout'], 'L3_ffn_W1': _L3_ffn_in['W1'], 'L3_ffn_b1': _L3_ffn_in['b1'], 'L3_ffn_W2': _L3_ffn_in['W2'], 'L3_ffn_b2': _L3_ffn_in['b2'], 'L3_ffn_Wu': _L3_ffn_in['Wu'], 'L3_ffn_bu': _L3_ffn_in['bu']}
    _x0 = _d['L0_attn_x']
    _d['L0_attn_x'] = jax.random.normal(jax.random.fold_in(jax.random.key(seed), 1), (8, 512, 128), dtype=_x0.dtype)
    del _x0
    return _d

def reference(L0_attn_x, L0_attn_Wq, L0_attn_Wk, L0_attn_Wv, L0_ffn_W_r, L0_ffn_W_k, L0_ffn_W_v, L0_ffn_mu_r, L0_ffn_mu_k, L1_attn_t_k, L1_attn_t_v, L1_attn_t_q, L1_attn_W1, L1_attn_b1, L1_attn_W2, L1_attn_b2, L1_ffn_w_switch, L1_ffn_b_switch, L1_ffn_w1, L1_ffn_b1, L1_ffn_w2, L1_ffn_b2, L2_attn_W_qkv, L2_ffn_gate_w, L2_ffn_ln_w, L2_ffn_ln_b, L2_ffn_fc1s, L2_ffn_b1s, L2_ffn_fc2s, L2_ffn_b2s, L3_attn_Wqkv, L3_attn_bqkv, L3_attn_Wout, L3_attn_bout, L3_ffn_W1, L3_ffn_b1, L3_ffn_W2, L3_ffn_b2, L3_ffn_Wu, L3_ffn_bu):

    def _L0_attn_ref(x, Wq, Wk, Wv):
        import jax, jax.numpy as jnp
        import numpy as np
        B, S, D = (2, 256, 128)
        H = 16
        DK = 128
        DV = 128
        EPS = 1e-05
        b, s, d = x.shape
        dkh = DK // H
        dvh = DV // H
        Q = (x @ Wq.T).reshape(H, b, s, dkh)
        K = (x @ Wk.T).reshape(H, b, s, dkh)
        V = (x @ Wv.T).reshape(H, b, s, dvh)
        scores = jnp.einsum('hbqd,hbkd->hbqk', Q, K)
        atten = jax.nn.softmax(scores, axis=-1)
        out = jnp.einsum('hbqk,hbkd->hbqd', atten, V).reshape(b, s, -1)
        y = out + x
        mu = jnp.mean(y, axis=(1, 2), keepdims=True)
        var = jnp.var(y, axis=(1, 2), keepdims=True)
        return (y - mu) / jnp.sqrt(var + EPS)

    def _L0_ffn_ref(x, W_r, W_k, W_v, mu_r, mu_k):
        import jax, jax.numpy as jnp
        import numpy as np
        DIM = 128

        def _reference_tuple_inner(x, W_r, W_k, W_v, mu_r, mu_k):
            B, T, C = x.shape
            x_prev = jnp.concatenate([jnp.zeros((B, 1, C), x.dtype), x[:, :-1, :]], axis=1)
            xr = mu_r * x + (1.0 - mu_r) * x_prev
            xk = mu_k * x + (1.0 - mu_k) * x_prev
            r = jax.nn.sigmoid(jnp.einsum('btc,dc->btd', xr, W_r))
            k = jnp.einsum('btc,dc->btd', xk, W_k)
            k_act = jnp.square(jax.nn.relu(k))
            out = r * jnp.einsum('btc,dc->btd', k_act, W_v)
            new_state = x[:, -1, :]
            return (out, new_state)
        return _reference_tuple_inner(x, W_r, W_k, W_v, mu_r, mu_k)[0]

    def _L1_attn_ref(in_seq, t_k, t_v, t_q, W1, b1, W2, b2):
        import jax, jax.numpy as jnp
        import numpy as np
        T, N, D, H = (128, 32, 128, 128)
        LR = 0.001

        def _recon(params, z):
            W1, b1, W2, b2 = params
            h = jax.nn.gelu(z @ W1.T + b1, approximate=False)
            return z + h @ W2.T + b2

        def loss_fn(params, z, y):
            return jnp.mean((_recon(params, z) - y) ** 2)

        def step(params, x):
            z = x @ t_k.T
            y = x @ t_v.T
            grads = jax.grad(loss_fn)(params, z, y)
            new_params = jax.tree_util.tree_map(lambda p, g: jax.lax.stop_gradient(p - LR * g), params, grads)
            out = _recon(new_params, x @ t_q.T)
            return (new_params, out)
        _, outs = jax.lax.scan(step, (W1, b1, W2, b2), in_seq)
        return outs

    def _L1_ffn_ref(input, w_switch, b_switch, w1, b1, w2, b2):
        import jax, jax.numpy as jnp
        import numpy as np
        D_MODEL = 128
        EXPERT_DIM = 512
        N_EXPERTS = 8
        CAP_FACTOR = 0.5
        B, S, D = input.shape
        T = B * S
        E = b_switch.shape[0]
        capacity = int(CAP_FACTOR * T / E)
        x = input.reshape(T, D)
        logits = x @ w_switch + b_switch
        probs = jax.nn.softmax(logits, axis=-1)
        pmax = probs.max(axis=-1)
        routes = probs.argmax(axis=-1)
        oh = (routes[:, None] == jnp.arange(E)[None, :]).astype(jnp.int32)
        pos = (jnp.cumsum(oh, axis=0) * oh).sum(-1) - 1
        keep = pos < capacity
        slot = jnp.where(keep, routes * capacity + pos, E * capacity)
        buf = jnp.zeros((E * capacity + 1, D), x.dtype).at[slot].set(x)
        buf_e = buf[:E * capacity].reshape(E, capacity, D)
        h = jax.nn.relu(jnp.einsum('ecd,edh->ech', buf_e, w1) + b1[:, None, :])
        y = jnp.einsum('ech,ehd->ecd', h, w2) + b2[:, None, :]
        y_flat = jnp.concatenate([y.reshape(E * capacity, D), jnp.zeros((1, D), x.dtype)], axis=0)
        out = jnp.where(keep[:, None], y_flat[slot], x)
        scale = pmax / jax.lax.stop_gradient(pmax)
        out = out * scale[:, None]
        return out.reshape(B, S, D)

    def _L2_attn_ref(x, W_qkv):
        import jax, jax.numpy as jnp
        import numpy as np
        NUM_HEADS = 16
        EPS = 1e-06
        L2_EPS = 1e-12

        def _l2_normalize(x):
            n = jnp.linalg.norm(x, axis=-1, keepdims=True)
            return x / jnp.maximum(n, L2_EPS)
        b, n, dim = x.shape
        h = NUM_HEADS
        d = dim // h
        scale = d ** (-0.5)
        qkv = x @ W_qkv.T
        q, k, v = jnp.split(qkv, 3, axis=-1)
        to_heads = lambda t: t.reshape(b, n, h, d).transpose(0, 2, 1, 3)
        q, k, v = (to_heads(q), to_heads(k), to_heads(v))
        q = jax.nn.softplus(_l2_normalize(q))
        k = jax.nn.softplus(_l2_normalize(k))
        kv = jnp.einsum('bhnd,bhnc->bhdc', k, v) * scale
        ksum = jnp.sum(k, axis=2) + EPS
        norm = 1.0 / jnp.einsum('bhnd,bhd->bhn', q, ksum)
        out = jnp.einsum('bhnd,bhdc,bhn->bhnc', q, kv, norm)
        return out.transpose(0, 2, 1, 3).reshape(b, n, dim)

    def _L2_ffn_ref(x, gate_w, ln_w, ln_b, fc1s, b1s, fc2s, b2s):
        import jax, jax.numpy as jnp
        import numpy as np
        B, S, D = (4, 512, 128)
        DD = 4 * D
        N_EXPERTS = 8
        CAPACITY = 1.0
        LN_EPS = 1e-05
        og_shape = x.shape
        d = og_shape[-1]
        xf = x.reshape(-1, d)
        bs = xf.shape[0]
        n = gate_w.shape[0]
        k = int(bs * CAPACITY) // n
        scores = jax.nn.softmax(xf @ gate_w.T, axis=-1)
        vals, idx = jax.lax.top_k(scores.T, k)
        kept_w = vals.T
        kept_idx = idx.T
        flat_idx = kept_idx.reshape(-1)
        y = xf[flat_idx].reshape(k, n, d)
        mu = y.mean(-1, keepdims=True)
        var = ((y - mu) ** 2).mean(-1, keepdims=True)
        y = (y - mu) * jax.lax.rsqrt(var + LN_EPS) * ln_w + ln_b
        h = jnp.einsum('knd,nfd->knf', y, fc1s) + b1s
        h = jax.nn.gelu(h, approximate=True)
        out = jnp.einsum('knf,ndf->knd', h, fc2s) + b2s
        out = out * kept_w[..., None]
        xf = xf.at[flat_idx].add(out.reshape(k * n, d))
        return xf.reshape(og_shape)

    def _L3_attn_ref(x, Wqkv, bqkv, Wout, bout):
        import jax, jax.numpy as jnp
        import numpy as np
        B, T, D = (4, 256, 128)
        NHEAD = 16
        HEAD_DIM = D // NHEAD

        def _rope_cache(seq_len, dim):
            inv_freq = 1.0 / 10000.0 ** (jnp.arange(0, dim, 2, dtype=jnp.float32) / dim)
            t = jnp.arange(seq_len, dtype=jnp.float32)
            freqs = jnp.outer(t, inv_freq)
            return (jnp.cos(freqs), jnp.sin(freqs))

        def _apply_rope(x, cos, sin):
            d2 = x.shape[-1] // 2
            x1, x2 = (x[..., :d2], x[..., d2:])
            cos = cos[None, None]
            sin = sin[None, None]
            return jnp.concatenate([x1 * cos - x2 * sin, x2 * cos + x1 * sin], axis=-1)
        b, t, d = x.shape
        qkv = x @ Wqkv.T + bqkv
        qkv = qkv.reshape(b, t, 3, NHEAD, HEAD_DIM).transpose(2, 0, 3, 1, 4)
        q, k, v = (qkv[0], qkv[1], qkv[2])
        cos, sin = _rope_cache(t, HEAD_DIM)
        q = _apply_rope(q, cos, sin)
        k = _apply_rope(k, cos, sin)
        scale = jnp.sqrt(jnp.float32(HEAD_DIM))
        attn = jnp.einsum('bhqd,bhkd->bhqk', q, k) / scale
        attn = jax.nn.softmax(attn, axis=-1)
        out = jnp.einsum('bhqk,bhkd->bhqd', attn, v)
        out = out.transpose(0, 2, 1, 3).reshape(b, t, d)
        return out @ Wout.T + bout

    def _L3_ffn_ref(x, W1, b1, W2, b2, Wu, bu):
        import jax, jax.numpy as jnp
        import numpy as np
        B, S, D, F, E = (4, 256, 128, 512, 4)
        n_exp = W1.shape[0]
        seq = x.shape[1]
        u = jax.nn.sigmoid(jnp.einsum('bsd,do->bso', x, Wu) + bu)[..., 0]
        k = jnp.clip(jnp.ceil(u * n_exp), 1, n_exp).astype(jnp.int32)
        h = jax.nn.relu(jnp.einsum('bsd,edf->bsef', x, W1) + b1)
        y = jnp.einsum('bsef,efd->bsed', h, W2) + b2
        s_idx = jnp.arange(seq)
        out = jnp.zeros_like(x)
        for i in range(1, n_exp + 1):
            e_idx = (s_idx + i - 1) % n_exp
            y_i = jnp.take_along_axis(y, e_idx[None, :, None, None], axis=2)[:, :, 0, :]
            w = jnp.where(k >= i, u / i, 0.0)
            out = out + w[..., None] * y_i
        return out
    x = L0_attn_x
    x = x + _layernorm(_L0_attn_ref(_layernorm(x, axis=-1), L0_attn_Wq, L0_attn_Wk, L0_attn_Wv), axis=-1)
    x = x + _layernorm(_L0_ffn_ref(_layernorm(x, axis=-1), L0_ffn_W_r, L0_ffn_W_k, L0_ffn_W_v, L0_ffn_mu_r, L0_ffn_mu_k), axis=-1)
    x = x + _layernorm(_L1_attn_ref(_layernorm(x, axis=-1), L1_attn_t_k, L1_attn_t_v, L1_attn_t_q, L1_attn_W1, L1_attn_b1, L1_attn_W2, L1_attn_b2), axis=-1)
    x = x + _layernorm(_L1_ffn_ref(_layernorm(x, axis=-1), L1_ffn_w_switch, L1_ffn_b_switch, L1_ffn_w1, L1_ffn_b1, L1_ffn_w2, L1_ffn_b2), axis=-1)
    x = x + _layernorm(_L2_attn_ref(_layernorm(x, axis=-1), L2_attn_W_qkv), axis=-1)
    x = x + _layernorm(_L2_ffn_ref(_layernorm(x, axis=-1), L2_ffn_gate_w, L2_ffn_ln_w, L2_ffn_ln_b, L2_ffn_fc1s, L2_ffn_b1s, L2_ffn_fc2s, L2_ffn_b2s), axis=-1)
    x = x + _layernorm(_L3_attn_ref(_layernorm(x, axis=-1), L3_attn_Wqkv, L3_attn_bqkv, L3_attn_Wout, L3_attn_bout), axis=-1)
    x = x + _layernorm(_L3_ffn_ref(_layernorm(x, axis=-1), L3_ffn_W1, L3_ffn_b1, L3_ffn_W2, L3_ffn_b2, L3_ffn_Wu, L3_ffn_bu), axis=-1)
    return x

_drawn_inputs = setup_inputs


def setup_inputs(seed=0):
    import zlib

    import numpy as np

    out = dict(_drawn_inputs(seed))
    spreads = {'L1_attn_b1': (0.0, 0.1),
     'L1_attn_b2': (0.0, 0.1),
     'L1_ffn_b_switch': (0.0, 0.1),
     'L1_ffn_b1': (0.0, 0.1),
     'L1_ffn_b2': (0.0, 0.1),
     'L2_ffn_ln_w': (1.0, 0.6),
     'L2_ffn_ln_b': (0.0, 2.0)}
    factors = {'L0_attn_Wq': 4.916,
     'L0_attn_Wk': 6.591,
     'L1_attn_t_k': 8.0,
     'L1_attn_t_v': 35.812,
     'L2_ffn_b1s': 23.797,
     'L2_ffn_b2s': 29.23,
     'L3_ffn_b1': 2.727}
    for name, (base, spread) in spreads.items():
        noise = np.random.default_rng([zlib.crc32(name.encode()), seed]).standard_normal(out[name].shape)
        drawn = base * np.exp(spread * noise) if base else spread * noise
        out[name] = jnp.asarray(drawn.astype(out[name].dtype))
    for name, factor in factors.items():
        out[name] = (out[name] * factor).astype(out[name].dtype)
    return out
```

```python
import concourse.bass as bass
from concourse import mybir
from contextlib import ExitStack

F32 = mybir.dt.float32
BF16 = mybir.dt.bfloat16
I32 = mybir.dt.int32
ACT = mybir.ActivationFunctionType
ALU = mybir.AluOpType
AX = mybir.AxisListType

B, S, D = 8, 512, 128
TOK = B * S
TILES = TOK // 128
TPB = S // 128
HEADS, HD = 16, 8
QUADS = TILES
LN_EPS = 1e-5


class Core:

    def __init__(self, nc, ctx):
        self.nc, self.ctx, self.sems = nc, ctx, []
        self.arena = ctx.enter_context(nc.sbuf_tensor("arena", [128, 48 * 1024], F32))
        self.psum = ctx.enter_context(nc.psum_tensor("psum", [128, 8 * 512], F32))
        self.used = 0
        self.x = self.take(TILES * D).rearrange("p (t c) -> p t c", c=D)
        self.n = self.take(TILES * D).rearrange("p (t c) -> p t c", c=D)
        self.o = self.take(TILES * D).rearrange("p (t c) -> p t c", c=D)
        self.nT = self.take(B * (S + 2)).rearrange("p (b s) -> p b s", s=S + 2)
        self.stats = self.take(TILES * 6).rearrange("p (t k) -> p t k", k=6)
        self.mv = self.take(TILES * 2).rearrange("p (t k) -> p t k", k=2)
        self.rstd = self.take(TILES)
        self.var_eps = self.take(TILES)
        self.minus_half = self.take(TILES)
        self.ident = self.take(128)
        self.ident_bf = self.take(64).bitcast(BF16)
        self.ones = self.take(128)
        self.wT = self.take(16 * 128).rearrange("p (w c) -> p w c", c=128)
        self.base = self.used

    def take(self, words):
        at = self.used
        self.used += words
        assert self.used <= 48 * 1024, self.used
        return self.arena[:, at:at + words]

    def free_work(self):
        self.used = self.base

    def sem(self, name):
        self.sems.append(self.nc.alloc_semaphore(name))
        return self.sems[-1]

    def end_stage(self):
        self.nc.clear_and_free_semaphores(self.sems)
        self.sems = []
        self.nc.all_engine_barrier()

    def bank(self, n, k=1):
        return self.psum[:, n * 512:(n + k) * 512]


class Chain:

    def __init__(self, eng, sem, base=0):
        self.eng, self.sem, self.at, self.base = eng, sem, 0, base

    def next(self, ins):
        self.mark(ins)
        self.wait()

    def mark(self, ins):
        ins.then_inc(self.sem, 1)
        self.at += 1

    def wait(self):
        self.eng.wait_ge(self.sem, self.base + self.at)


SQUARE = ["L0_attn_Wq", "L0_attn_Wk", "L0_attn_Wv", "L0_ffn_W_r", "L0_ffn_W_k", "L0_ffn_W_v",
          "L1_attn_t_k", "L1_attn_t_v", "L1_attn_t_q", "L2_attn_W_qkv", "L3_attn_Wqkv", "L3_attn_Wout"]
W_Q0, W_K0, W_V0, W_R, W_K, W_V, T_K, T_V, T_Q, W_QKV2, W_QKV3, W_OUT = 0, 1, 2, 3, 4, 5, 6, 7, 8, 9, 12, 15


def setup(c, d, counting):
    nc = c.nc
    w_nat = c.take(16 * 128).rearrange("p (w c) -> p w c", c=128)
    x_in, w_in = c.sem("x_in"), c.sem("w_in")
    consts, ident_built = c.sem("consts"), c.sem("ident_built")
    w_turned, w_copied = c.sem("w_turned"), c.sem("w_copied")
    with nc.Block() as block:
        @block.sync
        def _(sp):
            sp.dma_start(c.x, d["L0_attn_x"].rearrange("b (t p) c -> p (b t) c", p=128)).then_inc(x_in, 16)

        @block.scalar
        def _(act):
            at = 0
            for name in SQUARE:
                rows = d[name].shape[0] // 128
                act.dma_start(w_nat[:, at:at + rows, :], d[name].rearrange("(w p) c -> p w c", p=128)).then_inc(w_in, 16)
                at += rows
            for k in range(4):
                act.wait_ge(w_turned, k + 1)
                nc.scalar.activation(c.wT[:, 4 * k:4 * k + 4, :], c.bank(k).rearrange("p (w c) -> p w c", c=128),
                                     ACT.Copy).then_inc(w_copied, 1)
            act.wait_ge(w_copied, 4)
            act.wait_ge(x_in, 16)

        @block.gpsimd
        def _(pool):
            counting.build(c, pool)
            nc.gpsimd.memset(c.minus_half, -0.5)
            nc.gpsimd.memset(c.ones, 1.0)
            nc.gpsimd.memset(c.nT[:, :, 0:1], 0.0)
            nc.gpsimd.memset(c.ident, 0.0).then_inc(consts, 1)
            pool.wait_ge(consts, 1)
            nc.gpsimd.affine_select(out=c.ident, in_=c.ident, compare_op=ALU.not_equal, fill=1.0, base=0,
                                    pattern=[[-1, 128]], channel_multiplier=1).then_inc(ident_built, 1)
            pool.wait_ge(ident_built, 1)
            nc.gpsimd.tensor_copy(c.ident_bf, c.ident).then_inc(consts, 1)

        @block.tensor
        def _(pe):
            pe.wait_ge(w_in, 16 * len(SQUARE))
            pe.wait_ge(ident_built, 1)
            for k in range(16):
                last = nc.tensor.transpose(c.bank(k // 4)[:, (k % 4) * 128:(k % 4) * 128 + 128], w_nat[:, k, :], c.ident)
                if k % 4 == 3:
                    last.then_inc(w_turned, 1)


def norms(c, tag, after_layer, x_norm=True, scale_of_batch=False):
    nc = c.nc
    sem = lambda name: c.sem(f"{tag}_{name}")
    o_stats, o_mv, o_rstd, o_norm, x_sum = (sem(s) for s in ("o_stats", "o_mv", "o_rstd", "o_norm", "x_sum"))
    x_stats, x_mv, x_rstd, n_done = (sem(s) for s in ("x_stats", "x_mv", "x_rstd", "n_done"))
    turned, copied, pool_step = sem("turned"), sem("copied"), sem("pool_step")
    step, summed = sem("step"), sem("summed")
    work = c.take(64 * 4)
    sums = c.bank(7)

    with nc.Block() as block:
        @block.vector
        def _(dve):
            def stats(src, t, s_stats, s_mv):
                for k in range(TPB):
                    nc.vector.bn_stats(c.stats[:, t + k, :], src[:, t + k, :]).then_inc(s_stats, 1)
                dve.wait_ge(s_stats, t + TPB)
                for k in range(TPB):
                    nc.vector.bn_aggr(c.mv[:, t + k, :], c.stats[:, t + k, :]).then_inc(s_mv, 1)

            if after_layer:
                for b in range(B):
                    stats(c.o, TPB * b, o_stats, o_mv)
                if scale_of_batch:
                    ch = Chain(dve, step)
                    mean, dev, tot = work[:, 0:8], work[:, 64:96], work[:, 32:64]
                    dve.wait_ge(summed, 1)
                    ch.next(nc.vector.tensor_reduce(mean, sums[:, 0:TILES].rearrange("p (b t) -> p b t", t=TPB),
                                                    axis=AX.X, op=ALU.add))
                    ch.next(nc.vector.tensor_scalar(mean, mean, 1.0 / S, None, ALU.mult))
                    ch.next(nc.vector.tensor_tensor(dev.rearrange("p (b t) -> p b t", t=TPB),
                                                    c.mv[:, :, 0].rearrange("p (b t) -> p b t", t=TPB),
                                                    mean.unsqueeze(2).to_broadcast([128, B, TPB]), ALU.subtract))
                    ch.next(nc.vector.tensor_tensor(dev, dev, dev, ALU.mult))
                    ch.next(nc.vector.tensor_tensor(tot, dev, c.mv[:, :, 1], ALU.add))
                    dve.wait_ge(summed, 2)
                    ch.next(nc.vector.tensor_reduce(mean, sums[:, 64:64 + TILES].rearrange("p (b t) -> p b t", t=TPB),
                                                    axis=AX.X, op=ALU.add))
                    ch.next(nc.vector.tensor_scalar(work[:, 8:16], mean, 1.0 / S, LN_EPS, ALU.mult, ALU.add))
                for b in range(B):
                    if b == 0:
                        dve.wait_ge(o_rstd, 1)
                    for k in range(TPB):
                        t = TPB * b + k
                        nc.vector.tensor_scalar(c.o[:, t, :], c.o[:, t, :], c.mv[:, t, 0:1], c.rstd[:, t:t + 1],
                                                ALU.subtract, ALU.mult).then_inc(o_norm, 1)
                    dve.wait_ge(o_norm, TPB * (b + 1))
                    nc.vector.tensor_tensor(c.x[:, TPB * b:TPB * b + TPB, :], c.x[:, TPB * b:TPB * b + TPB, :],
                                            c.o[:, TPB * b:TPB * b + TPB, :], ALU.add).then_inc(x_sum, 1)
            if x_norm:
                for b in range(B):
                    if after_layer:
                        dve.wait_ge(x_sum, b + 1)
                        if b == 0:
                            dve.wait_ge(o_norm, TILES)
                    stats(c.x, TPB * b, x_stats, x_mv)
                dve.wait_ge(x_rstd, 1)
                for t in range(TILES):
                    nc.vector.tensor_scalar(c.n[:, t, :], c.x[:, t, :], c.mv[:, t, 0:1], c.rstd[:, t:t + 1],
                                            ALU.subtract, ALU.mult).then_inc(n_done, 1)

        @block.gpsimd
        def _(pool):
            ch = Chain(pool, pool_step)

            def inverse_root(out, var, eps):
                ch.next(nc.gpsimd.tensor_scalar(c.var_eps, var, eps, None, ALU.add))
                return nc.gpsimd.tensor_tensor(out, c.var_eps, c.minus_half, ALU.pow)

            if after_layer:
                pool.wait_ge(o_mv, TILES)
                if scale_of_batch:
                    pool.wait_ge(step, 7)
                    rs, rs2, full = work[:, 16:24], work[:, 24:32], work[:, 128:160]
                    ch.next(nc.gpsimd.tensor_tensor(rs, work[:, 8:16], c.minus_half[:, 0:B], ALU.pow))
                    ch.next(nc.gpsimd.tensor_tensor(rs2, rs, rs, ALU.mult))
                    wide = lambda v: v.unsqueeze(2).to_broadcast([128, B, TPB])
                    tiles = lambda v: v.rearrange("p (b t) -> p b t", t=TPB)
                    ch.next(nc.gpsimd.tensor_tensor(tiles(full), tiles(c.mv[:, :, 1]), wide(rs2), ALU.mult))
                    ch.next(inverse_root(work[:, 160:192], full, LN_EPS))
                    nc.gpsimd.tensor_tensor(tiles(c.rstd), tiles(work[:, 160:192]), wide(rs), ALU.mult).then_inc(o_rstd, 1)
                else:
                    inverse_root(c.rstd, c.mv[:, :, 1], LN_EPS).then_inc(o_rstd, 1)
            if x_norm:
                pool.wait_ge(x_mv, TILES)
                inverse_root(c.rstd, c.mv[:, :, 1], LN_EPS).then_inc(x_rstd, 1)

        @block.tensor
        def _(pe):
            if scale_of_batch:
                pe.wait_ge(o_mv, TILES)
                nc.tensor.matmul(sums[:, 0:TILES], c.ones, c.mv[:, :, 0], start=True, stop=True).then_inc(summed, 1)
                pe.wait_ge(step, 5)
                nc.tensor.matmul(sums[:, 64:64 + TILES], c.ones, work[:, 32:64], start=True, stop=True).then_inc(summed, 1)
            if x_norm:
                for b in range(B):
                    pe.wait_ge(n_done, TPB * (b + 1))
                    if b >= 2:
                        pe.wait_ge(copied, b - 1)
                    for k in range(TPB):
                        last = nc.tensor.transpose(c.bank(b % 2)[:, k * 128:(k + 1) * 128], c.n[:, TPB * b + k, :], c.ident)
                    last.then_inc(turned, 1)

        @block.scalar
        def _(act):
            if x_norm:
                for b in range(B):
                    act.wait_ge(turned, b + 1)
                    nc.scalar.activation(c.nT[:, b, 1:S + 1], c.bank(b % 2), ACT.Copy).then_inc(copied, 1)


PARTS = 3
QK_ROWS = PARTS * PARTS * HD
MAX_ROW = 96
ROWS = MAX_ROW + PARTS
RING = 4


class Attention:

    def __init__(self, c, tag, by_tokens, scale):
        self.c, self.tag, self.by_tokens, self.scale = c, tag, by_tokens, scale
        nc = c.nc
        self.q_parts = nc.dram_tensor(f"{tag}_q_parts", (QUADS, PARTS, HD, 2048), BF16).ap()
        self.k_parts = nc.dram_tensor(f"{tag}_k_parts", (QUADS, PARTS, HD, 2048), BF16).ap()
        self.v = c.take(QUADS * 128).rearrange("p (q g k d) -> p q g k d", g=4, k=4, d=HD)
        self.rope = None

    def columns(self, rows, g, first, n):
        if self.by_tokens:
            return rows[:, 4 * first + g:4 * (first + n - 1) + g + 1:4]
        return rows[:, 512 * g + first:512 * g + first + n]


def attention_operands(c, a, d, w, bias=None, tables=None):
    nc = c.nc
    tag = a.tag + "_op"
    sem = lambda name: c.sem(f"{tag}_{name}")
    q_made, v_made = sem("qk_made"), sem("v_made")
    high, rest, mid, parts, v_laid = (sem(s) for s in ("high", "rest", "mid", "parts", "v_laid"))
    stored = [sem("stored_q"), sem("stored_k")]
    exact = sem("exact")
    part = c.take(2 * PARTS * 256).bitcast(BF16).rearrange("p (s a t) -> p s a t", s=2, a=PARTS)
    left = c.take(2 * S).rearrange("p (s t) -> p s t", s=2)
    full = c.take(2 * S).rearrange("p (s t) -> p s t", s=2)
    turn = c.take(2 * S).rearrange("p (s t) -> p s t", s=2)
    const_in = sem("const_in")
    rope = tables is not None
    if rope:
        qk_bias = c.take(4)
        v_bias = c.take(128)
        cos_t, sin_t = c.take(S), c.take(S)
        w_swap = c.take(256).rearrange("p (w c) -> p w c", w=2)
        swapped = sem("swapped")
        rope_cos, rope_sin = sem("rope_cos"), sem("rope_sin")

    with nc.Block() as block:
        @block.sync
        def _(sp):
            if rope:
                for n in range(2):
                    sp.dma_start(qk_bias[:, n:n + 1], bias[128 * n:128 * n + 128].rearrange("(c o) -> c o", o=1)).then_inc(const_in, 16)
                sp.dma_start(qk_bias[:, 2:4], tables["bias_swapped"]).then_inc(const_in, 16)
                sp.dma_start(v_bias, bias[256:384].partition_broadcast(128)).then_inc(const_in, 16)
                sp.dma_start(cos_t, tables["cos"]).then_inc(const_in, 16)
                sp.dma_start(sin_t, tables["sin"]).then_inc(const_in, 16)
            for n in range(2 * B):
                b, dst = n // 2, (a.q_parts, a.k_parts)[n % 2]
                sp.wait_ge(parts, n + 1)
                for k in range(PARTS):
                    for t in range(4):
                        if a.by_tokens:
                            src = part[:, n % 2, k, 128 * t:128 * t + 128]
                            out = dst[TPB * b + t, k].rearrange("d (j t) -> j d t", j=HEADS)
                        else:
                            src = part[32 * t:32 * t + 32, n % 2, k, :]
                            out = dst[TPB * b + t, k].rearrange("d (h t) -> h d t", h=4)
                        sp.dma_start(out, src).then_inc(stored[n % 2], 16)
            for n in range(2):
                sp.wait_ge(stored[n], B * PARTS * 4 * 16)

        @block.tensor
        def _(pe):
            if rope:
                pe.wait_ge(swapped, 1)
            for b in range(B):
                for n in range(2):
                    at = 2 * b + n
                    if at >= 2:
                        pe.wait_ge(rest if not rope else rope_sin, at - 1)
                        if not rope:
                            pe.wait_ge(high, at - 1)
                    tokens = c.nT[:, b, 1:S + 1]
                    if a.by_tokens:
                        tokens = tokens.rearrange("p (t g l) -> p t l g", g=4, l=32)
                    last = nc.tensor.matmul(c.bank(n), c.wT[:, w + n, :], tokens, start=True, stop=True)
                    if rope:
                        last = nc.tensor.matmul(c.bank(4 + n), w_swap[:, n, :], c.nT[:, b, 1:S + 1], start=True, stop=True)
                    last.then_inc(q_made, 1)
                if b >= 2:
                    pe.wait_ge(v_laid, b - 1)
                for k in range(TPB):
                    last = nc.tensor.matmul(c.bank(2 + b % 2)[:, 128 * k:128 * k + 128],
                                            c.nT[:, b, 1 + 128 * k:129 + 128 * k], c.wT[:, w + 2, :], start=True, stop=True)
                last.then_inc(v_made, 1)

        @block.scalar
        def _(act):
            for n in range(2 * B):
                if rope:
                    act.wait_ge(exact, n + 1)
                else:
                    act.wait_ge(q_made, n + 1)
                if n >= 2:
                    act.wait_ge(stored[n % 2], n // 2 * PARTS * 4 * 16)
                src = full[:, n % 2, :] if rope else c.bank(n % 2)
                nc.scalar.activation(part[:, n % 2, 0, :], src, ACT.Copy).then_inc(high, 1)

        @block.vector
        def _(dve):
            if rope:
                dve.wait_ge(const_in, 16 * 6)
                for n in range(2):
                    v = lambda m: m.rearrange("p (h two f) -> p h two f", two=2, f=HD // 2)
                    nc.vector.tensor_copy(v(w_swap[:, n, :])[:, :, 0, :], v(c.wT[:, w + n, :])[:, :, 1, :])
                    last = nc.vector.tensor_copy(v(w_swap[:, n, :])[:, :, 1, :], v(c.wT[:, w + n, :])[:, :, 0, :])
                last.then_inc(swapped, 1)
            for b in range(B):
                for n in range(2):
                    at = 2 * b + n
                    if rope:
                        dve.wait_ge(q_made, at + 1)
                        if at >= 2:
                            dve.wait_ge(exact, at - 1)
                            dve.wait_ge(high, at - 1)
                            dve.wait_ge(rest, at - 1)
                        nc.vector.scalar_tensor_tensor(full[:, n, :], c.bank(n), qk_bias[:, n:n + 1], cos_t,
                                                       op0=ALU.add, op1=ALU.mult).then_inc(rope_cos, 1)
                        nc.vector.scalar_tensor_tensor(turn[:, n, :], c.bank(4 + n), qk_bias[:, 2 + n:3 + n], sin_t,
                                                       op0=ALU.add, op1=ALU.mult).then_inc(rope_sin, 1)
                    dve.wait_ge(high, at + 1)
                    if at >= 2:
                        dve.wait_ge(parts, at - 1)
                    src = full[:, n, :] if rope else c.bank(n)
                    nc.vector.tensor_tensor(left[:, n, :], src, part[:, n, 0, :], ALU.subtract).then_inc(rest, 1)
                dve.wait_ge(v_made, b + 1)
                vb = c.bank(2 + b % 2)
                if a.by_tokens:
                    for g in range(4):
                        for j in range(4):
                            src = vb[32 * g:32 * g + 32, :].rearrange("p (t k j d) -> p t k j d", t=4, k=4, j=4)[:, :, :, j, :]
                            last = nc.vector.tensor_copy(a.v[32 * j:32 * j + 32, TPB * b:TPB * b + TPB, g, :, :], src)
                else:
                    for k in range(TPB):
                        src = vb[:, 128 * k:128 * k + 128].rearrange("p (q g d) -> p q g d", q=4, g=4)
                        last = nc.vector.tensor_tensor(a.v[:, TPB * b:TPB * b + TPB, :, k, :], src,
                                                       v_bias.rearrange("p (q g d) -> p q g d", q=4, g=4), ALU.add)
                last.then_inc(v_laid, 1)

        @block.gpsimd
        def _(pool):
            for n in range(2 * B):
                if rope:
                    pool.wait_ge(rope_cos, n + 1)
                    pool.wait_ge(rope_sin, n + 1)
                    nc.gpsimd.tensor_tensor(full[:, n % 2, :], full[:, n % 2, :], turn[:, n % 2, :], ALU.add).then_inc(exact, 1)
                pool.wait_ge(rest, n + 1)
                if n >= 2:
                    pool.wait_ge(stored[n % 2], n // 2 * PARTS * 4 * 16)
                nc.gpsimd.tensor_copy(part[:, n % 2, 1, :], left[:, n % 2, :]).then_inc(mid, 1)
                pool.wait_ge(mid, n + 1)
                nc.gpsimd.tensor_tensor(part[:, n % 2, 2, :], left[:, n % 2, :], part[:, n % 2, 1, :], ALU.subtract).then_inc(parts, 1)


def attention(c, a, select=None):
    nc = c.nc
    sem = lambda name: c.sem(f"{a.tag}_{name}")
    qk_in = [sem(f"qk_in{s}") for s in range(RING)]
    max_in = [sem(f"max_in{s}") for s in range(RING)]
    pads, v_ones = sem("pads"), sem("v_ones")
    max_scores, max_taken, max_step, max_split = (sem(s) for s in ("max_scores", "max_taken", "max_step", "max_split"))
    max_turned, max_rows, max_set = sem("max_turned"), sem("max_rows"), sem("max_set")
    scores, probs, pv_step = sem("scores"), sem("probs"), sem("pv_step")
    v_ready, out_taken = sem("v_ready"), sem("out_taken")
    picked, recip_done, o_done = sem("picked"), sem("recip_done"), sem("o_done")
    CREDITS = 2

    bf = lambda words: c.take(words).bitcast(BF16)
    q9 = bf(RING * 1024).rearrange("p (s t) -> p s t", s=RING)
    k9 = bf(RING * 1024).rearrange("p (s t) -> p s t", s=RING)
    prob = c.take(2 * 2048).rearrange("p (s g t) -> p s g t", s=2, g=4)
    v32 = c.take(2 * 512).rearrange("p (s g k d) -> p s g k d", s=2, g=4, k=4)
    neg_max = c.take(2 * 16).rearrange("p (s m) -> p s m", s=2)
    max_left = c.take(16)
    max_part = bf(2 * 24).rearrange("p (s m) -> p s m", s=2)
    max_row = bf(2 * 64).rearrange("p (s t) -> p s t", s=2)
    row_stage = bf(2 * 1024).rearrange("p (s t) -> p s t", s=2) if a.by_tokens else None
    o_quad = c.take(2 * S).rearrange("p (s t) -> p s t", s=2)
    recip = c.take(2 * 16).rearrange("p (s t) -> p s t", s=2)

    max_bank = [c.bank(0, 2), c.bank(2, 2)]
    score_bank = [c.bank(4), c.bank(5)]
    out_bank = c.bank(6)
    turn_bank = c.bank(7)[0:48, 0:64].bitcast(BF16)
    pick_bank = c.bank(7)[:, 128:128 + 144]
    LAST = QUADS - RING
    LOADS = 16 * (PARTS + 1)
    ROW_DMAS = 16 * PARTS

    def quads(eng, body):
        with eng.Fori(0, LAST // RING) as turn:
            for s in range(RING):
                body(turn * RING + s, s, turn, True, True)
        for s in range(RING):
            body(LAST + s, s, LAST // RING, s + 1 < RING, s + 2 < RING)

    def ahead(s, turn, n):
        return (s + n) % RING, turn + (s + n) // RING

    def max_column(g, m):
        return 4 * g + m

    with nc.Block() as block:
        @block.sync
        def _(sp):
            def load(i, s):
                for p in range(PARTS):
                    src = a.q_parts[bass.ds(i, 1), p].rearrange("o d t -> (o d) t")
                    sp.dma_start(q9[24 * p:24 * p + 24, s, :],
                                 src.unsqueeze(0).to_broadcast([PARTS, HD, 2048])).then_inc(qk_in[s], 16)
                src = a.k_parts[bass.ds(i, 1)].rearrange("o r d t -> (o r d) t")
                sp.dma_start(k9[0:QK_ROWS, s, :],
                             src.unsqueeze(0).to_broadcast([PARTS, 24, 2048])).then_inc(qk_in[s], 16)

            def rows(i, s):
                sp.wait_ge(max_rows, i + 2)
                src = max_row[0:48, s % 2, :]
                to = row_stage[MAX_ROW:ROWS, s % 2, :] if a.by_tokens else q9[MAX_ROW:ROWS, s, :]
                for p in range(PARTS):
                    sp.dma_start(to[p:p + 1, :], src[16 * p:16 * p + 16, :]).then_inc(max_in[s], 16)

            sp.wait_ge(pads, 3)
            for s in range(RING):
                load(s, s)
            rows(0, 0)

            def body(i, s, turn, next1, next2):
                if next1:
                    rows(i + 1, (s + 1) % RING)
                if turn is not LAST // RING:
                    sp.wait_ge(scores, 16 * i + 16)
                    load(i + RING, s)

            quads(sp, body)

        @block.gpsimd
        def _(pool):
            pool.wait_ge(v_ones, 1)

            def values(i, s):
                nc.gpsimd.tensor_copy(v32[:, s % 2, :, :, 0:HD].rearrange("p g k d -> p (g k) d"),
                                      a.v[:, bass.ds(i, 1), :, :, :].rearrange("p o g k d -> p (o g k) d")).then_inc(v_ready, 1)

            def split(i, s):
                part = lambda p: max_part[:, s % 2, 16 * p:16 * p + 16]
                pool.wait_ge(max_taken, 8 * i + 8)
                pool.wait_ge(max_split, i + 1)
                nc.gpsimd.tensor_tensor(part(0), neg_max[:, s % 2, :], c.ones[:, 0:16], ALU.mult).then_inc(max_step, 1)
                pool.wait_ge(max_step, 3 * i + 1)
                nc.gpsimd.tensor_tensor(max_left, neg_max[:, s % 2, :], part(0), ALU.subtract).then_inc(max_step, 1)
                pool.wait_ge(max_step, 3 * i + 2)
                nc.gpsimd.tensor_tensor(part(1), max_left, c.ones[:, 0:16], ALU.mult).then_inc(max_step, 1)
                pool.wait_ge(max_step, 3 * i + 3)
                nc.gpsimd.tensor_tensor(part(2), max_left, part(1), ALU.subtract).then_inc(max_split, 1)

            pool.sem_inc(max_split, 1)
            split(0, 0)
            values(0, 0)
            split(1, 1)

            def body(i, s, turn, next1, next2):
                if next1:
                    pool.wait_ge(pv_step, CREDITS + 4 * i)
                    values(i + 1, s + 1)
                if next2:
                    pool.wait_ge(max_turned, i + 1)
                    split(i + 2, s)

            quads(pool, body)

        @block.tensor
        def _(pe):
            def max_tile(s, m):
                for h in range(2):
                    last = nc.tensor.matmul(max_bank[m % 2][:, 512 * h:512 * h + 512],
                                            a.columns(q9[0:QK_ROWS, s, :], m // 2, 128 * (2 * (m % 2) + h), 128),
                                            a.columns(k9[0:QK_ROWS, s, :], m // 2, 0, 512), start=True, stop=True)
                last.then_inc(max_scores, 1)

            def turn_max_wait(i):
                pe.wait_ge(max_split, i + 2)
                pe.wait_ge(max_rows, i + 1)
                if not a.by_tokens:
                    pe.wait_ge(o_done, i)

            def turn_max(i, s):
                nc.tensor.transpose(turn_bank, max_part[:, s % 2, :], c.ident_bf).then_inc(max_turned, 1)

            def score_tile(i, s, k, g):
                n = 16 * i + 4 * k + g
                pe.wait_ge(probs, n - 2 + 1 + CREDITS)
                nc.tensor.matmul(score_bank[g % 2], a.columns(k9[0:ROWS, s, :], g, 128 * k, 128),
                                 a.columns(q9[0:ROWS, s, :], g, 0, 512), start=True, stop=True).then_inc(scores, 1)

            def pv(i, s, k):
                pe.wait_ge(probs, 16 * i + 4 * k + 4 + CREDITS)
                if k == 0:
                    pe.wait_ge(v_ready, i + 1)
                    pe.wait_ge(out_taken, i + 1)
                for g in range(4):
                    last = nc.tensor.matmul(out_bank[32 * g:32 * g + 32, :], v32[:, s % 2, g, k, :],
                                            prob[:, k % 2, g, :], start=(k == 0), stop=(k == 3))
                last.then_inc(pv_step, 1)

            def pick(i, s, next1):
                pe.wait_ge(out_taken, i + 2)
                pe.wait_ge(o_done, i + 1)
                if next1:
                    pe.wait_ge(max_rows, i + 3)
                for t in range(4):
                    last = nc.tensor.matmul(pick_bank[:, 36 * t:36 * t + 36], o_quad[:, s % 2, 128 * t:128 * t + 128],
                                            select, start=True, stop=True)
                last.then_inc(picked, 1)

            def max_rows_set(i, s, turn):
                if a.by_tokens:
                    pe.wait_ge(max_set, i + 1)
                else:
                    pe.wait_ge(max_in[s], ROW_DMAS * (turn + 1))

            pe.sem_inc(pv_step, CREDITS)
            for i in range(2):
                pe.wait_ge(qk_in[i], LOADS)
                for m in range(8):
                    if 8 * i + m >= 2:
                        pe.wait_ge(max_taken, 8 * i + m - 1)
                    max_tile(i, m)
            turn_max_wait(0)
            turn_max(0, 0)
            max_rows_set(0, 0, 0)
            for k in range(2):
                for g in range(4):
                    score_tile(0, 0, k, g)

            def body(i, s, turn, next1, next2):
                pv(i, s, 0)
                if next1:
                    turn_max_wait(i + 1)
                s1, turn1 = ahead(s, turn, 1)
                s2, turn2 = ahead(s, turn, 2)
                for n in range(2, 6):
                    if n < 4 or next1:
                        if n == 4:
                            max_rows_set(i + 1, s1, turn1)
                        for g in range(4):
                            if n < 4:
                                score_tile(i, s, n, g)
                                if next1 and (n, g) == (2, 0):
                                    turn_max(i + 1, s + 1)
                            else:
                                score_tile(i + 1, s1, n - 4, g)
                            if next2 and g % 2 == 1:
                                m = 2 * (n - 2) + g // 2
                                if m == 0:
                                    pe.wait_ge(qk_in[s2], LOADS * (turn2 + 1))
                                pe.wait_ge(max_taken, 8 * (i + 2) + m - 1)
                                max_tile(s2, m)
                    if n < 5:
                        pv(i, s, n - 1)
                if not a.by_tokens:
                    pick(i, s, next1)

            quads(pe, body)

        @block.scalar
        def _(act):
            def exps(i, s, k):
                act.wait_ge(pv_step, 4 * i + k - 2 + 1 + CREDITS)
                for g in range(4):
                    act.wait_ge(scores, 16 * i + 4 * k + g + 1)
                    nc.scalar.activation(prob[:, k % 2, g, :], score_bank[g % 2], ACT.Exp, scale=a.scale).then_inc(probs, 1)

            def rows(i, s):
                act.wait_ge(max_turned, i + 1)
                nc.scalar.activation(max_row[0:48, s % 2, :], turn_bank, ACT.Copy).then_inc(max_rows, 1)

            def set_rows(i, s, turn):
                if a.by_tokens:
                    act.wait_ge(max_in[s], ROW_DMAS * (turn + 1))
                    nc.scalar.activation(q9[MAX_ROW:ROWS, s, :].rearrange("p (t g) -> p g t", g=4),
                                         row_stage[MAX_ROW:ROWS, s % 2, :].rearrange("p (g t) -> p g t", g=4),
                                         ACT.Copy).then_inc(max_set, 1)

            act.sem_inc(probs, CREDITS)
            act.sem_inc(max_rows, 1)
            rows(0, 0)
            set_rows(0, 0, 0)
            exps(0, 0, 0)
            exps(0, 0, 1)

            def body(i, s, turn, next1, next2):
                if next1:
                    rows(i + 1, s + 1)
                exps(i, s, 2)
                exps(i, s, 3)
                if next1:
                    set_rows(i + 1, *ahead(s, turn, 1))
                    exps(i + 1, s + 1, 0)
                    exps(i + 1, s + 1, 1)

            quads(act, body)

        @block.vector
        def _(dve):
            def take(i, s, m):
                dve.wait_ge(max_scores, 8 * i + m + 1)
                col = max_column(m // 2, 2 * (m % 2))
                nc.vector.tensor_reduce(neg_max[:, s % 2, col:col + 2],
                                        max_bank[m % 2].rearrange("p (h t) -> p h t", h=2),
                                        axis=AX.X, op=ALU.max, negate=True).then_inc(max_taken, 1)

            def out(i, s):
                dve.wait_ge(pv_step, 4 * i + 4 + CREDITS)
                dve.wait_ge(o_done, i + 1)
                if a.by_tokens:
                    nc.vector.transpose(o_quad[:, s % 2, :], out_bank).then_inc(out_taken, 1)
                else:
                    nc.vector.tensor_copy(o_quad[:, s % 2, :], out_bank).then_inc(out_taken, 1)

            def normalise(i, s, turn):
                if a.by_tokens:
                    dve.wait_ge(out_taken, i + 2)
                    o = o_quad[:, s % 2, :].rearrange("p (j r) -> p j r", r=32)
                    nc.vector.reciprocal(recip[:, s % 2, :], o[:, :, HD]).then_inc(recip_done, 1)
                    dve.wait_ge(recip_done, i + 1)
                    nc.vector.tensor_tensor(c.o[:, bass.ds(i, 1), :].rearrange("p o (j d) -> p (o j) d", d=HD), o[:, :, 0:HD],
                                            recip[:, s % 2, :].unsqueeze(2).to_broadcast([128, HEADS, HD]),
                                            ALU.mult).then_inc(o_done, 1)
                else:
                    dve.wait_ge(picked, i + 1)
                    o = pick_bank.rearrange("p (t r) -> p t r", r=36)
                    r = recip[:, s % 2, :].rearrange("p (t g) -> p t g", t=4)
                    nc.vector.reciprocal(r, o[:, :, 32:36]).then_inc(recip_done, 1)
                    dve.wait_ge(recip_done, i + 1)
                    nc.vector.tensor_tensor(c.o[:, bass.ds(turn * TPB, TPB), 32 * s:32 * s + 32].rearrange("p t (g d) -> p t g d", g=4),
                                            o[:, :, 0:32].rearrange("p t (g d) -> p t g d", g=4),
                                            r.unsqueeze(3).to_broadcast([128, TPB, 4, HD]), ALU.mult).then_inc(o_done, 1)

            dve.sem_inc(out_taken, 1)
            dve.sem_inc(o_done, 1)
            nc.vector.memset(q9[64:96, :, :], 0.0).then_inc(pads, 1)
            nc.vector.memset(k9[64:96, :, :], 0.0).then_inc(pads, 1)
            nc.vector.memset(k9[96:128, :, :], 1.0).then_inc(pads, 1)
            nc.vector.memset(v32[:, :, :, :, HD:32], 1.0).then_inc(v_ones, 1)
            for i in range(2):
                for m in range(8):
                    take(i, i, m)

            def body(i, s, turn, next1, next2):
                if next2:
                    dve.wait_ge(max_split, i + 2)
                    for m in range(6):
                        take(i + 2, s, m)
                out(i, s)
                if next2:
                    for m in range(6, 8):
                        take(i + 2, s, m)
                normalise(i, s, turn)

            quads(dve, body)


def channel_mix(c, d):
    nc = c.nc
    sem = lambda name: c.sem(f"mix_{name}")
    mu_in, mu_done = sem("mu_in"), sem("mu_done")
    part_done, mixed = sem("part_done"), sem("mixed")
    k_made, k_relu, k_sq = sem("k_made"), sem("k_relu"), sem("k_sq")
    r_made, r_sig, v_made, o_done = sem("r_made"), sem("r_sig"), sem("v_made"), sem("o_done")
    mu = c.take(4)
    ring = lambda: c.take(2 * S).rearrange("p (s t) -> p s t", s=2)
    prev, x_r, x_k, k_pos, k_act, gate = ring(), ring(), ring(), ring(), ring(), ring()
    k_bank, r_bank, v_bank = ([c.bank(n), c.bank(n + 1)] for n in (0, 2, 4))

    with nc.Block() as block:
        @block.sync
        def _(sp):
            for n, name in enumerate(("L0_ffn_mu_r", "L0_ffn_mu_k")):
                sp.dma_start(mu[:, n:n + 1], d[name].rearrange("(c o) -> c o", o=1)).then_inc(mu_in, 16)
            sp.wait_ge(mu_in, 32)

        @block.vector
        def _(dve):
            def output(b):
                dve.wait_ge(v_made, b + 1)
                dve.wait_ge(r_sig, b + 1)
                nc.vector.tensor_tensor(c.o[:, TPB * b:TPB * b + TPB, :].rearrange("p t c -> p (t c)"), v_bank[b % 2],
                                        gate[:, b % 2, :], ALU.mult).then_inc(o_done, 1)

            dve.wait_ge(mu_in, 32)
            nc.vector.tensor_scalar(mu[:, 2:4], mu[:, 0:2], -1.0, 1.0, ALU.mult, ALU.add).then_inc(mu_done, 1)
            dve.wait_ge(mu_done, 1)
            for b in range(B):
                now, before = c.nT[:, b, 1:S + 1], c.nT[:, b, 0:S]
                for n, x_mix in enumerate((x_r, x_k)):
                    if b or n:
                        dve.wait_ge(mixed, 2 * b + n)
                    if b >= 2:
                        dve.wait_ge(r_made, b - 1)
                        dve.wait_ge(k_made, b - 1)
                    nc.vector.tensor_scalar(prev[:, n, :], before, mu[:, 2 + n:3 + n], None, ALU.mult).then_inc(part_done, 1)
                    dve.wait_ge(part_done, 2 * b + n + 1)
                    nc.vector.scalar_tensor_tensor(x_mix[:, b % 2, :], now, mu[:, n:n + 1], prev[:, n, :],
                                                   op0=ALU.mult, op1=ALU.add).then_inc(mixed, 1)
                if b >= 1:
                    output(b - 1)
            output(B - 1)

        @block.tensor
        def _(pe):
            def values(b):
                pe.wait_ge(k_sq, b + 1)
                if b >= 2:
                    pe.wait_ge(o_done, b - 1)
                for k in range(TPB):
                    last = nc.tensor.matmul(v_bank[b % 2][:, 128 * k:128 * k + 128], k_act[:, b % 2, 128 * k:128 * k + 128],
                                            c.wT[:, W_V, :], start=True, stop=True)
                last.then_inc(v_made, 1)

            for b in range(B):
                pe.wait_ge(mixed, 2 * b + 2)
                if b >= 2:
                    pe.wait_ge(k_relu, b - 1)
                    pe.wait_ge(r_sig, b - 1)
                nc.tensor.matmul(k_bank[b % 2], c.wT[:, W_K, :], x_k[:, b % 2, :], start=True, stop=True).then_inc(k_made, 1)
                for k in range(TPB):
                    last = nc.tensor.matmul(r_bank[b % 2][:, 128 * k:128 * k + 128], x_r[:, b % 2, 128 * k:128 * k + 128],
                                            c.wT[:, W_R, :], start=True, stop=True)
                last.then_inc(r_made, 1)
                if b >= 1:
                    values(b - 1)
            values(B - 1)

        @block.scalar
        def _(act):
            for b in range(B):
                act.wait_ge(k_made, b + 1)
                if b >= 2:
                    act.wait_ge(k_sq, b - 1)
                nc.scalar.activation(k_pos[:, b % 2, :], k_bank[b % 2], ACT.Relu).then_inc(k_relu, 1)
                act.wait_ge(r_made, b + 1)
                if b >= 2:
                    act.wait_ge(o_done, b - 1)
                nc.scalar.activation(gate[:, b % 2, :], r_bank[b % 2], ACT.Sigmoid).then_inc(r_sig, 1)

        @block.gpsimd
        def _(pool):
            for b in range(B):
                pool.wait_ge(k_relu, b + 1)
                if b >= 2:
                    pool.wait_ge(v_made, b - 1)
                nc.gpsimd.tensor_tensor(k_act[:, b % 2, :], k_pos[:, b % 2, :], k_pos[:, b % 2, :], ALU.mult).then_inc(k_sq, 1)


HID = 32
STEP = 1e-3 * 2.0 / (S * D)
TINY = 1e-6


def test_time_learner(c, d):
    nc = c.nc
    sem = lambda name: c.sem(f"ttl_{name}")
    flat = lambda v: v.rearrange("p t c -> p (t c)")
    tokens = lambda: c.take(TILES * D).rearrange("p (b s) -> p b s", b=B)
    z_nat, z_T, zy_nat, zy_T, q_T = tokens(), tokens(), tokens(), tokens(), tokens()
    w1_nat, w1T, w2, w2T = c.take(128), c.take(HID), c.take(HID), c.take(128)
    b1, ones_row = c.take(HID), c.take(S)

    w_in, turned, w_ready = sem("w_in"), sem("turned"), sem("w_ready")
    made, act_out, dve_out = sem("made"), sem("act_out"), sem("dve_out")
    with nc.Block() as block:
        @block.sync
        def _(sp):
            sp.dma_start(w1_nat[0:HID, :], d["L1_attn_W1"]).then_inc(w_in, 16)
            sp.dma_start(w2, d["L1_attn_W2"]).then_inc(w_in, 16)
            sp.dma_start(b1[0:1, :], d["L1_attn_b1"].rearrange("(o c) -> o c", o=1)).then_inc(w_in, 16)
            sp.dma_start(w2T[HID:HID + 1, :], d["L1_attn_b2"].rearrange("(o c) -> o c", o=1)).then_inc(w_in, 16)
            sp.wait_ge(w_in, 64)

        @block.gpsimd
        def _(pool):
            nc.gpsimd.memset(ones_row[0:1, :], 1.0)

        @block.tensor
        def _(pe):
            pe.wait_ge(w_in, 64)
            nc.tensor.transpose(c.bank(6)[:, 0:HID], w1_nat[0:HID, :], c.ident[0:HID, 0:HID])
            nc.tensor.transpose(c.bank(6)[0:HID, 128:256], w2, c.ident).then_inc(turned, 1)
            for b in range(B):
                if b >= 1:
                    pe.wait_ge(act_out, 3 * b)
                    pe.wait_ge(dve_out, 3 * b)
                x = c.nT[:, b, 1:S + 1]
                for n, w in enumerate((T_K, T_V, T_Q)):
                    for k in range(TPB):
                        nc.tensor.matmul(c.bank(n)[:, 128 * k:128 * k + 128], x[:, 128 * k:128 * k + 128], c.wT[:, w, :],
                                         start=True, stop=True)
                    nc.tensor.matmul(c.bank(3 + n), c.wT[:, w, :], x, start=True, stop=True).then_inc(made, 1)

        @block.scalar
        def _(act):
            act.wait_ge(turned, 1)
            nc.scalar.activation(w1T, c.bank(6)[:, 0:HID], ACT.Copy).then_inc(w_ready, 1)
            nc.scalar.activation(w2T[0:HID, :], c.bank(6)[0:HID, 128:256], ACT.Copy).then_inc(w_ready, 1)
            for b in range(B):
                act.wait_ge(made, 3 * b + 1)
                nc.scalar.activation(z_nat[:, b, :], c.bank(0), ACT.Copy).then_inc(act_out, 1)
                nc.scalar.activation(z_T[:, b, :], c.bank(3), ACT.Copy).then_inc(act_out, 1)
                act.wait_ge(made, 3 * b + 3)
                nc.scalar.activation(q_T[:, b, :], c.bank(5), ACT.Copy).then_inc(act_out, 1)

        @block.vector
        def _(dve):
            for b in range(B):
                dve.wait_ge(made, 3 * b + 2)
                dve.wait_ge(act_out, 3 * b + 1)
                nc.vector.tensor_tensor(zy_nat[:, b, :], z_nat[:, b, :], c.bank(1), ALU.subtract).then_inc(dve_out, 1)
                dve.wait_ge(act_out, 3 * b + 2)
                nc.vector.tensor_tensor(zy_T[:, b, :], z_T[:, b, :], c.bank(4), ALU.subtract).then_inc(dve_out, 1)
                dve.wait_ge(made, 3 * b + 3)
                nc.vector.tensor_copy(flat(c.o[:, TPB * b:TPB * b + TPB, :]), c.bank(2)).then_inc(dve_out, 1)

    small = lambda: c.take(128)
    a, a_sq, a_off, a_safe, gel, th, inv, phi, low, high, dens, slope, d_a = (small() for _ in range(13))
    h_one = c.take(TPB * (HID + 1)).rearrange("p (k h) -> p k h", k=TPB)
    hT, hqT = c.take(S), c.take(S)
    r_nat, r_T = c.take(S), c.take(S)
    tiles = lambda v: v.rearrange("p (k h) -> p k h", k=TPB)

    a_made, aT_made, r_made, rT_made, dh_made = (sem(s) for s in ("a_made", "aT_made", "r_made", "rT_made", "dh_made"))
    grad1, grad2, q_made, o_made = sem("grad1"), sem("grad2"), sem("q_made"), sem("o_made")
    a_ready, safe_ready, gel_done, hT_done, hq_done = (sem(s) for s in ("a_ready", "safe_ready", "gel_done", "hT_done", "hq_done"))
    step, h_ready, r_done, da_done, moved, o_done = (sem(s) for s in ("step", "h_ready", "r_done", "da_done", "moved", "o_done"))
    ones_set = sem("ones_set")
    pa, paT, pr, prT, pd, pq, po = (c.bank(n) for n in range(7))
    pg = c.bank(7)
    g_w1, g_b1, g_w2, g_w2T = pd[:, 256:288], pd[0:1, 288:320], pg[:, 64:96], pg[0:HID + 1, 128:256]

    with nc.Block() as block:
        @block.tensor
        def _(pe):
            def hidden_T(out, x, b):
                nc.tensor.matmul(out[0:HID, :], w1T, x[:, b, :], start=True, stop=False)
                return nc.tensor.matmul(out[0:HID, :], b1[0:1, :], ones_row[0:1, :], start=False, stop=True)

            def output(b):
                hidden_T(pq, q_T, b).then_inc(q_made, 1)
                pe.wait_ge(hq_done, b + 1)
                if b >= 1:
                    pe.wait_ge(o_done, b)
                for k in range(TPB):
                    last = nc.tensor.matmul(po[:, 128 * k:128 * k + 128], hqT[0:HID + 1, 128 * k:128 * k + 128],
                                            w2T[0:HID + 1, :], start=True, stop=True)
                last.then_inc(o_made, 1)

            pe.wait_ge(ones_set, 3)
            for b in range(B):
                if b >= 1:
                    pe.wait_ge(moved, 4 * b)
                hidden_T(paT, z_T, b).then_inc(aT_made, 1)
                for k in range(TPB):
                    nc.tensor.matmul(pa[:, 32 * k:32 * k + 32], z_T[:, b, 128 * k:128 * k + 128], w1T, start=True, stop=False)
                    last = nc.tensor.matmul(pa[:, 32 * k:32 * k + 32], ones_row[0:1, 0:128], b1[0:1, :], start=False, stop=True)
                last.then_inc(a_made, 1)
                pe.wait_ge(hT_done, b + 1)
                nc.tensor.matmul(prT, w2T[0:HID + 1, :], hT[0:HID + 1, :], start=True, stop=True).then_inc(rT_made, 1)
                for k in range(TPB):
                    last = nc.tensor.matmul(pr[:, 128 * k:128 * k + 128], hT[0:HID + 1, 128 * k:128 * k + 128],
                                            w2T[0:HID + 1, :], start=True, stop=True)
                last.then_inc(r_made, 1)
                if b >= 1:
                    output(b - 1)
                pe.wait_ge(r_done, 2 * b + 1)
                for k in range(TPB):
                    last = nc.tensor.matmul(pd[:, 32 * k:32 * k + 32], r_T[:, 128 * k:128 * k + 128], w2, start=True, stop=True)
                last.then_inc(dh_made, 1)
                pe.wait_ge(r_done, 2 * b + 2)
                pe.wait_ge(h_ready, b + 1)
                for k in range(TPB):
                    nc.tensor.matmul(g_w2, r_nat[:, 128 * k:128 * k + 128], h_one[:, k, 0:HID], start=(k == 0), stop=(k == TPB - 1))
                for k in range(TPB):
                    last = nc.tensor.matmul(g_w2T, h_one[:, k, :], r_nat[:, 128 * k:128 * k + 128], start=(k == 0), stop=(k == TPB - 1))
                last.then_inc(grad2, 1)
                pe.wait_ge(da_done, b + 1)
                for k in range(TPB):
                    nc.tensor.matmul(g_w1, z_nat[:, b, 128 * k:128 * k + 128], d_a[:, 32 * k:32 * k + 32],
                                     start=(k == 0), stop=(k == TPB - 1))
                for k in range(TPB):
                    last = nc.tensor.matmul(g_b1, c.ones[:, 0:1], d_a[:, 32 * k:32 * k + 32], start=(k == 0), stop=(k == TPB - 1))
                last.then_inc(grad1, 1)
            pe.wait_ge(moved, 4 * B)
            output(B - 1)

        @block.scalar
        def _(act):
            def query(b):
                act.wait_ge(q_made, b + 1)
                if b >= 1:
                    act.wait_ge(o_made, b)
                nc.scalar.activation(hqT[0:HID, :], pq[0:HID, :], ACT.Gelu).then_inc(hq_done, 1)

            for b in range(B):
                act.wait_ge(aT_made, b + 1)
                if b >= 1:
                    act.wait_ge(r_made, b)
                nc.scalar.activation(hT[0:HID, :], paT[0:HID, :], ACT.Gelu).then_inc(hT_done, 1)
                act.wait_ge(safe_ready, b + 1)
                nc.scalar.activation(gel, a_safe, ACT.Gelu).then_inc(gel_done, 1)
                nc.scalar.activation(th, a_sq, ACT.Tanh, scale=0.25).then_inc(gel_done, 1)
                if b >= 1:
                    query(b - 1)
            query(B - 1)

        @block.vector
        def _(dve):
            nc.vector.memset(hT[HID:HID + 1, :], 1.0).then_inc(ones_set, 1)
            nc.vector.memset(hqT[HID:HID + 1, :], 1.0).then_inc(ones_set, 1)
            nc.vector.memset(h_one[:, :, HID:HID + 1], 1.0).then_inc(ones_set, 1)
            ch = Chain(dve, step)
            tt, ts, stt = nc.vector.tensor_tensor, nc.vector.tensor_scalar, nc.vector.scalar_tensor_tensor

            def output(b):
                dve.wait_ge(o_made, b + 1)
                o = flat(c.o[:, TPB * b:TPB * b + TPB, :])
                tt(o, o, po, ALU.add).then_inc(o_done, 1)

            for b in range(B):
                dve.wait_ge(a_made, b + 1)
                ch.next(nc.vector.tensor_copy(a, pa[:, 0:128]))
                ch.next(tt(a_sq, a, a, ALU.mult))
                ch.next(ts(a_off, a_sq, TINY * TINY, 4 * TINY, ALU.is_lt, ALU.mult))
                tt(a_safe, a, a_off, ALU.add).then_inc(safe_ready, 1)
                dve.wait_ge(safe_ready, b + 1)
                nc.vector.reciprocal(inv, a_safe).then_inc(step, 1)
                ch.at += 1
                dve.wait_ge(gel_done, 2 * b + 1)
                ch.wait()
                ch.next(tt(phi, gel, inv, ALU.mult))
                tt(h_one[:, :, 0:HID], tiles(a), tiles(phi), ALU.mult).then_inc(h_ready, 1)
                dve.wait_ge(rT_made, b + 1)
                tt(r_T, zy_T[:, b, :], prT, ALU.add).then_inc(r_done, 1)
                dve.wait_ge(r_made, b + 1)
                tt(r_nat, zy_nat[:, b, :], pr, ALU.add).then_inc(r_done, 1)
                dve.wait_ge(gel_done, 2 * b + 2)
                ch.next(ts(high, th, 1.0, None, ALU.add))
                ch.next(nc.vector.reciprocal(dens, high))
                ch.next(ts(low, th, -1.0, 1.0, ALU.mult, ALU.add))
                ch.next(tt(dens, dens, low, ALU.mult))
                ch.next(stt(slope, dens, 0.3989422804014327, a, op0=ALU.mult, op1=ALU.mult))
                ch.next(tt(slope, slope, phi, ALU.add))
                dve.wait_ge(dh_made, b + 1)
                tt(d_a, pd[:, 0:128], slope, ALU.mult).then_inc(da_done, 1)
                if b >= 1:
                    output(b - 1)
                dve.wait_ge(grad2, b + 1)
                stt(w2, g_w2, -STEP, w2, op0=ALU.mult, op1=ALU.add).then_inc(moved, 1)
                stt(w2T[0:HID + 1, :], g_w2T, -STEP, w2T[0:HID + 1, :], op0=ALU.mult, op1=ALU.add).then_inc(moved, 1)
                dve.wait_ge(grad1, b + 1)
                stt(w1T, g_w1, -STEP, w1T, op0=ALU.mult, op1=ALU.add).then_inc(moved, 1)
                stt(b1[0:1, :], g_b1, -STEP, b1[0:1, :], op0=ALU.mult, op1=ALU.add).then_inc(moved, 1)
                dve.wait_ge(moved, 4 * b + 4)
            output(B - 1)


EXPERTS, FFN = 8, 512
CHUNKS = FFN // 128
CAPACITY = TOK // EXPERTS // 2
SLOTS = EXPERTS * CAPACITY
FAR = 1 << 20


class Counting:

    def __init__(self, c):
        self.upto = c.take(64).bitcast(BF16)
        self.all = c.take(64).bitcast(BF16)
        self.goes_on = c.take(EXPERTS * TILES)
        self.expert = c.take(EXPERTS)
        self.built = c.sem("counting_built")

    def build(self, c, pool):
        nc = c.nc
        nc.gpsimd.memset(self.all, 1.0).then_inc(self.built, 1)
        nc.gpsimd.memset(self.goes_on, 1.0).then_inc(self.built, 1)
        pool.wait_ge(self.built, 2)
        nc.gpsimd.affine_select(out=self.upto, in_=self.all, compare_op=ALU.is_ge, fill=0.0, base=0,
                                pattern=[[1, 128]], channel_multiplier=-1).then_inc(self.built, 1)
        nc.gpsimd.memset(self.goes_on.rearrange("p (e t) -> p e t", e=EXPERTS)[:, :, 0:1], 0.0).then_inc(self.built, 1)
        nc.gpsimd.iota(self.expert, pattern=[[1, EXPERTS]], base=0, channel_multiplier=0,
                       allow_small_or_imprecise_dtypes=True).then_inc(self.built, 1)


def by_expert(v):
    return v.rearrange("p (e t) -> p e t", e=EXPERTS)


def over_tiles(v):
    return v.unsqueeze(2).to_broadcast([128, EXPERTS, TILES])


def switch_layer(c, d, n_count):
    nc = c.nc
    sem = lambda name: c.sem(f"sw_{name}")
    rows_in = nc.dram_tensor("sw_rows_in", (SLOTS, D), F32).ap()
    rows_out = nc.dram_tensor("sw_rows_out", (SLOTS, D), F32).ap()
    w_sw, b_sw = c.take(EXPERTS), c.take(EXPERTS)
    w1 = c.take(EXPERTS * FFN).rearrange("p (e f) -> p e f", e=EXPERTS)
    w2 = c.take(EXPERTS * FFN).rearrange("p (e k c) -> p e k c", e=EXPERTS, k=CHUNKS)
    b1_nat, b1T, b2 = c.take(128), c.take(EXPERTS * CHUNKS), c.take(EXPERTS * D)
    row = c.take(TILES).bitcast(I32)
    keep = c.used
    wide = lambda: c.take(EXPERTS * TILES)
    logit, tie, pick, total, upto, slot = (wide() for _ in range(6))
    chosen = c.take(EXPERTS * TILES // 2).bitcast(BF16)
    best, row_f = c.take(TILES), c.take(TILES)
    zeros = c.take(SLOTS)
    small_in, w_in, made, counted = sem("small_in"), sem("w_in"), sem("made"), sem("counted")
    chosen_done, step, zero_set, zero_out, row_done = sem("chosen_done"), sem("step"), sem("zero_set"), sem("zero_out"), sem("row_done")
    sent, b1_turned = sem("sent"), sem("b1_turned")
    tiles_last = lambda v: v.rearrange("p (e t) -> p t e", e=EXPERTS)
    per_tile = lambda v: v.unsqueeze(2).to_broadcast([128, TILES, EXPERTS])
    per_expert = lambda v: v.unsqueeze(1).to_broadcast([128, TILES, EXPERTS])

    with nc.Block() as block:
        @block.sync
        def _(sp):
            sp.dma_start(w_sw, d["L1_ffn_w_switch"]).then_inc(small_in, 16)
            sp.dma_start(b_sw, d["L1_ffn_b_switch"].partition_broadcast(128)).then_inc(small_in, 16)
            sp.dma_start(b1_nat[0:EXPERTS * CHUNKS, :], d["L1_ffn_b1"].rearrange("e (k p) -> (e k) p", p=128)).then_inc(small_in, 16)
            sp.dma_start(b2[0:1, :], d["L1_ffn_b2"].rearrange("(o e) c -> o (e c)", o=1)).then_inc(small_in, 16)
            sp.wait_ge(zero_set, 1)
            sp.dma_start(rows_in.rearrange("(p s) c -> p (s c)", p=128), zeros).then_inc(zero_out, 16)
            sp.dma_start(w1, d["L1_ffn_w1"].rearrange("e p f -> p e f")).then_inc(w_in, 16)
            sp.dma_start(w2, d["L1_ffn_w2"].rearrange("e (k p) c -> p e k c", p=128)).then_inc(w_in, 16)
            sp.wait_ge(small_in, 64)
            sp.wait_ge(w_in, 32)

        @block.tensor
        def _(pe):
            pe.wait_ge(small_in, 64)
            for t in range(TILES):
                b, k = t // TPB, t % TPB
                last = nc.tensor.matmul(c.bank(0)[:, EXPERTS * t:EXPERTS * t + EXPERTS],
                                        c.nT[:, b, 1 + 128 * k:129 + 128 * k], w_sw, start=True, stop=True)
            last.then_inc(made, 1)
            nc.tensor.transpose(c.bank(3)[:, 0:EXPERTS * CHUNKS], b1_nat[0:EXPERTS * CHUNKS, :],
                                c.ident[0:EXPERTS * CHUNKS, 0:EXPERTS * CHUNKS]).then_inc(made, 1)
            pe.wait_ge(chosen_done, 1)
            pe.wait_ge(n_count.built, 5)
            nc.tensor.matmul(c.bank(1)[:, 0:256], n_count.upto, chosen, start=True, stop=True)
            nc.tensor.matmul(c.bank(2)[:, 0:256], n_count.all, chosen, start=True, stop=True).then_inc(counted, 1)

        @block.scalar
        def _(act):
            act.wait_ge(made, 2)
            nc.scalar.activation(b1T, c.bank(3)[:, 0:EXPERTS * CHUNKS], ACT.Copy).then_inc(b1_turned, 1)

        @block.vector
        def _(dve):
            ch = Chain(dve, step)
            tt, ts = nc.vector.tensor_tensor, nc.vector.tensor_scalar
            nc.vector.memset(zeros, 0.0).then_inc(zero_set, 1)
            dve.wait_ge(n_count.built, 5)
            dve.wait_ge(small_in, 64)
            dve.wait_ge(made, 1)
            ch.next(tt(tiles_last(logit), c.bank(0)[:, 0:256].rearrange("p (t e) -> p t e", e=EXPERTS), per_expert(b_sw), ALU.add))
            ch.next(nc.vector.tensor_reduce(best, tiles_last(logit), axis=AX.X, op=ALU.max))
            ch.next(tt(tiles_last(tie), tiles_last(logit), per_tile(best), ALU.is_equal))
            ch.next(ts(slot[:, 0:EXPERTS], n_count.expert, -1.0, float(EXPERTS), ALU.mult, ALU.add))
            ch.next(tt(tiles_last(tie), tiles_last(tie), per_expert(slot[:, 0:EXPERTS]), ALU.mult))
            ch.next(nc.vector.tensor_reduce(best, tiles_last(tie), axis=AX.X, op=ALU.max))
            ch.next(tt(tiles_last(pick), tiles_last(tie), per_tile(best), ALU.is_equal))
            nc.vector.tensor_copy(chosen, pick).then_inc(chosen_done, 1)
            dve.wait_ge(counted, 1)
            ch.next(nc.vector.tensor_copy(total, c.bank(2)[:, 0:256]))
            ch.next(nc.vector.tensor_tensor_scan(upto, n_count.goes_on, total, 0.0, op0=ALU.mult, op1=ALU.add))
            ch.next(tt(upto, upto, total, ALU.subtract))
            ch.next(tt(upto, upto, c.bank(1)[:, 0:256], ALU.add))
            ch.next(ts(tie, upto, float(CAPACITY), float(FAR), ALU.is_gt, ALU.mult))
            ch.next(ts(slot[:, 0:EXPERTS], n_count.expert, float(CAPACITY), -1.0, ALU.mult, ALU.add))
            ch.next(tt(by_expert(upto), by_expert(upto), over_tiles(slot[:, 0:EXPERTS]), ALU.add))
            ch.next(tt(upto, upto, tie, ALU.add))
            ch.next(tt(upto, upto, pick, ALU.mult))
            ch.next(nc.vector.tensor_reduce(row_f, tiles_last(upto), axis=AX.X, op=ALU.add))
            nc.vector.tensor_copy(row, row_f).then_inc(row_done, 1)

        @block.gpsimd
        def _(pool):
            pool.wait_ge(zero_out, 16)
            pool.wait_ge(row_done, 1)
            for t in range(TILES):
                pool.indirect_dma_start(rows_in, bass.IndirectOffsetOnAxis(ap=row[:, t:t + 1], axis=0), c.n[:, t, :], None,
                                        bounds_check=SLOTS - 1, oob_is_err=False).then_inc(sent, 16)
            pool.wait_ge(sent, 16 * TILES)

    c.used = keep
    PER = CAPACITY // 128
    x_nat = c.take(SLOTS).rearrange("p (s c) -> p s c", c=D)
    y_nat = c.take(SLOTS).rearrange("p (s c) -> p s c", c=D)
    xT = c.take(2 * CAPACITY).rearrange("p (r s) -> p r s", r=2)
    hT = c.take(2 * CHUNKS * CAPACITY).rearrange("p (r k s) -> p r k s", r=2, k=CHUNKS)
    x_in, x_turned, xT_done, h_made, h_done = (sem(s) for s in ("x_in", "x_turned", "xT_done", "h_made", "h_done"))
    y_made, y_done, y_out, passed, fetched = (sem(s) for s in ("y_made", "y_done", "y_out", "passed", "fetched"))
    with nc.Block() as block:
        @block.sync
        def _(sp):
            sp.dma_start(x_nat, rows_in.rearrange("(s p) c -> p s c", p=128)).then_inc(x_in, 16)
            for e in range(EXPERTS):
                sp.wait_ge(y_done, e + 1)
                sp.dma_start(rows_out[CAPACITY * e:CAPACITY * (e + 1), :].rearrange("(s p) c -> p s c", p=128),
                             y_nat[:, PER * e:PER * (e + 1), :]).then_inc(y_out, 16)
            sp.wait_ge(y_out, 16 * EXPERTS)

        @block.tensor
        def _(pe):
            def turn(e):
                if e >= 2:
                    pe.wait_ge(xT_done, e - 1)
                for s in range(PER):
                    last = nc.tensor.transpose(c.bank(e % 2)[:, 128 * s:128 * s + 128], x_nat[:, PER * e + s, :], c.ident)
                last.then_inc(x_turned, 1)

            def up(e):
                pe.wait_ge(xT_done, e + 1)
                for k in range(CHUNKS):
                    if k % 2 == 0 and e >= 1:
                        pe.wait_ge(h_done, CHUNKS * (e - 1) + k + 2)
                    last = nc.tensor.matmul(c.bank(2 + k // 2)[:, CAPACITY * (k % 2):CAPACITY * (k % 2) + CAPACITY],
                                            w1[:, e, 128 * k:128 * k + 128], xT[:, e % 2, :], start=True, stop=True)
                    if k % 2:
                        last.then_inc(h_made, 1)

            def down(e):
                pe.wait_ge(h_done, CHUNKS * e + CHUNKS)
                if e >= 2:
                    pe.wait_ge(y_done, e - 1)
                for s in range(PER):
                    out = c.bank(4 + e % 2)[:, 128 * s:128 * s + 128]
                    for k in range(CHUNKS):
                        nc.tensor.matmul(out, hT[:, e % 2, k, 128 * s:128 * s + 128], w2[:, e, k, :], start=(k == 0), stop=False)
                    last = nc.tensor.matmul(out, c.ones[0:1, :], b2[0:1, D * e:D * e + D], start=False, stop=True)
                last.then_inc(y_made, 1)

            pe.wait_ge(x_in, 16)
            turn(0)
            for e in range(EXPERTS):
                if e + 1 < EXPERTS:
                    turn(e + 1)
                up(e)
                if e >= 1:
                    down(e - 1)
            down(EXPERTS - 1)

        @block.scalar
        def _(act):
            for e in range(EXPERTS):
                act.wait_ge(x_turned, e + 1)
                if e >= 2:
                    act.wait_ge(h_made, 2 * (e - 1))
                nc.scalar.activation(xT[:, e % 2, :], c.bank(e % 2)[:, 0:CAPACITY], ACT.Copy).then_inc(xT_done, 1)
                for k in range(CHUNKS):
                    act.wait_ge(h_made, 2 * e + k // 2 + 1)
                    if e >= 2:
                        act.wait_ge(y_made, e - 1)
                    nc.scalar.activation(hT[:, e % 2, k, :], c.bank(2 + k // 2)[:, CAPACITY * (k % 2):CAPACITY * (k % 2) + CAPACITY],
                                         ACT.Relu, bias=b1T[:, CHUNKS * e + k:CHUNKS * e + k + 1]).then_inc(h_done, 1)

        @block.vector
        def _(dve):
            nc.vector.tensor_copy(c.o, c.n).then_inc(passed, 1)
            for e in range(EXPERTS):
                dve.wait_ge(y_made, e + 1)
                nc.vector.tensor_copy(y_nat[:, PER * e:PER * (e + 1), :].rearrange("p s c -> p (s c)"),
                                      c.bank(4 + e % 2)[:, 0:PER * 128]).then_inc(y_done, 1)

        @block.gpsimd
        def _(pool):
            pool.wait_ge(passed, 1)
            pool.wait_ge(y_out, 16 * EXPERTS)
            for t in range(TILES):
                pool.indirect_dma_start(c.o[:, t, :], None, rows_out, bass.IndirectOffsetOnAxis(ap=row[:, t:t + 1], axis=0),
                                        bounds_check=SLOTS - 1, oob_is_err=False).then_inc(fetched, 16)
            pool.wait_ge(fetched, 16 * TILES)


def linear_attention(c, d):
    nc = c.nc
    sem = lambda name: c.sem(f"lin_{name}")
    QK = 2 * D
    ring = lambda n: c.take(2 * TPB * n).rearrange("p (s t c) -> p s t c", s=2, t=TPB)
    qk, sq, v_one = ring(QK), ring(QK), ring(D + 2)
    norm = c.take(2 * TPB * 32).rearrange("p (s h) -> p s h", s=2)
    half = c.take(TPB * 32)
    qT = c.take(2 * S).rearrange("p (s t) -> p s t", s=2)
    kv = c.take(2 * (D + HEADS)).rearrange("p (s c) -> p s c", s=2)
    k_sum, head_mask, block_mask = c.take(2), c.take(HEADS), c.take(D)
    recip = c.take(2 * TPB * HEADS).rearrange("p (s h) -> p s h", s=2)
    made, qk_out, v_out, sq_done, ss_done, root, inv_done, unit = (sem(s) for s in (
        "made", "qk_out", "v_out", "sq_done", "ss_done", "root", "inv_done", "unit"))
    expd, soft, kv_made, kv_done, qT_made, qT_done, o_made, o_done = (sem(s) for s in (
        "expd", "soft", "kv_made", "kv_done", "qT_made", "qT_done", "o_made", "o_done"))
    masks, step = sem("masks"), sem("step")
    heads = lambda v: v.rearrange("p t (h d) -> p (t h) d", d=HD)
    OW = D + HEADS

    with nc.Block() as block:
        @block.gpsimd
        def _(pool):
            nc.gpsimd.memset(half, 0.5).then_inc(masks, 1)
            nc.gpsimd.memset(head_mask, 1.0).then_inc(masks, 1)
            pool.wait_ge(masks, 2)
            nc.gpsimd.affine_select(out=head_mask, in_=head_mask, compare_op=ALU.is_ge, fill=0.0, base=0,
                                    pattern=[[-HD, HEADS]], channel_multiplier=1).then_inc(masks, 1)
            pool.wait_ge(masks, 3)
            nc.gpsimd.affine_select(out=head_mask, in_=head_mask, compare_op=ALU.is_ge, fill=0.0, base=HD - 1,
                                    pattern=[[HD, HEADS]], channel_multiplier=-1).then_inc(masks, 1)
            pool.wait_ge(masks, 4)
            nc.gpsimd.tensor_copy(block_mask.rearrange("p (h d) -> p h d", d=HD),
                                  head_mask.unsqueeze(2).to_broadcast([128, HEADS, HD])).then_inc(masks, 1)
            for b in range(B):
                pool.wait_ge(ss_done, b + 1)
                nc.gpsimd.tensor_tensor(norm[:, b % 2, :], norm[:, b % 2, :], half, ALU.pow).then_inc(root, 1)

        @block.tensor
        def _(pe):
            def project(b):
                for k in range(TPB):
                    n = TPB * b + k
                    if n >= 3:
                        pe.wait_ge(qk_out, n - 2)
                        pe.wait_ge(v_out, n - 2)
                    nc.tensor.matmul(c.bank(n % 3)[:, 0:3 * D], c.nT[:, b, 1 + 128 * k:129 + 128 * k],
                                     c.wT[:, W_QKV2:W_QKV2 + 3, :].rearrange("p w c -> p (w c)"), start=True, stop=True).then_inc(made, 1)

            def finish(b):
                pe.wait_ge(soft, b + 1)
                if b >= 1:
                    pe.wait_ge(kv_done, b)
                    pe.wait_ge(qT_done, b)
                for k in range(TPB):
                    last = nc.tensor.matmul(c.bank(3)[:, 0:D + 1], qk[:, b % 2, k, D:QK], v_one[:, b % 2, k, 0:D + 1],
                                            start=(k == 0), stop=(k == TPB - 1))
                last.then_inc(kv_made, 1)
                for k in range(TPB):
                    last = nc.tensor.transpose(c.bank(4)[:, 128 * k:128 * k + 128], qk[:, b % 2, k, 0:D], c.ident)
                last.then_inc(qT_made, 1)
                pe.wait_ge(kv_done, b + 1)
                pe.wait_ge(qT_done, b + 1)
                if b >= 1:
                    pe.wait_ge(o_done, b)
                for k in range(TPB):
                    last = nc.tensor.matmul(c.bank(5 + k // 2)[:, OW * (k % 2):OW * (k % 2) + OW], qT[:, b % 2, 128 * k:128 * k + 128],
                                            kv[:, b % 2, :], start=True, stop=True)
                last.then_inc(o_made, 1)

            for b in range(B):
                project(b)
                if b >= 1:
                    finish(b - 1)
            finish(B - 1)

        @block.scalar
        def _(act):
            def soften(b):
                act.wait_ge(unit, b + 1)
                nc.scalar.activation(sq[:, b % 2], qk[:, b % 2], ACT.Exp).then_inc(expd, 1)
                act.wait_ge(expd, b + 1)
                nc.scalar.activation(qk[:, b % 2], sq[:, b % 2], ACT.Ln, bias=1.0).then_inc(soft, 1)

            def turn(b):
                act.wait_ge(qT_made, b + 1)
                if b >= 2:
                    act.wait_ge(o_made, b - 1)
                nc.scalar.activation(qT[:, b % 2, :], c.bank(4), ACT.Copy).then_inc(qT_done, 1)

            for b in range(B):
                for k in range(TPB):
                    n = TPB * b + k
                    act.wait_ge(made, n + 1)
                    if b >= 2 and k == 0:
                        act.wait_ge(qT_made, b - 1)
                    nc.scalar.activation(qk[:, b % 2, k, :], c.bank(n % 3)[:, 0:QK], ACT.Copy).then_inc(qk_out, 1)
                act.wait_ge(qk_out, TPB * (b + 1))
                nc.scalar.activation(sq[:, b % 2], qk[:, b % 2], ACT.Square).then_inc(sq_done, 1)
                if b >= 1:
                    soften(b - 1)
                    turn(b - 1)
            soften(B - 1)
            turn(B - 1)

        @block.vector
        def _(dve):
            ch = Chain(dve, step)
            nc.vector.memset(v_one[:, :, :, D:D + 1], 1.0).then_inc(step, 1)
            ch.at += 1
            dve.wait_ge(masks, 5)

            def mask(b):
                dve.wait_ge(kv_made, b + 1)
                if b >= 2:
                    dve.wait_ge(o_made, b - 1)
                ch.next(nc.vector.tensor_scalar(k_sum[:, 0:1], c.bank(3)[:, D:D + 1], 1e-6, None, ALU.add))
                ch.next(nc.vector.scalar_tensor_tensor(kv[:, b % 2, 0:D], c.bank(3)[:, 0:D], float(HD) ** -0.5, block_mask,
                                                       op0=ALU.mult, op1=ALU.mult))
                nc.vector.tensor_scalar(kv[:, b % 2, D:OW], head_mask, k_sum[:, 0:1], None, ALU.mult).then_inc(kv_done, 1)

            def output(b):
                dve.wait_ge(o_made, b + 1)
                for k in range(2):
                    o = c.bank(5 + k)[:, 0:2 * OW].rearrange("p (t c) -> p t c", t=2)
                    r = recip[:, k, 0:2 * HEADS].rearrange("p (t h) -> p t h", t=2)
                    ch.next(nc.vector.reciprocal(r, o[:, :, D:OW]))
                    t = TPB * b + 2 * k
                    last = nc.vector.tensor_tensor(c.o[:, t:t + 2, :].rearrange("p t (h d) -> p t h d", d=HD),
                                                   o[:, :, 0:D].rearrange("p t (h d) -> p t h d", d=HD),
                                                   r.unsqueeze(3).to_broadcast([128, 2, HEADS, HD]), ALU.mult)
                    if k == 0:
                        ch.mark(last)
                ch.wait()
                last.then_inc(o_done, 1)

            for b in range(B):
                for k in range(TPB):
                    n = TPB * b + k
                    dve.wait_ge(made, n + 1)
                    dve.wait_ge(qk_out, n + 1)
                    if b >= 2 and k == 0:
                        dve.wait_ge(kv_made, b - 1)
                    nc.vector.tensor_copy(v_one[:, b % 2, k, 0:D], c.bank(n % 3)[:, QK:3 * D]).then_inc(v_out, 1)
                dve.wait_ge(sq_done, b + 1)
                if b >= 2:
                    dve.wait_ge(unit, b - 1)
                nc.vector.tensor_reduce(norm[:, b % 2, :], heads(sq[:, b % 2]), axis=AX.X, op=ALU.add).then_inc(ss_done, 1)
                dve.wait_ge(root, b + 1)
                ch.next(nc.vector.tensor_scalar(norm[:, b % 2, :], norm[:, b % 2, :], 1e-12, None, ALU.max))
                ch.next(nc.vector.reciprocal(norm[:, b % 2, :], norm[:, b % 2, :]))
                nc.vector.tensor_tensor(heads(qk[:, b % 2]), heads(qk[:, b % 2]),
                                        norm[:, b % 2, :].unsqueeze(2).to_broadcast([128, TPB * 32, HD]), ALU.mult).then_inc(unit, 1)
                if b >= 1:
                    mask(b - 1)
                    output(b - 1)
            mask(B - 1)
            output(B - 1)


BITS = 30
KEPT = TOK // EXPERTS
PICKS = TOK // 128
PER_EXPERT = KEPT // 128


def expert_choice(c, d, n_count):
    nc = c.nc
    sem = lambda name: c.sem(f"ec_{name}")
    gate_nat, gateT = c.take(128), c.take(EXPERTS)
    idx = c.take(PICKS).bitcast(I32)
    weight = c.take(PICKS)
    lnw, lnb = c.take(1), c.take(1)
    b1_nat, b1T, b2 = c.take(128), c.take(EXPERTS * CHUNKS), c.take(EXPERTS * D)
    normed = nc.dram_tensor("ec_normed", (TOK, D), F32).ap()
    result = nc.dram_tensor("ec_result", (TOK, D), F32).ap()
    keep = c.used
    wide = lambda: c.take(EXPERTS * TILES)
    half_wide = lambda: c.take(EXPERTS * TILES // 2).bitcast(BF16)
    score, above, equal, total, place, chosen, work = (wide() for _ in range(7))
    mask_a, mask_b = half_wide(), half_wide()
    best = c.take(TILES)
    limit, cand, bump = (c.take(EXPERTS).bitcast(I32) for _ in range(3))
    count, need = c.take(EXPERTS), c.take(EXPERTS)
    count_bf = c.take(EXPERTS // 2).bitcast(BF16)
    lane, slot_tile = wide(), wide()
    whole, cand_wide = wide().bitcast(I32), wide().bitcast(I32)
    iota128, iota4, p_id, t_id = c.take(128), c.take(4), c.take(1), c.take(TILES)
    one_hot = c.take(2 * TILES * 64).bitcast(BF16).rearrange("p (s t a) -> p s t a", s=2, t=TILES)
    VALS = 5
    vals = c.take(2 * TILES * 4 * VALS // 2).bitcast(BF16).rearrange("p (s t v b) -> p s t v b", s=2, t=TILES, v=VALS)
    here = c.take(2 * TILES * 4).rearrange("p (s t b) -> p s t b", s=2, t=TILES)
    w_part = c.take(3 * EXPERTS * TILES // 2).bitcast(BF16).rearrange("p (v e) -> p v e", v=3)
    w_left = wide()
    found = c.take(EXPERTS * 4 * VALS).rearrange("p (e v b) -> p e v b", e=EXPERTS, v=VALS)
    small_in, made, turned, gate_done, step, expd = (sem(s) for s in ("small_in", "made", "turned", "gate_done", "step", "expd"))
    counted, counts = sem("counted"), sem("counts")
    ids, tallied, mask_done, hot, hot_used, xf_out, idx_done = (sem(s) for s in (
        "ids", "tallied", "mask_done", "hot", "hot_used", "xf_out", "idx_done"))
    y_stats, y_mv, y_rstd, y_step, yn_done = (sem(s) for s in ("y_stats", "y_mv", "y_rstd", "y_step", "yn_done"))
    tiles_last = lambda v: v.rearrange("p (e t) -> p t e", e=EXPERTS)
    per_tile = lambda v: v.unsqueeze(2).to_broadcast([128, TILES, EXPERTS])

    with nc.Block() as block:
        @block.sync
        def _(sp):
            sp.dma_start(gate_nat[0:EXPERTS, :], d["L2_ffn_gate_w"]).then_inc(small_in, 16)
            sp.dma_start(b1_nat[0:EXPERTS * CHUNKS, :], d["L2_ffn_b1s"].rearrange("e (k p) -> (e k) p", p=128)).then_inc(small_in, 16)
            sp.dma_start(b2[0:1, :], d["L2_ffn_b2s"].rearrange("(o e) c -> o (e c)", o=1)).then_inc(small_in, 16)
            sp.dma_start(lnw, d["L2_ffn_ln_w"].rearrange("(c o) -> c o", o=1)).then_inc(small_in, 16)
            sp.dma_start(lnb, d["L2_ffn_ln_b"].rearrange("(c o) -> c o", o=1)).then_inc(small_in, 16)
            sp.dma_start(result.rearrange("(t p) c -> p t c", p=128), c.n).then_inc(xf_out, 16)
            sp.wait_ge(yn_done, TILES)
            sp.dma_start(normed.rearrange("(t p) c -> p t c", p=128), c.o).then_inc(xf_out, 16)
            sp.wait_ge(small_in, 80)
            sp.wait_ge(xf_out, 32)

        @block.gpsimd
        def _(pool):
            io = dict(allow_small_or_imprecise_dtypes=True)
            nc.gpsimd.iota(iota128, pattern=[[1, 128]], base=0, channel_multiplier=0, **io).then_inc(ids, 1)
            nc.gpsimd.iota(iota4, pattern=[[1, 4]], base=0, channel_multiplier=0, **io).then_inc(ids, 1)
            nc.gpsimd.iota(p_id, pattern=[[0, 1]], base=0, channel_multiplier=1, **io).then_inc(ids, 1)
            nc.gpsimd.iota(t_id, pattern=[[1, TILES]], base=0, channel_multiplier=0, **io).then_inc(ids, 1)
            pool.wait_ge(y_mv, TILES)
            nc.gpsimd.tensor_scalar(c.var_eps, c.mv[:, :, 1], LN_EPS, None, ALU.add).then_inc(y_step, 1)
            pool.wait_ge(y_step, 1)
            nc.gpsimd.tensor_tensor(c.rstd, c.var_eps, c.minus_half, ALU.pow).then_inc(y_rstd, 1)

        @block.tensor
        def _(pe):
            pe.wait_ge(small_in, 80)
            nc.tensor.transpose(c.bank(7)[:, 0:EXPERTS], gate_nat[0:EXPERTS, :], c.ident[0:EXPERTS, 0:EXPERTS])
            nc.tensor.transpose(c.bank(7)[:, 32:64], b1_nat[0:EXPERTS * CHUNKS, :],
                                c.ident[0:EXPERTS * CHUNKS, 0:EXPERTS * CHUNKS]).then_inc(turned, 1)
            pe.wait_ge(gate_done, 1)
            for t in range(TILES):
                b, k = t // TPB, t % TPB
                last = nc.tensor.matmul(c.bank(0)[:, EXPERTS * t:EXPERTS * t + EXPERTS],
                                        c.nT[:, b, 1 + 128 * k:129 + 128 * k], gateT, start=True, stop=True)
            last.then_inc(made, 1)
            for n in range(BITS):
                pe.wait_ge(counts, n + 1)
                nc.tensor.matmul(c.bank(1)[:, 0:EXPERTS], n_count.all, count_bf, start=True, stop=True).then_inc(counted, 1)
            pe.wait_ge(mask_done, 2)
            nc.tensor.matmul(c.bank(2)[:, 0:256], n_count.all, mask_a, start=True, stop=True)
            nc.tensor.matmul(c.bank(3)[:, 0:256], n_count.all, mask_b, start=True, stop=True)
            nc.tensor.matmul(c.bank(4)[:, 0:256], n_count.upto, mask_b, start=True, stop=True).then_inc(tallied, 1)
            pe.wait_ge(mask_done, 3)
            nc.tensor.matmul(c.bank(2)[:, 0:256], n_count.all, mask_a, start=True, stop=True)
            nc.tensor.matmul(c.bank(3)[:, 0:256], n_count.upto, mask_a, start=True, stop=True).then_inc(tallied, 1)
            for e in range(EXPERTS):
                pe.wait_ge(hot, 2 * e + 2)
                for t in range(TILES):
                    last = nc.tensor.matmul(c.bank(5)[:, 20 * e:20 * e + 20], one_hot[:, e % 2, t, :],
                                            vals[:, e % 2, t].rearrange("p v b -> p (v b)"), start=(t == 0), stop=(t == TILES - 1))
                last.then_inc(hot_used, 1)

        @block.scalar
        def _(act):
            act.wait_ge(turned, 1)
            nc.scalar.activation(b1T, c.bank(7)[:, 32:64], ACT.Copy)
            nc.scalar.activation(gateT, c.bank(7)[:, 0:EXPERTS], ACT.Copy).then_inc(gate_done, 1)
            act.wait_ge(step, 2)
            nc.scalar.activation(score, work, ACT.Exp).then_inc(expd, 1)

        @block.vector
        def _(dve):
            ch = Chain(dve, step)
            tt, ts = nc.vector.tensor_tensor, nc.vector.tensor_scalar
            dve.wait_ge(made, 1)
            logits = c.bank(0)[:, 0:256].rearrange("p (t e) -> p t e", e=EXPERTS)
            ch.next(nc.vector.tensor_reduce(best, logits, axis=AX.X, op=ALU.max))
            ch.next(tt(tiles_last(work), logits, per_tile(best), ALU.subtract))
            for t in range(TILES):
                nc.vector.bn_stats(c.stats[:, t, :], c.n[:, t, :]).then_inc(y_stats, 1)
            dve.wait_ge(y_stats, TILES)
            for t in range(TILES):
                nc.vector.bn_aggr(c.mv[:, t, :], c.stats[:, t, :]).then_inc(y_mv, 1)
            dve.wait_ge(expd, 1)
            ch.next(nc.vector.tensor_reduce(best, tiles_last(score), axis=AX.X, op=ALU.add))
            ch.next(nc.vector.reciprocal(best, best))
            ch.next(tt(tiles_last(score), tiles_last(score), per_tile(best), ALU.mult))
            dve.wait_ge(y_rstd, 1)
            for t in range(TILES):
                ts(c.o[:, t, :], c.n[:, t, :], c.mv[:, t, 0:1], c.rstd[:, t:t + 1], ALU.subtract, ALU.mult).then_inc(yn_done, 1)
            ch.next(nc.vector.memset(limit, 0))
            for n in range(BITS):
                bit = 1 << (BITS - 1 - n)
                ch.next(ts(cand, limit, bit, None, ALU.bitwise_or))
                ch.next(tt(by_expert(above), by_expert(score), over_tiles(cand.bitcast(F32)), ALU.is_ge))
                with nc.allow_low_precision(reason="whole numbers up to TILES"):
                    nc.vector.tensor_reduce(count_bf, by_expert(above), axis=AX.X, op=ALU.add).then_inc(counts, 1)
                dve.wait_ge(counted, n + 1)
                ch.next(ts(bump, c.bank(1)[:, 0:EXPERTS], float(KEPT), float(bit), ALU.is_ge, ALU.mult))
                ch.next(tt(limit, limit, bump, ALU.bitwise_or))
            lim = over_tiles(limit.bitcast(F32))
            ch.next(tt(by_expert(above), by_expert(score), lim, ALU.is_gt))
            ch.next(tt(by_expert(equal), by_expert(score), lim, ALU.is_equal))
            nc.vector.tensor_copy(mask_a, above).then_inc(mask_done, 1)
            nc.vector.tensor_copy(mask_b, equal).then_inc(mask_done, 1)
            dve.wait_ge(tallied, 1)
            ch.next(nc.vector.tensor_reduce(count, by_expert(c.bank(2)[:, 0:256]), axis=AX.X, op=ALU.add))
            ch.next(ts(need, count, -1.0, float(KEPT), ALU.mult, ALU.add))
            ch.next(nc.vector.tensor_copy(total, c.bank(3)[:, 0:256]))
            ch.next(nc.vector.tensor_tensor_scan(place, n_count.goes_on, total, 0.0, op0=ALU.mult, op1=ALU.add))
            ch.next(tt(place, place, total, ALU.subtract))
            ch.next(tt(place, place, c.bank(4)[:, 0:256], ALU.add))
            ch.next(tt(by_expert(work), by_expert(place), over_tiles(need), ALU.is_le))
            ch.next(tt(work, work, equal, ALU.mult))
            ch.next(tt(chosen, work, above, ALU.add))
            nc.vector.tensor_copy(mask_a, chosen).then_inc(mask_done, 1)
            dve.wait_ge(tallied, 2)
            ch.next(nc.vector.tensor_copy(total, c.bank(2)[:, 0:256]))
            ch.next(nc.vector.memset(work, 1.0))
            ch.next(nc.vector.tensor_tensor_scan(place, work, total, 0.0, op0=ALU.mult, op1=ALU.add))
            ch.next(tt(place, place, total, ALU.subtract))
            ch.next(tt(place, place, c.bank(3)[:, 0:256], ALU.add))
            ch.next(tt(place, place, chosen, ALU.subtract))
            ch.next(nc.vector.tensor_copy(whole, place))
            ch.next(ts(cand_wide, whole, 127, None, ALU.bitwise_and))
            ch.next(nc.vector.tensor_copy(lane, cand_wide))
            ch.next(ts(whole, whole, 7, None, ALU.logical_shift_right))
            ch.next(nc.vector.tensor_copy(slot_tile, whole))
            ch.next(ts(lane, lane, 1.0, None, ALU.add))
            ch.next(tt(lane, lane, chosen, ALU.mult))
            ch.next(ts(lane, lane, -1.0, None, ALU.add))
            ch.next(nc.vector.tensor_copy(w_part[:, 0, :], score))
            ch.next(tt(w_left, score, w_part[:, 0, :], ALU.subtract))
            ch.next(nc.vector.tensor_copy(w_part[:, 1, :], w_left))
            ch.next(tt(w_part[:, 2, :], w_left, w_part[:, 1, :], ALU.subtract))
            dve.wait_ge(ids, 4)
            for e in range(EXPERTS):
                at = slice(TILES * e, TILES * e + TILES)
                s = e % 2
                if e >= 2:
                    dve.wait_ge(hot_used, e - 1)
                tt(one_hot[:, s], lane[:, at].unsqueeze(2).to_broadcast([128, TILES, 128]),
                   iota128.unsqueeze(1).to_broadcast([128, TILES, 128]), ALU.is_equal).then_inc(hot, 1)
                four = lambda v: v.unsqueeze(2).to_broadcast([128, TILES, 4])
                ch.next(ts(work[:, 0:TILES], slot_tile[:, at], float(-PER_EXPERT * e), None, ALU.add))
                ch.next(tt(here[:, s], four(work[:, 0:TILES]), iota4.unsqueeze(1).to_broadcast([128, TILES, 4]), ALU.is_equal))
                ch.mark(tt(vals[:, s, :, 0, :], here[:, s], p_id.unsqueeze(2).to_broadcast([128, TILES, 4]), ALU.mult))
                ch.mark(tt(vals[:, s, :, 1, :], here[:, s], four(t_id), ALU.mult))
                for v in range(2):
                    ch.mark(tt(vals[:, s, :, 2 + v, :], here[:, s], four(w_part[:, v, at]), ALU.mult))
                ch.wait()
                tt(vals[:, s, :, 4, :], here[:, s], four(w_part[:, 2, at]), ALU.mult).then_inc(hot, 1)
            dve.wait_ge(hot_used, EXPERTS)
            ch.next(nc.vector.tensor_copy(found.rearrange("p e v b -> p (e v b)"), c.bank(5)[:, 0:20 * EXPERTS]))
            by_slot = lambda v: v.rearrange("p (e b) -> p e b", e=EXPERTS)
            ch.next(nc.vector.scalar_tensor_tensor(by_slot(work[:, 0:PICKS]), found[:, :, 1, :], 128.0, found[:, :, 0, :],
                                                   op0=ALU.mult, op1=ALU.add))
            ch.next(nc.vector.tensor_copy(idx, work[:, 0:PICKS]))
            ch.next(tt(by_slot(weight), found[:, :, 2, :], found[:, :, 3, :], ALU.add))
            ch.next(tt(by_slot(weight), by_slot(weight), found[:, :, 4, :], ALU.add))

    c.used = keep
    fc1 = c.take(EXPERTS * FFN).rearrange("p (e k c) -> p e k c", e=EXPERTS, k=CHUNKS)
    fc2 = c.take(EXPERTS * FFN).rearrange("p (e f) -> p e f", e=EXPERTS)
    rows = c.take(TOK).rearrange("p (s c) -> p s c", c=D)
    fc1T = c.take(2 * FFN).rearrange("p (r f) -> p r f", r=2)
    fc2T = c.take(2 * FFN).rearrange("p (r k c) -> p r k c", r=2, k=CHUNKS)
    yT = c.take(2 * KEPT).rearrange("p (r s) -> p r s", r=2)
    hT = c.take(2 * CHUNKS * KEPT).rearrange("p (r k s) -> p r k s", r=2, k=CHUNKS)
    out = c.take(2 * KEPT).rearrange("p (r s c) -> p r s c", r=2, c=D)
    w_in, got = sem("w_in"), sem("got")
    w1_turned, w2_turned, w1_done, w2_done, y_turned, yT_done = (sem(s) for s in (
        "w1_turned", "w2_turned", "w1_done", "w2_done", "y_turned", "yT_done"))
    h_made, h_done, o_made, o_done, added, back = (sem(s) for s in ("h_made", "h_done", "o_made", "o_done", "added", "back"))
    with nc.Block() as block:
        @block.sync
        def _(sp):
            sp.dma_start(fc1, d["L2_ffn_fc1s"].rearrange("e (k p) c -> p e k c", p=128)).then_inc(w_in, 16)
            sp.dma_start(fc2, d["L2_ffn_fc2s"].rearrange("e c f -> c e f")).then_inc(w_in, 16)
            sp.wait_ge(w_in, 32)
            sp.wait_ge(added, 16 * PICKS)
            sp.dma_start(c.o, result.rearrange("(t p) c -> p t c", p=128)).then_inc(back, 16)
            sp.wait_ge(back, 16)

        @block.gpsimd
        def _(pool):
            for s in range(PICKS):
                pool.indirect_dma_start(rows[:, s, :], None, normed, bass.IndirectOffsetOnAxis(ap=idx[:, s:s + 1], axis=0),
                                        bounds_check=TOK - 1, oob_is_err=False).then_inc(got, 16)
            for e in range(EXPERTS):
                pool.wait_ge(o_done, PER_EXPERT * (e + 1))
                if e >= 1:
                    pool.wait_ge(added, 16 * PER_EXPERT * e)
                for s in range(PER_EXPERT):
                    n = PER_EXPERT * e + s
                    pool.indirect_dma_start(result, bass.IndirectOffsetOnAxis(ap=idx[:, n:n + 1], axis=0), out[:, e % 2, s, :], None,
                                            bounds_check=TOK - 1, oob_is_err=True, compute_op=ALU.add).then_inc(added, 16)
            pool.wait_ge(added, 16 * PICKS)

        @block.tensor
        def _(pe):
            def prepare(e):
                if e >= 1:
                    pe.wait_ge(w1_done, e)
                    pe.wait_ge(w2_done, e)
                    pe.wait_ge(yT_done, e)
                for k in range(CHUNKS):
                    last = nc.tensor.transpose(c.bank(0)[:, 128 * k:128 * k + 128], fc1[:, e, k, :], c.ident)
                last.then_inc(w1_turned, 1)
                for k in range(CHUNKS):
                    last = nc.tensor.transpose(c.bank(1)[:, 128 * k:128 * k + 128], fc2[:, e, 128 * k:128 * k + 128], c.ident)
                last.then_inc(w2_turned, 1)
                if e == 0:
                    pe.wait_ge(got, 16 * PICKS)
                for s in range(PER_EXPERT):
                    last = nc.tensor.transpose(c.bank(2)[:, 128 * s:128 * s + 128], rows[:, PER_EXPERT * e + s, :], c.ident)
                last.then_inc(y_turned, 1)

            def up(e):
                pe.wait_ge(w1_done, e + 1)
                pe.wait_ge(yT_done, e + 1)
                for k in range(CHUNKS):
                    n = CHUNKS * e + k
                    if n >= 3:
                        pe.wait_ge(h_done, n - 2)
                    nc.tensor.matmul(c.bank(3 + n % 3), fc1T[:, e % 2, 128 * k:128 * k + 128], yT[:, e % 2, :],
                                     start=True, stop=True).then_inc(h_made, 1)

            def down(e):
                pe.wait_ge(h_done, CHUNKS * e + CHUNKS)
                pe.wait_ge(w2_done, e + 1)
                if e >= 2:
                    pe.wait_ge(o_done, PER_EXPERT * (e - 1))
                for s in range(PER_EXPERT):
                    o = c.bank(6 + e % 2)[:, 128 * s:128 * s + 128]
                    for k in range(CHUNKS):
                        nc.tensor.matmul(o, hT[:, e % 2, k, 128 * s:128 * s + 128], fc2T[:, e % 2, k, :], start=(k == 0), stop=False)
                    last = nc.tensor.matmul(o, c.ones[0:1, :], b2[0:1, D * e:D * e + D], start=False, stop=True)
                last.then_inc(o_made, 1)

            pe.wait_ge(w_in, 32)
            prepare(0)
            for e in range(EXPERTS):
                if e + 1 < EXPERTS:
                    prepare(e + 1)
                up(e)
                if e >= 1:
                    down(e - 1)
            down(EXPERTS - 1)

        @block.scalar
        def _(act):
            def tokens(e):
                act.wait_ge(y_turned, e + 1)
                if e >= 2:
                    act.wait_ge(h_made, CHUNKS * (e - 1))
                nc.scalar.activation(yT[:, e % 2, :], c.bank(2), ACT.Identity, bias=lnb, scale=lnw).then_inc(yT_done, 1)

            tokens(0)
            for e in range(EXPERTS):
                if e + 1 < EXPERTS:
                    tokens(e + 1)
                for k in range(CHUNKS):
                    n = CHUNKS * e + k
                    act.wait_ge(h_made, n + 1)
                    if e >= 2:
                        act.wait_ge(o_made, e - 1)
                    nc.scalar.activation(hT[:, e % 2, k, :], c.bank(3 + n % 3), ACT.Gelu_apprx_tanh,
                                         bias=b1T[:, n:n + 1]).then_inc(h_done, 1)

        @block.vector
        def _(dve):
            def weights(e):
                dve.wait_ge(w1_turned, e + 1)
                if e >= 2:
                    dve.wait_ge(h_made, CHUNKS * (e - 1))
                    dve.wait_ge(o_made, e - 1)
                nc.vector.tensor_copy(fc1T[:, e % 2, :], c.bank(0)).then_inc(w1_done, 1)
                dve.wait_ge(w2_turned, e + 1)
                nc.vector.tensor_copy(fc2T[:, e % 2].rearrange("p k c -> p (k c)"), c.bank(1)).then_inc(w2_done, 1)

            def output(e):
                dve.wait_ge(o_made, e + 1)
                if e >= 2:
                    dve.wait_ge(added, 16 * PER_EXPERT * (e - 1))
                for s in range(PER_EXPERT):
                    n = PER_EXPERT * e + s
                    nc.vector.tensor_scalar(out[:, e % 2, s, :], c.bank(6 + e % 2)[:, 128 * s:128 * s + 128],
                                            weight[:, n:n + 1], None, ALU.mult).then_inc(o_done, 1)

            weights(0)
            for e in range(EXPERTS):
                if e + 1 < EXPERTS:
                    weights(e + 1)
                if e >= 1:
                    output(e - 1)
            output(EXPERTS - 1)


def project_heads(c, d):
    nc = c.nc
    sem = lambda name: c.sem(f"out_{name}")
    bias_in, turned, oT_done, made, added = (sem(s) for s in ("bias_in", "turned", "oT_done", "made", "added"))
    bias = c.take(D)
    oT = c.take(2 * S).rearrange("p (s t) -> p s t", s=2)
    with nc.Block() as block:
        @block.sync
        def _(sp):
            sp.dma_start(bias, d["L3_attn_bout"].partition_broadcast(128)).then_inc(bias_in, 16)

        @block.tensor
        def _(pe):
            def turn(b):
                if b >= 2:
                    pe.wait_ge(oT_done, b - 1)
                for k in range(TPB):
                    last = nc.tensor.transpose(c.bank(b % 2)[:, 128 * k:128 * k + 128], c.o[:, TPB * b + k, :], c.ident)
                last.then_inc(turned, 1)

            turn(0)
            for b in range(B):
                if b + 1 < B:
                    turn(b + 1)
                pe.wait_ge(oT_done, b + 1)
                if b >= 2:
                    pe.wait_ge(added, b - 1)
                for k in range(TPB):
                    last = nc.tensor.matmul(c.bank(2 + b % 2)[:, 128 * k:128 * k + 128], oT[:, b % 2, 128 * k:128 * k + 128],
                                            c.wT[:, W_OUT, :], start=True, stop=True)
                last.then_inc(made, 1)

        @block.scalar
        def _(act):
            for b in range(B):
                act.wait_ge(turned, b + 1)
                if b >= 2:
                    act.wait_ge(made, b - 1)
                nc.scalar.activation(oT[:, b % 2, :], c.bank(b % 2), ACT.Copy).then_inc(oT_done, 1)

        @block.vector
        def _(dve):
            dve.wait_ge(bias_in, 16)
            for b in range(B):
                dve.wait_ge(made, b + 1)
                nc.vector.tensor_tensor(c.o[:, TPB * b:TPB * b + TPB, :], c.bank(2 + b % 2).rearrange("p (t c) -> p t c", t=TPB),
                                        bias.unsqueeze(1).to_broadcast([128, TPB, D]), ALU.add).then_inc(added, 1)


MIX = 4


def elastic_mixture(c, d):
    nc = c.nc
    sem = lambda name: c.sem(f"mix_{name}")
    w1 = c.take(MIX * FFN).rearrange("p (e f) -> p e f", e=MIX)
    w2 = c.take(MIX * FFN).rearrange("p (e k c) -> p e k c", e=MIX, k=CHUNKS)
    b1_nat, b1T, b2 = c.take(128), c.take(MIX * CHUNKS), c.take(D)
    wu, bu = c.take(1), c.take(1)
    below, share = c.take(MIX), c.take(MIX)
    u, u4 = c.take(TILES), c.take(TILES)
    w = c.take(TILES * MIX).rearrange("p (t e) -> p t e", e=MIX)
    taken = c.take(TILES * MIX).rearrange("p (t e) -> p t e", e=MIX)
    wT4 = c.take(TOK)
    hT = c.take(2 * CHUNKS * S).rearrange("p (s k t) -> p s k t", s=2, k=CHUNKS)
    w_now = c.take(2 * TPB * MIX).rearrange("p (s t e) -> p s t e", s=2, e=MIX)
    small_in, w1_in, w2_in = sem("small_in"), sem("w1_in"), sem("w2_in")
    u_made, u_done, step, w_turned, wT_done, b2_made, o_started, b1_turned, b1_done = (sem(s) for s in (
        "u_made", "u_done", "step", "w_turned", "wT_done", "b2_made", "o_started", "b1_turned", "b1_done"))
    SMALL = 6
    with nc.Block() as block:
        @block.sync
        def _(sp):
            sp.dma_start(wu, d["L3_ffn_Wu"]).then_inc(small_in, 16)
            sp.dma_start(bu, d["L3_ffn_bu"].partition_broadcast(128)).then_inc(small_in, 16)
            sp.dma_start(below, d["expert_below"]).then_inc(small_in, 16)
            sp.dma_start(share, d["expert_share"]).then_inc(small_in, 16)
            sp.dma_start(b2[0:MIX, :], d["L3_ffn_b2"]).then_inc(small_in, 16)
            sp.dma_start(b1_nat[0:MIX * CHUNKS, :], d["L3_ffn_b1"].rearrange("e (k p) -> (e k) p", p=128)).then_inc(small_in, 16)
            sp.dma_start(w1, d["L3_ffn_W1"].rearrange("e c f -> c e f")).then_inc(w1_in, 16)
            sp.dma_start(w2, d["L3_ffn_W2"].rearrange("e (k p) c -> p e k c", p=128)).then_inc(w2_in, 16)
            sp.wait_ge(w1_in, 16)
            sp.wait_ge(w2_in, 16)

        @block.tensor
        def _(pe):
            pe.wait_ge(small_in, 16 * SMALL)
            for t in range(TILES):
                b, k = t // TPB, t % TPB
                last = nc.tensor.matmul(c.bank(0)[:, t:t + 1], c.nT[:, b, 1 + 128 * k:129 + 128 * k], wu, start=True, stop=True)
            last.then_inc(u_made, 1)
            nc.tensor.transpose(c.bank(1)[:, 0:MIX * CHUNKS], b1_nat[0:MIX * CHUNKS, :],
                                c.ident[0:MIX * CHUNKS, 0:MIX * CHUNKS]).then_inc(b1_turned, 1)
            pe.wait_ge(step, 4)
            for b in range(B):
                if b >= 2:
                    pe.wait_ge(wT_done, b - 1)
                for k in range(TPB):
                    last = nc.tensor.transpose(c.bank(2 + b % 2)[0:MIX, 128 * k:128 * k + 128], w[:, TPB * b + k, :], c.ident)
                last.then_inc(w_turned, 1)
            for b in range(B):
                pe.wait_ge(wT_done, b + 1)
                if b >= 2:
                    pe.wait_ge(o_started, b - 1)
                for k in range(TPB):
                    last = nc.tensor.matmul(c.bank(4 + b % 2)[:, 128 * k:128 * k + 128], wT4[0:MIX, S * b + 128 * k:S * b + 128 * k + 128],
                                            b2[0:MIX, :], start=True, stop=True)
                last.then_inc(b2_made, 1)

        @block.scalar
        def _(act):
            act.wait_ge(small_in, 16 * SMALL)
            act.wait_ge(u_made, 1)
            nc.scalar.activation(u, c.bank(0)[:, 0:TILES], ACT.Sigmoid, bias=bu).then_inc(u_done, 1)
            act.wait_ge(b1_turned, 1)
            nc.scalar.activation(b1T, c.bank(1)[:, 0:MIX * CHUNKS], ACT.Copy).then_inc(b1_done, 1)
            for b in range(B):
                act.wait_ge(w_turned, b + 1)
                nc.scalar.activation(wT4[0:MIX, S * b:S * b + S], c.bank(2 + b % 2)[0:MIX, :], ACT.Copy).then_inc(wT_done, 1)

        @block.vector
        def _(dve):
            ch = Chain(dve, step)
            dve.wait_ge(small_in, 16 * SMALL)
            dve.wait_ge(u_done, 1)
            wide = lambda v: v.unsqueeze(2).to_broadcast([128, TILES, MIX])
            each = lambda v: v.unsqueeze(1).to_broadcast([128, TILES, MIX])
            ch.next(nc.vector.tensor_scalar(u4, u, float(MIX), None, ALU.mult))
            ch.next(nc.vector.tensor_tensor(taken, wide(u4), each(below), ALU.is_gt))
            ch.next(nc.vector.tensor_tensor(w, wide(u), each(share), ALU.mult))
            ch.next(nc.vector.tensor_tensor(w, w, taken, ALU.mult))
            for b in range(B):
                dve.wait_ge(b2_made, b + 1)
                nc.vector.tensor_copy(c.o[:, TPB * b:TPB * b + TPB, :].rearrange("p t c -> p (t c)"),
                                      c.bank(4 + b % 2)).then_inc(o_started, 1)

    h_made, h_done, y_made, y_done, w_there = (sem(s) for s in ("h_made", "h_done", "y_made", "y_done", "w_there"))
    H0, Y0, OUT0 = CHUNKS, 2, 2 * TPB
    with nc.Block() as block:
        def batches(eng, body):
            with eng.Fori(0, B - 1) as b:
                body(b, True)
            body(B - 1, False)

        @block.tensor
        def _(pe):
            def up(b, e, batch):
                for k in range(CHUNKS):
                    pe.wait_ge(h_done, 16 * b + 4 * e + k + 1 - CHUNKS + H0)
                    nc.tensor.matmul(c.bank(k), w1[:, e, 128 * k:128 * k + 128], batch, start=True, stop=True).then_inc(h_made, 1)

            def down(b, e):
                pe.wait_ge(h_done, 16 * b + 4 * e + CHUNKS + H0)
                pe.wait_ge(y_done, TPB * (4 * b + e - 1) + OUT0)
                for t in range(TPB):
                    for k in range(CHUNKS):
                        last = nc.tensor.matmul(c.bank(4 + e % 2)[:, 128 * t:128 * t + 128], hT[:, e % 2, k, 128 * t:128 * t + 128],
                                                w2[:, e, k, :], start=(k == 0), stop=(k == CHUNKS - 1))
                last.then_inc(y_made, 1)

            pe.sem_inc(y_made, Y0)
            up(0, 0, c.nT[:, 0, 1:S + 1])

            def body(b, more):
                now = c.nT[:, bass.ds(b, 1), 1:S + 1].rearrange("p o s -> p (o s)")
                for e in range(1, MIX):
                    up(b, e, now)
                    down(b, e - 1)
                if more:
                    up(b + 1, 0, c.nT[:, bass.ds(b + 1, 1), 1:S + 1].rearrange("p o s -> p (o s)"))
                down(b, MIX - 1)

            batches(pe, body)

        @block.scalar
        def _(act):
            act.sem_inc(h_done, H0)

            def body(b, more):
                for e in range(MIX):
                    act.wait_ge(y_made, 4 * b + e - 1 + Y0)
                    for k in range(CHUNKS):
                        act.wait_ge(h_made, 16 * b + 4 * e + k + 1)
                        nc.scalar.activation(hT[:, e % 2, k, :], c.bank(k), ACT.Relu,
                                             bias=b1T[:, CHUNKS * e + k:CHUNKS * e + k + 1]).then_inc(h_done, 1)

            batches(act, body)

        @block.vector
        def _(dve):
            dve.sem_inc(y_done, OUT0)

            def body(b, more):
                dve.wait_ge(y_done, 16 * b + OUT0)
                nc.vector.tensor_copy(w_now[:, 0], w[:, bass.ds(b * TPB, TPB), :]).then_inc(w_there, 1)
                dve.wait_ge(w_there, b + 1)
                for e in range(MIX):
                    dve.wait_ge(y_made, 4 * b + e + 1 + Y0)
                    dve.wait_ge(y_done, 16 * b + 4 * e + OUT0)
                    for t in range(TPB):
                        o = c.o[:, bass.ds(b * TPB + t, 1), :].rearrange("p o c -> p (o c)")
                        nc.vector.scalar_tensor_tensor(o, c.bank(4 + e % 2)[:, 128 * t:128 * t + 128], w_now[:, 0, t, e:e + 1], o,
                                                       op0=ALU.mult, op1=ALU.add).then_inc(y_done, 1)

            batches(dve, body)


def shape_constants():
    import numpy as np
    half = HD // 2
    freq = (1.0 / np.float32(10000.0) ** (np.arange(0, HD, 2, dtype=np.float32) / np.float32(HD))).astype(np.float32)
    angle = np.outer(np.arange(S, dtype=np.float32), freq)
    row = np.arange(128)
    sign = np.where(row % HD < half, -1.0, 1.0).astype(np.float32)
    select = np.zeros((128, 36), np.float32)
    for g in range(4):
        for r in range(HD):
            select[32 * g + r, HD * g + r] = 1.0
        select[32 * g + HD, 4 * HD + g] = 1.0
    number = (np.arange(4)[None, :] - row[:, None]) % 4 + 1
    return {"rope_cos": np.cos(angle).astype(np.float32).T[row % half].copy(),
            "rope_sin": (np.sin(angle).astype(np.float32).T[row % half] * sign[:, None]).astype(np.float32),
            "select_rows": select,
            "expert_below": np.where(number == 1, -1.0, number - 1.0).astype(np.float32),
            "expert_share": (1.0 / number).astype(np.float32)}


def laid_out(inputs):
    import numpy as np
    bias = np.asarray(inputs["L3_attn_bqkv"])[0:2 * D].reshape(2, HEADS, 2, HD // 2)
    return {"bias_swapped": bias[:, :, ::-1, :].reshape(2, D).T}


def rotary_attention(c, d):
    nc = c.nc
    select = c.take(36)
    select_in = c.sem("select_in")
    with nc.Block() as block:
        @block.sync
        def _(sp):
            sp.dma_start(select, d["select_rows"]).then_inc(select_in, 16)
            sp.wait_ge(select_in, 16)
    a = Attention(c, "L3", by_tokens=False, scale=float(HD) ** -0.5)
    keep = c.used
    tables = {"bias_swapped": d["bias_swapped"], "cos": d["rope_cos"], "sin": d["rope_sin"]}
    attention_operands(c, a, d, W_QKV3, bias=d["L3_attn_bqkv"], tables=tables)
    c.used = keep
    attention(c, a, select)
    c.free_work()
    project_heads(c, d)


def add_inputs(c):
    nc = c.nc
    with nc.Block() as block:
        @block.vector
        def _(dve):
            nc.vector.tensor_tensor(c.o[:, 0:TILES // 2, :], c.o[:, 0:TILES // 2, :], c.n[:, 0:TILES // 2, :], ALU.add)

        @block.gpsimd
        def _(pool):
            nc.gpsimd.tensor_tensor(c.o[:, TILES // 2:TILES, :], c.o[:, TILES // 2:TILES, :], c.n[:, TILES // 2:TILES, :], ALU.add)


def store(c, out, src):
    nc = c.nc
    stored = c.sem("stored")
    with nc.Block() as block:
        @block.sync
        def _(sp):
            sp.dma_start(out.rearrange("b (t p) c -> p (b t) c", p=128), src).then_inc(stored, 16)
            sp.wait_ge(stored, 16)


def reshaped_attention(c, d):
    a = Attention(c, "L0", by_tokens=True, scale=1.0)
    keep = c.used
    attention_operands(c, a, d, W_Q0)
    c.used = keep
    attention(c, a)
    add_inputs(c)


def program(nc, d, out):
    with ExitStack() as ctx:
        c = Core(nc, ctx)
        counting = Counting(c)
        c.base = c.used

        def stage(run, *args, **kw):
            c.free_work()
            run(c, *args, **kw)
            c.end_stage()

        stage(setup, d, counting)
        stage(norms, "norm0", after_layer=False)
        stage(reshaped_attention, d)
        stage(norms, "norm1", after_layer=True, scale_of_batch=True)
        stage(channel_mix, d)
        stage(norms, "norm2", after_layer=True)
        stage(test_time_learner, d)
        stage(norms, "norm3", after_layer=True)
        stage(switch_layer, d, counting)
        stage(norms, "norm4", after_layer=True)
        stage(linear_attention, d)
        stage(norms, "norm5", after_layer=True)
        stage(expert_choice, d, counting)
        stage(norms, "norm6", after_layer=True)
        stage(rotary_attention, d)
        stage(norms, "norm7", after_layer=True)
        stage(elastic_mixture, d)
        stage(norms, "norm8", after_layer=True, x_norm=False)
        store(c, out, c.x)


def kernel(**inputs):
    import numpy as _np
    import concourse.bacc as _bacc
    from concourse import mybir as _mybir
    from concourse.bass_utils import run_bass_kernel_spmd as _run

    nc = _bacc.Bacc("TRN2", target_bir_lowering=False, num_devices=1)
    arrays, d = {}, {}
    for name, a in list(inputs.items()) + list(laid_out(inputs).items()) + list(shape_constants().items()):
        a = _np.ascontiguousarray(a)
        arrays[f"in_{name}"] = a
        d[name] = nc.dram_tensor(f"in_{name}", a.shape, _mybir.dt.from_np(a.dtype), kind="ExternalInput").ap()
    out = nc.dram_tensor("out_0", (B, S, D), F32, kind="ExternalOutput").ap()
    program(nc, d, out)
    return _run(nc, [arrays], core_ids=[0]).results[0]["out_0"]
```

```python
import concourse.bass as bass
from concourse import mybir
from contextlib import ExitStack

F32 = mybir.dt.float32
BF16 = mybir.dt.bfloat16
I32 = mybir.dt.int32
ACT = mybir.ActivationFunctionType
ALU = mybir.AluOpType
AX = mybir.AxisListType

B, S, D = 8, 512, 128
TOK = B * S
TILES = TOK // 128
TPB = S // 128
HEADS, HD = 16, 8
QUADS = TILES
LN_EPS = 1e-5


class Core:

    def __init__(self, nc, ctx):
        self.nc, self.ctx, self.sems = nc, ctx, []
        self.arena = ctx.enter_context(nc.sbuf_tensor("arena", [128, 48 * 1024], F32))
        self.psum = ctx.enter_context(nc.psum_tensor("psum", [128, 8 * 512], F32))
        self.used = 0
        self.x = self.take(TILES * D).rearrange("p (t c) -> p t c", c=D)
        self.n = self.take(TILES * D).rearrange("p (t c) -> p t c", c=D)
        self.o = self.take(TILES * D).rearrange("p (t c) -> p t c", c=D)
        self.nT = self.take(B * (S + 2)).rearrange("p (b s) -> p b s", s=S + 2)
        self.stats = self.take(TILES * 6).rearrange("p (t k) -> p t k", k=6)
        self.mv = self.take(TILES * 2).rearrange("p (t k) -> p t k", k=2)
        self.rstd = self.take(TILES)
        self.var_eps = self.take(TILES)
        self.minus_half = self.take(TILES)
        self.ident = self.take(128)
        self.ident_bf = self.take(64).bitcast(BF16)
        self.ones = self.take(128)
        self.wT = self.take(16 * 128).rearrange("p (w c) -> p w c", c=128)
        self.base = self.used
        self.gated = self.bank(6)

    def take(self, words):
        at = self.used
        self.used += words
        assert self.used <= 48 * 1024, self.used
        return self.arena[:, at:at + words]

    def free_work(self):
        self.used = self.base

    def sem(self, name):
        self.sems.append(self.nc.alloc_semaphore(name))
        return self.sems[-1]

    def end_stage(self):
        self.nc.clear_and_free_semaphores(self.sems)
        self.sems = []
        self.nc.all_engine_barrier()

    def bank(self, n, k=1):
        return self.psum[:, n * 512:(n + k) * 512]


class Chain:

    def __init__(self, eng, sem, base=0):
        self.eng, self.sem, self.at, self.base = eng, sem, 0, base

    def next(self, ins):
        self.mark(ins)
        self.wait()

    def mark(self, ins):
        ins.then_inc(self.sem, 1)
        self.at += 1

    def wait(self):
        self.eng.wait_ge(self.sem, self.base + self.at)


SQUARE = ["L0_attn_Wq", "L0_attn_Wk", "L0_attn_Wv", "L0_ffn_W_r", "L0_ffn_W_k", "L0_ffn_W_v",
          "L1_attn_t_k", "L1_attn_t_v", "L1_attn_t_q", "L2_attn_W_qkv", "L3_attn_Wqkv", "L3_attn_Wout"]
W_Q0, W_K0, W_V0, W_R, W_K, W_V, T_K, T_V, T_Q, W_QKV2, W_QKV3, W_OUT = 0, 1, 2, 3, 4, 5, 6, 7, 8, 9, 12, 15


def setup(c, d, counting, early):
    nc = c.nc
    w_nat = c.take(16 * 128).rearrange("p (w c) -> p w c", c=128)
    x_in, w_in = c.sem("x_in"), c.sem("w_in")
    consts, ident_built, early_in = c.sem("consts"), c.sem("ident_built"), c.sem("early_in")
    w_turned, w_copied = c.sem("w_turned"), c.sem("w_copied")
    with nc.Block() as block:
        @block.sync
        def _(sp):
            sp.dma_start(c.x, d["L0_attn_x"].rearrange("b (t p) c -> p (b t) c", p=128)).then_inc(x_in, 16)
            for inputs in early:
                inputs.load(sp, d, early_in)
            sp.wait_ge(early_in, 16 * sum(inputs.loads for inputs in early))

        @block.scalar
        def _(act):
            at = 0
            for name in SQUARE:
                rows = d[name].shape[0] // 128
                act.dma_start(w_nat[:, at:at + rows, :], d[name].rearrange("(w p) c -> p w c", p=128)).then_inc(w_in, 16)
                at += rows
            for k in range(4):
                act.wait_ge(w_turned, k + 1)
                nc.scalar.activation(c.wT[:, 4 * k:4 * k + 4, :], c.bank(k).rearrange("p (w c) -> p w c", c=128),
                                     ACT.Copy).then_inc(w_copied, 1)
            act.wait_ge(w_copied, 4)
            act.wait_ge(x_in, 16)

        @block.gpsimd
        def _(pool):
            counting.build(c, pool)
            nc.gpsimd.memset(c.minus_half, -0.5)
            nc.gpsimd.memset(c.ones, 1.0)
            nc.gpsimd.memset(c.nT[:, :, 0:1], 0.0)
            nc.gpsimd.memset(c.ident, 0.0).then_inc(consts, 1)
            pool.wait_ge(consts, 1)
            nc.gpsimd.affine_select(out=c.ident, in_=c.ident, compare_op=ALU.not_equal, fill=1.0, base=0,
                                    pattern=[[-1, 128]], channel_multiplier=1).then_inc(ident_built, 1)
            pool.wait_ge(ident_built, 1)
            nc.gpsimd.tensor_copy(c.ident_bf, c.ident).then_inc(consts, 1)

        @block.tensor
        def _(pe):
            pe.wait_ge(w_in, 16 * len(SQUARE))
            pe.wait_ge(ident_built, 1)
            for k in range(16):
                last = nc.tensor.transpose(c.bank(k // 4)[:, (k % 4) * 128:(k % 4) * 128 + 128], w_nat[:, k, :], c.ident)
                if k % 4 == 3:
                    last.then_inc(w_turned, 1)


FETCH_AHEAD = 2


def norms(c, tag, after_layer, x_norm=True, scale_of_batch=False, fetch=None, reload=None, gate=None, out=None):
    nc = c.nc
    sem = lambda name: c.sem(f"{tag}_{name}")
    o_stats, o_mv, o_fact, o_norm, x_sum = (sem(s) for s in ("o_stats", "o_mv", "o_fact", "o_norm", "x_sum"))
    x_stats, x_mv, x_fact, n_done = (sem(s) for s in ("x_stats", "x_mv", "x_fact", "n_done"))
    turned, copied, pool_step = sem("turned"), sem("copied"), sem("pool_step")
    first_residual, o_ready, x_ready = sem("first_residual"), sem("o_ready"), sem("x_ready")
    step, summed, residual, stored = sem("step"), sem("summed"), sem("residual"), sem("stored")
    fetched = [sem(f"fetched{b}") for b in range(B)] if fetch or reload is not None else None
    work = c.take(64 * 4)
    sums = c.bank(7)
    of_batch = lambda v, b: v[:, TPB * b:TPB * b + TPB]
    batch_rows = lambda v, b: v[:, TPB * b:TPB * b + TPB, :].rearrange("p t c -> p (t c)")

    class Factors:

        def __init__(self):
            self.stats = c.take(TILES * 6).rearrange("p (t k) -> p t k", k=6)
            self.mv = c.take(TILES * 2).rearrange("p (t k) -> p t k", k=2)
            self.scale, self.shift, self.var_eps = c.take(TILES), c.take(TILES), c.take(TILES)

    of_o, of_x = Factors(), Factors()

    with nc.Block() as block:
        @block.vector
        def _(dve):
            def stats(src, f, b, s_stats, s_mv, s_ready):
                for t in range(TPB * b, TPB * b + TPB):
                    nc.vector.bn_stats(f.stats[:, t, :], src[:, t, :]).then_inc(s_stats, 1)
                dve.wait_ge(s_stats, TPB * (b + 1))
                for t in range(TPB * b, TPB * b + TPB):
                    nc.vector.bn_aggr(f.mv[:, t, :], f.stats[:, t, :]).then_inc(s_mv, 1)
                if fetch:
                    dve.wait_ge(s_mv, TPB * (b + 1))
                    at = slice(TPB * b, TPB * b + TPB)
                    nc.vector.tensor_scalar(f.var_eps[:, at], f.mv[:, at, 1], LN_EPS, None, ALU.add).then_inc(s_ready, 1)
                    nc.vector.tensor_scalar(f.shift[:, at], f.mv[:, at, 0], -1.0, None, ALU.mult).then_inc(s_ready, 1)

            def batch_variance():
                ch = Chain(dve, step)
                mean, dev, tot = work[:, 0:8], work[:, 64:96], work[:, 32:64]
                tiles = lambda v: v.rearrange("p (b t) -> p b t", t=TPB)
                dve.wait_ge(summed, 1)
                ch.next(nc.vector.tensor_reduce(mean, tiles(sums[:, 0:TILES]), axis=AX.X, op=ALU.add))
                ch.next(nc.vector.tensor_scalar(mean, mean, 1.0 / S, None, ALU.mult))
                ch.next(nc.vector.tensor_tensor(tiles(dev), tiles(of_o.mv[:, :, 0]),
                                                mean.unsqueeze(2).to_broadcast([128, B, TPB]), ALU.subtract))
                ch.next(nc.vector.tensor_tensor(dev, dev, dev, ALU.mult))
                ch.next(nc.vector.tensor_tensor(tot, dev, of_o.mv[:, :, 1], ALU.add))
                dve.wait_ge(summed, 2)
                ch.next(nc.vector.tensor_reduce(mean, tiles(sums[:, 64:64 + TILES]), axis=AX.X, op=ALU.add))
                ch.next(nc.vector.tensor_scalar(work[:, 8:16], mean, 1.0 / S, LN_EPS, ALU.mult, ALU.add))

            def o_part(b):
                if fetch:
                    dve.wait_ge(fetched[b], 16 * TPB)
                if reload is not None:
                    dve.wait_ge(fetched[b], 16)
                if scale_of_batch and b == 0:
                    nc.vector.tensor_tensor(batch_rows(c.o, b), batch_rows(c.o, b), batch_rows(c.n, b), ALU.add).then_inc(first_residual, 1)
                    dve.wait_ge(first_residual, 1)
                elif scale_of_batch:
                    dve.wait_ge(residual, b)
                stats(c.o, of_o, b, o_stats, o_mv, o_ready)

            def sum_part(b):
                dve.wait_ge(o_norm, TPB * (b + 1))
                nc.vector.tensor_tensor(batch_rows(c.x, b), batch_rows(c.x, b), batch_rows(c.o, b), ALU.add).then_inc(x_sum, 1)

            def copy(b):
                dve.wait_ge(turned, b + 1)
                nc.vector.tensor_copy(c.nT[:, b, 1:S + 1], c.bank(b % 2)).then_inc(copied, 1)

            def x_part(b):
                if after_layer:
                    dve.wait_ge(x_sum, b + 1)
                stats(c.x, of_x, b, x_stats, x_mv, x_ready)

            if scale_of_batch:
                for b in range(B):
                    o_part(b)
                batch_variance()
            for i in range(B + 5):
                if after_layer and not scale_of_batch and i < B:
                    o_part(i)
                if after_layer and 2 <= i < B + 2:
                    sum_part(i - 2)
                if x_norm and 2 <= i < B + 2:
                    x_part(i - 2)
                if x_norm and i >= 5:
                    copy(i - 5)

        @block.gpsimd
        def _(pool):
            ch = Chain(pool, pool_step)
            rs, rs2 = work[:, 16:24], work[:, 24:32]

            def factors(f, at, var, signal):
                n = at.stop - at.start
                if not fetch:
                    ch.mark(nc.gpsimd.tensor_scalar(f.var_eps[:, at], var, LN_EPS, None, ALU.add))
                    ch.next(nc.gpsimd.tensor_scalar(f.shift[:, at], f.mv[:, at, 0], -1.0, None, ALU.mult))
                ch.next(nc.gpsimd.tensor_tensor(f.scale[:, at], f.var_eps[:, at], c.minus_half[:, 0:n], ALU.pow))
                nc.gpsimd.tensor_tensor(f.shift[:, at], f.shift[:, at], f.scale[:, at], ALU.mult).then_inc(signal, 1)

            def batch_scales():
                ch.next(nc.gpsimd.tensor_tensor(rs, work[:, 8:16], c.minus_half[:, 0:B], ALU.pow))
                ch.next(nc.gpsimd.tensor_tensor(rs2, rs, rs, ALU.mult))

            def factors_of_batch_norm(first, last):
                n = last - first
                at, full = slice(TPB * first, TPB * last), work[:, 128 + TPB * first:128 + TPB * last]
                wide = lambda v: v[:, first:last].unsqueeze(2).to_broadcast([128, n, TPB])
                tiles = lambda v: v.rearrange("p (b t) -> p b t", t=TPB)
                ch.next(nc.gpsimd.tensor_tensor(tiles(full), tiles(of_o.mv[:, at, 1]), wide(rs2), ALU.mult))
                ch.mark(nc.gpsimd.tensor_scalar(of_o.var_eps[:, at], full, LN_EPS, None, ALU.add))
                ch.next(nc.gpsimd.tensor_scalar(of_o.shift[:, at], of_o.mv[:, at, 0], -1.0, None, ALU.mult))
                ch.next(nc.gpsimd.tensor_tensor(full, of_o.var_eps[:, at], c.minus_half[:, 0:TPB * n], ALU.pow))
                ch.next(nc.gpsimd.tensor_tensor(tiles(of_o.scale[:, at]), tiles(full), wide(rs), ALU.mult))
                nc.gpsimd.tensor_tensor(of_o.shift[:, at], of_o.shift[:, at], of_o.scale[:, at], ALU.mult).then_inc(o_fact, n)

            def o_part(b):
                if fetch:
                    pool.wait_ge(o_ready, 2 * (b + 1))
                else:
                    pool.wait_ge(o_mv, TPB * (b + 1))
                factors(of_o, slice(TPB * b, TPB * b + TPB), of_batch(of_o.mv[:, :, 1], b), o_fact)

            def x_part(b):
                if fetch:
                    pool.wait_ge(x_ready, 2 * (b + 1))
                else:
                    pool.wait_ge(x_mv, TPB * (b + 1))
                factors(of_x, slice(TPB * b, TPB * b + TPB), of_batch(of_x.mv[:, :, 1], b), x_fact)

            if scale_of_batch:
                for b in range(1, B):
                    nc.gpsimd.tensor_tensor(batch_rows(c.o, b), batch_rows(c.o, b), batch_rows(c.n, b), ALU.add).then_inc(residual, 1)
                pool.wait_ge(step, 7)
                batch_scales()
                for first, last in ((0, 1), (1, 3), (3, B)):
                    factors_of_batch_norm(first, last)
            for i in range(B + 3):
                if after_layer and not scale_of_batch and i < B:
                    if fetch:
                        for b in (range(FETCH_AHEAD + 1) if i == 0 else [i + FETCH_AHEAD]):
                            if b < B:
                                fetch(pool, b, fetched[b])
                    o_part(i)
                if x_norm and i >= 3:
                    x_part(i - 3)

        @block.tensor
        def _(pe):
            def gate_part(b):
                pe.wait_ge(copied, b + 1)
                n = gate.shape[-1]
                for t in range(TPB * b, TPB * b + TPB):
                    k = t % TPB
                    nc.tensor.matmul(c.gated[:, n * t:n * t + n], c.nT[:, b, 1 + 128 * k:129 + 128 * k], gate, start=True, stop=True)

            if scale_of_batch:
                pe.wait_ge(o_mv, TILES)
                nc.tensor.matmul(sums[:, 0:TILES], c.ones, of_o.mv[:, :, 0], start=True, stop=True).then_inc(summed, 1)
                pe.wait_ge(step, 5)
                nc.tensor.matmul(sums[:, 64:64 + TILES], c.ones, work[:, 32:64], start=True, stop=True).then_inc(summed, 1)
            if x_norm:
                for b in range(B):
                    pe.wait_ge(n_done, TPB * (b + 1))
                    if b >= 2:
                        pe.wait_ge(copied, b - 1)
                    for k in range(TPB):
                        last = nc.tensor.transpose(c.bank(b % 2)[:, k * 128:(k + 1) * 128], c.n[:, TPB * b + k, :], c.ident)
                    last.then_inc(turned, 1)
                    if gate is not None and b >= 1:
                        gate_part(b - 1)
                if gate is not None:
                    gate_part(B - 1)

        @block.scalar
        def _(act):
            def normalise(dst, src, f, b, ready, signal):
                act.wait_ge(ready, b + 1)
                for t in range(TPB * b, TPB * b + TPB):
                    nc.scalar.activation(dst[:, t, :], src[:, t, :], ACT.Identity, bias=f.shift[:, t:t + 1],
                                         scale=f.scale[:, t:t + 1]).then_inc(signal, 1)

            for i in range(B + 3):
                if after_layer and i < B:
                    normalise(c.o, c.o, of_o, i, o_fact, o_norm)
                if x_norm and 3 <= i < B + 3:
                    normalise(c.n, c.x, of_x, i - 3, x_fact, n_done)

        @block.sync
        def _(sp):
            if reload is not None:
                for b in range(B):
                    sp.dma_start(c.o[:, TPB * b:TPB * b + TPB, :], reload[:, TPB * b:TPB * b + TPB, :]).then_inc(fetched[b], 16)
            if out is not None:
                rows = out.rearrange("b (t p) c -> p (b t) c", p=128)
                for b in range(B):
                    sp.wait_ge(x_sum, b + 1)
                    sp.dma_start(rows[:, TPB * b:TPB * b + TPB, :], c.x[:, TPB * b:TPB * b + TPB, :]).then_inc(stored, 16)
                sp.wait_ge(stored, 16 * B)


PARTS = 3
QK_ROWS = PARTS * PARTS * HD
MAX_ROW = 96
ROWS = MAX_ROW + PARTS
RING = 4


class Attention:

    def __init__(self, c, tag, by_tokens, scale):
        self.c, self.tag, self.by_tokens, self.scale = c, tag, by_tokens, scale
        nc = c.nc
        self.q_parts = nc.dram_tensor(f"{tag}_q_parts", (B, PARTS, TPB, HD, 2048), BF16).ap()
        self.k_parts = nc.dram_tensor(f"{tag}_k_parts", (B, PARTS, TPB, HD, 2048), BF16).ap()
        self.q9 = c.take(RING * 1024).bitcast(BF16).rearrange("p (s t) -> p s t", s=RING)
        self.k9 = c.take(RING * 1024).bitcast(BF16).rearrange("p (s t) -> p s t", s=RING)
        self.v32 = c.take(2 * 512).rearrange("p (s g k d) -> p s g k d", s=2, g=4, k=4)
        self.qk_in = [c.sem(f"{tag}_qk_in{s}") for s in range(RING)]
        self.v = c.take(QUADS * 128).rearrange("p (q g k d) -> p q g k d", g=4, k=4, d=HD)

    def load(self, sp, b, s):
        for p in range(PARTS):
            src = self.q_parts[bass.ds(b, 1), p, s].rearrange("o d t -> (o d) t")
            sp.dma_start(self.q9[24 * p:24 * p + 24, s, :],
                         src.unsqueeze(0).to_broadcast([PARTS, HD, 2048])).then_inc(self.qk_in[s], 16)
            sp.dma_start(self.k9[24 * p:24 * p + 24, s, :],
                         self.k_parts[bass.ds(b, 1), :, s].rearrange("o r d t -> (o r) d t")).then_inc(self.qk_in[s], 16)

    def columns(self, rows, g, first, n):
        if self.by_tokens:
            return rows[:, 4 * first + g:4 * (first + n - 1) + g + 1:4]
        return rows[:, 512 * g + first:512 * g + first + n]


def attention_operands(c, a, w, tables=None):
    nc = c.nc
    tag = a.tag + "_op"
    sem = lambda name: c.sem(f"{tag}_{name}")
    q_made, v_made = sem("qk_made"), sem("v_made")
    high, rest, mid, parts, v_laid = (sem(s) for s in ("high", "rest", "mid", "parts", "v_laid"))
    SLOTS = 4
    stored = [sem(f"stored{s}") for s in range(SLOTS)]
    exact = sem("exact")
    LOAD_AT = SLOTS - 1
    part = c.take(SLOTS * PARTS * 256).bitcast(BF16).rearrange("p (s a t) -> p s a t", s=SLOTS, a=PARTS)
    left = c.take(SLOTS * S).rearrange("p (s t) -> p s t", s=SLOTS)
    full = c.take(SLOTS * S).rearrange("p (s t) -> p s t", s=SLOTS)
    turn = c.take(SLOTS * S).rearrange("p (s t) -> p s t", s=SLOTS)
    q_pads, k_pads, k_ones = sem("q_pads"), sem("k_pads"), sem("k_ones")
    pairs = lambda v: v.rearrange("p s t -> p (s t)").bitcast(I32)
    w_qk = c.take(256).rearrange("p (w c) -> p w c", w=2)
    ordered = sem("ordered")
    rope = tables is not None
    if rope:
        qk_bias, v_bias, cos_t, sin_t = tables.qk_bias, tables.v_bias, tables.cos, tables.sin
        w_swap = c.take(256).rearrange("p (w c) -> p w c", w=2)
        swapped = sem("swapped")
        rope_cos, rope_sin = sem("rope_cos"), sem("rope_sin")

    with nc.Block() as block:
        @block.sync
        def _(sp):
            for n in range(2 * B):
                b, dst = n // 2, (a.q_parts, a.k_parts)[n % 2]
                sp.wait_ge(parts, n + 1)
                if n >= SLOTS:
                    sp.wait_ge(stored[n % SLOTS], 16 * (n // SLOTS))
                if a.by_tokens:
                    src = part[:, n % SLOTS, :, :].rearrange("p a (t l) -> p (a t) l", t=TPB)
                    out = dst[b].rearrange("a t d (j l) -> (d j) (a t) l", j=HEADS)
                else:
                    src = part[:, n % SLOTS, :, :]
                    out = dst[b].rearrange("a t d (g l) -> (t d g) a l", g=4)
                sp.dma_start(out, src).then_inc(stored[n % SLOTS], 16)
                if n == LOAD_AT:
                    for s in range(2):
                        sp.wait_ge(stored[s], 16)
                    sp.wait_ge(q_pads, 1)
                    sp.wait_ge(k_pads, 2)
                    sp.wait_ge(k_ones, 1)
                    for s in range(RING):
                        a.load(sp, 0, s)
            for n in range(SLOTS):
                sp.wait_ge(stored[n], 16 * (2 * B // SLOTS))

        @block.tensor
        def _(pe):
            pe.wait_ge(ordered, 1)
            if rope:
                pe.wait_ge(swapped, 1)
            for b in range(B):
                for n in range(2):
                    at = 2 * b + n
                    if at >= 2:
                        pe.wait_ge(rest if not rope else rope_sin, at - 1)
                        if not rope:
                            pe.wait_ge(high, at - 1)
                    tokens = c.nT[:, b, 1:S + 1]
                    if a.by_tokens:
                        tokens = tokens.rearrange("p (t g l) -> p t l g", g=4, l=32)
                    last = nc.tensor.matmul(c.bank(n), w_qk[:, n, :], tokens, start=True, stop=True)
                    if rope:
                        last = nc.tensor.matmul(c.bank(4 + n), w_swap[:, n, :], c.nT[:, b, 1:S + 1], start=True, stop=True)
                    last.then_inc(q_made, 1)
                if b >= 2:
                    pe.wait_ge(v_laid, b - 1)
                for k in range(TPB):
                    last = nc.tensor.matmul(c.bank(2 + b % 2)[:, 128 * k:128 * k + 128],
                                            c.nT[:, b, 1 + 128 * k:129 + 128 * k], c.wT[:, w + 2, :], start=True, stop=True)
                last.then_inc(v_made, 1)

        @block.scalar
        def _(act):
            def middle(n):
                act.wait_ge(rest, n + 1)
                nc.scalar.activation(part[:, n % SLOTS, 1, :], left[:, n % SLOTS, :], ACT.Copy).then_inc(mid, 1)

            for n in range(2 * B):
                if rope:
                    act.wait_ge(exact, n + 1)
                else:
                    act.wait_ge(q_made, n + 1)
                if n >= SLOTS:
                    act.wait_ge(stored[n % SLOTS], 16 * (n // SLOTS))
                src = full[:, n % SLOTS, :] if rope else c.bank(n % 2)
                nc.scalar.activation(part[:, n % SLOTS, 0, :], src, ACT.Copy).then_inc(high, 1)
                if n >= 1:
                    middle(n - 1)
                if n == 2:
                    nc.scalar.activation(a.k9[MAX_ROW:128, :, :].rearrange("p s (t c) -> p (s t) c", c=128),
                                         c.ones[MAX_ROW:128, :].unsqueeze(1).to_broadcast([128 - MAX_ROW, RING * 16, 128]),
                                         ACT.Copy).then_inc(k_ones, 1)
            middle(2 * B - 1)

        @block.vector
        def _(dve):
            for n in range(2):
                if a.by_tokens:
                    old, new = ("p (j d) -> p d j", dict(d=HD)), ("p (d j) -> p d j", dict(d=HD))
                    ways = [(old, new, c.wT[:, w + n, :], w_qk[:, n, :])]
                else:
                    old, new = ("p (g d) -> p d g", dict(d=HD)), ("p (d g) -> p d g", dict(d=HD))
                    ways = [(old, new, c.wT[:, w + n, 32 * t:32 * t + 32], w_qk[:, n, 32 * t:32 * t + 32]) for t in range(4)]
                for (o, o_k), (m, m_k), src, dst in ways:
                    last = nc.vector.tensor_copy(dst.rearrange(m, **m_k), src.rearrange(o, **o_k))
            last.then_inc(ordered, 1)
            if rope:
                dve.wait_ge(ordered, 1)
                halves = lambda m: m.rearrange("p w (t two f) -> p (w t) two f", two=2, f=16)
                nc.vector.tensor_copy(halves(w_swap)[:, :, 0, :], halves(w_qk)[:, :, 1, :])
                nc.vector.tensor_copy(halves(w_swap)[:, :, 1, :], halves(w_qk)[:, :, 0, :]).then_inc(swapped, 1)

            def rotate(n):
                dve.wait_ge(q_made, n + 1)
                if n >= SLOTS:
                    dve.wait_ge(exact, n - SLOTS + 1)
                    dve.wait_ge(high, n - SLOTS + 1)
                    dve.wait_ge(rest, n - SLOTS + 1)
                w = n % 2
                nc.vector.scalar_tensor_tensor(full[:, n % SLOTS, :], c.bank(w), qk_bias[:, w:w + 1], cos_t,
                                               op0=ALU.add, op1=ALU.mult).then_inc(rope_cos, 1)
                nc.vector.scalar_tensor_tensor(turn[:, n % SLOTS, :], c.bank(4 + w), qk_bias[:, 2 + w:3 + w], sin_t,
                                               op0=ALU.add, op1=ALU.mult).then_inc(rope_sin, 1)

            def remainder(n):
                dve.wait_ge(high, n + 1)
                if n >= SLOTS:
                    dve.wait_ge(parts, n - SLOTS + 1)
                    dve.wait_ge(mid, n - SLOTS + 1)
                src = full[:, n % SLOTS, :] if rope else c.bank(n % 2)
                nc.vector.tensor_tensor(left[:, n % SLOTS, :], src, part[:, n % SLOTS, 0, :], ALU.subtract).then_inc(rest, 1)

            if rope:
                rotate(0)
            for b in range(B):
                for n in range(2 * b, 2 * b + 2):
                    if rope and n + 1 < 2 * B:
                        rotate(n + 1)
                    remainder(n)
                if b == 0:
                    nc.vector.memset(pairs(a.q9[64:96, :, :]), 0).then_inc(q_pads, 1)
                dve.wait_ge(v_made, b + 1)
                vb = c.bank(2 + b % 2)
                if a.by_tokens:
                    for g in range(4):
                        for j in range(4):
                            src = vb[32 * g:32 * g + 32, :].rearrange("p (t k j d) -> p t k j d", t=4, k=4, j=4)[:, :, :, j, :]
                            last = nc.vector.tensor_copy(a.v[32 * j:32 * j + 32, TPB * b:TPB * b + TPB, g, :, :], src)
                else:
                    for k in range(TPB):
                        src = vb[:, 128 * k:128 * k + 128].rearrange("p (q g d) -> p q g d", q=4, g=4)
                        last = nc.vector.tensor_tensor(a.v[:, TPB * b:TPB * b + TPB, :, k, :], src,
                                                       v_bias.rearrange("p (q g d) -> p q g d", q=4, g=4), ALU.add)
                last.then_inc(v_laid, 1)

        @block.gpsimd
        def _(pool):
            def rotated(n):
                if rope and n < 2 * B:
                    pool.wait_ge(rope_cos, n + 1)
                    pool.wait_ge(rope_sin, n + 1)
                    nc.gpsimd.tensor_tensor(full[:, n % SLOTS, :], full[:, n % SLOTS, :], turn[:, n % SLOTS, :], ALU.add).then_inc(exact, 1)

            rotated(0)
            for n in range(2 * B):
                if n == 2:
                    nc.gpsimd.memset(a.v32[:, :, :, :, HD:32], 1.0).then_inc(k_pads, 1)
                    pool.wait_ge(k_pads, 1)
                    nc.gpsimd.memset(pairs(a.k9[64:96, :, :]), 0).then_inc(k_pads, 1)
                    pool.wait_ge(k_pads, 2)
                rotated(n + 1)
                pool.wait_ge(mid, n + 1)
                nc.gpsimd.tensor_tensor(part[:, n % SLOTS, 2, :], left[:, n % SLOTS, :], part[:, n % SLOTS, 1, :], ALU.subtract).then_inc(parts, 1)


def attention(c, a, select=None):
    nc = c.nc
    sem = lambda name: c.sem(f"{a.tag}_{name}")
    qk_in, q9, k9, v32 = a.qk_in, a.q9, a.k9, a.v32
    max_in = [sem(f"max_in{s}") for s in range(RING)]
    max_scores, max_taken, max_step, max_split = (sem(s) for s in ("max_scores", "max_taken", "max_step", "max_split"))
    max_turned, max_rows, max_set = sem("max_turned"), sem("max_rows"), sem("max_set")
    scores, probs, pv_step = sem("scores"), sem("probs"), sem("pv_step")
    v_ready, out_taken = sem("v_ready"), sem("out_taken")
    picked, recip_done, o_done = sem("picked"), sem("recip_done"), sem("o_done")
    CREDITS = 2

    bf = lambda words: c.take(words).bitcast(BF16)
    prob = c.take(2 * 2048).rearrange("p (s g t) -> p s g t", s=2, g=4)
    neg_max = c.take(2 * 16).rearrange("p (s m) -> p s m", s=2)
    max_left = c.take(16)
    max_part = bf(2 * 24).rearrange("p (s m) -> p s m", s=2)
    max_row = bf(2 * 64).rearrange("p (s t) -> p s t", s=2)
    row_stage = bf(2 * 1024).rearrange("p (s t) -> p s t", s=2) if a.by_tokens else None
    o_quad = c.take(2 * S).rearrange("p (s t) -> p s t", s=2)
    recip = c.take(2 * 16).rearrange("p (s t) -> p s t", s=2)

    max_bank = [c.bank(0, 2), c.bank(2, 2)]
    score_bank = [c.bank(4), c.bank(5)]
    out_bank = c.bank(6)
    turn_bank = c.bank(7)[0:48, 0:64].bitcast(BF16)
    pick_bank = c.bank(7)[:, 128:128 + 144]
    LAST = QUADS - RING
    LOADS = 16 * 2 * PARTS
    ROW_DMA = 16

    def quads(eng, body):
        with eng.Fori(0, LAST // RING) as turn:
            for s in range(RING):
                body(turn * RING + s, s, turn, True, True, True)
        for s in range(RING):
            body(LAST + s, s, LAST // RING, *(s + n < RING for n in (1, 2, 3)))

    def ahead(s, turn, n):
        return (s + n) % RING, turn + (s + n) // RING

    def max_column(g, m):
        return 4 * g + m

    with nc.Block() as block:
        @block.sync
        def _(sp):
            def rows(i, s):
                sp.wait_ge(max_rows, i + 2)
                src = max_row[0:48, s % 2, :]
                to = row_stage[MAX_ROW:ROWS, s % 2, :] if a.by_tokens else q9[MAX_ROW:ROWS, s, :]
                sp.dma_start(to, src).then_inc(max_in[s], 16)

            rows(0, 0)
            rows(1, 1)

            def body(i, s, turn, next1, next2, next3):
                if turn is not LAST // RING:
                    sp.wait_ge(scores, 16 * i + 16)
                    a.load(sp, turn + 1, s)
                if next2:
                    rows(i + 2, (s + 2) % RING)

            quads(sp, body)

        @block.gpsimd
        def _(pool):
            def values(i, s):
                nc.gpsimd.tensor_copy(v32[:, s % 2, :, :, 0:HD].rearrange("p g k d -> p (g k) d"),
                                      a.v[:, bass.ds(i, 1), :, :, :].rearrange("p o g k d -> p (o g k) d")).then_inc(v_ready, 1)

            def split(i, s):
                part = lambda p: max_part[:, s % 2, 16 * p:16 * p + 16]
                pool.wait_ge(max_taken, 8 * i + 8)
                pool.wait_ge(max_split, i + 1)
                nc.gpsimd.tensor_tensor(part(0), neg_max[:, s % 2, :], c.ones[:, 0:16], ALU.mult).then_inc(max_step, 1)
                pool.wait_ge(max_step, 3 * i + 1)
                nc.gpsimd.tensor_tensor(max_left, neg_max[:, s % 2, :], part(0), ALU.subtract).then_inc(max_step, 1)
                pool.wait_ge(max_step, 3 * i + 2)
                nc.gpsimd.tensor_tensor(part(1), max_left, c.ones[:, 0:16], ALU.mult).then_inc(max_step, 1)
                pool.wait_ge(max_step, 3 * i + 3)
                nc.gpsimd.tensor_tensor(part(2), max_left, part(1), ALU.subtract).then_inc(max_split, 1)

            def set_rows(i, s, turn):
                if a.by_tokens:
                    pool.wait_ge(max_in[s], ROW_DMA * (turn + 1))
                    pool.wait_ge(v_ready, i + 1)
                    nc.gpsimd.tensor_tensor(q9[MAX_ROW:ROWS, s, :].rearrange("p (t g) -> p g t", g=4),
                                            row_stage[MAX_ROW:ROWS, s % 2, :].rearrange("p (g t) -> p g t", g=4),
                                            k9[MAX_ROW:ROWS, s, :].rearrange("p (g t) -> p g t", g=4), ALU.mult).then_inc(max_set, 1)
                    pool.wait_ge(max_set, i + 1)

            pool.sem_inc(max_split, 1)
            split(0, 0)
            values(0, 0)
            set_rows(0, 0, 0)
            split(1, 1)

            def body(i, s, turn, next1, next2, next3):
                if next1:
                    pool.wait_ge(pv_step, CREDITS + 4 * i)
                    values(i + 1, s + 1)
                    set_rows(i + 1, *ahead(s, turn, 1))
                if next2:
                    pool.wait_ge(max_turned, i + 1)
                    split(i + 2, s)

            quads(pool, body)

        @block.tensor
        def _(pe):
            def max_tile(s, m):
                for h in range(2):
                    last = nc.tensor.matmul(max_bank[m % 2][:, 512 * h:512 * h + 512],
                                            a.columns(q9[0:QK_ROWS, s, :], m // 2, 128 * (2 * (m % 2) + h), 128),
                                            a.columns(k9[0:QK_ROWS, s, :], m // 2, 0, 512), start=True, stop=True)
                last.then_inc(max_scores, 1)

            def turn_max_wait(i):
                pe.wait_ge(max_split, i + 2)
                pe.wait_ge(max_rows, i + 1)
                if not a.by_tokens:
                    if not (isinstance(i, int) and i < 2):
                        pe.wait_ge(o_done, i - 1)

            def turn_max(i, s):
                nc.tensor.transpose(turn_bank, max_part[:, s % 2, :], c.ident_bf).then_inc(max_turned, 1)

            def score_tile(i, s, k, g):
                n = 16 * i + 4 * k + g
                pe.wait_ge(probs, n - 2 + 1 + CREDITS)
                nc.tensor.matmul(score_bank[g % 2], a.columns(k9[0:ROWS, s, :], g, 128 * k, 128),
                                 a.columns(q9[0:ROWS, s, :], g, 0, 512), start=True, stop=True).then_inc(scores, 1)

            def pv(i, s, k):
                pe.wait_ge(probs, 16 * i + 4 * k + 4 + CREDITS)
                if k == 0:
                    pe.wait_ge(v_ready, i + 1)
                    pe.wait_ge(out_taken, i + 1)
                for g in range(4):
                    last = nc.tensor.matmul(out_bank[32 * g:32 * g + 32, :], v32[:, s % 2, g, k, :],
                                            prob[:, k % 2, g, :], start=(k == 0), stop=(k == 3))
                last.then_inc(pv_step, 1)

            def pick(i, s, next2):
                pe.wait_ge(out_taken, i + 2)
                pe.wait_ge(o_done, i + 1)
                if next2:
                    pe.wait_ge(max_rows, i + 4)
                for t in range(4):
                    last = nc.tensor.matmul(pick_bank[:, 36 * t:36 * t + 36], o_quad[:, s % 2, 128 * t:128 * t + 128],
                                            select, start=True, stop=True)
                last.then_inc(picked, 1)

            def max_rows_set(i, s, turn):
                if a.by_tokens:
                    pe.wait_ge(max_set, i + 1)
                else:
                    pe.wait_ge(max_in[s], ROW_DMA * (turn + 1))

            TURN = (5, 0)
            pe.sem_inc(pv_step, CREDITS)
            def first_max_tile(m):
                if m % 8 == 0:
                    pe.wait_ge(qk_in[m // 8], LOADS)
                if m >= 2:
                    pe.wait_ge(max_taken, m - 1)
                max_tile(m // 8, m % 8)

            for m in range(16):
                if m == 12:
                    turn_max_wait(0)
                first_max_tile(m)
                if m == 12:
                    turn_max(0, 0)
            max_rows_set(0, 0, 0)
            for k in range(2):
                for g in range(4):
                    if (k, g) == (1, 0):
                        turn_max_wait(1)
                    score_tile(0, 0, k, g)
                    if (k, g) == (1, 0):
                        turn_max(1, 1)
                    if (k, g) == (1, 1):
                        pv(0, 0, 0)
                    if g >= 2:
                        first_max_tile(16 + 2 * k + g - 2)

            def body(i, s, turn, next1, next2, next3):
                s1, turn1 = ahead(s, turn, 1)
                s3, turn3 = ahead(s, turn, 3)
                for n in range(2, 6):
                    this = n < 4
                    if n == 4 and next1:
                        max_rows_set(i + 1, s1, turn1)
                    for g in range(4):
                        if next2 and (n, g) == TURN:
                            turn_max_wait(i + 2)
                        if this:
                            score_tile(i, s, n, g)
                        elif next1:
                            score_tile(i + 1, s1, n - 4, g)
                        if next2 and (n, g) == TURN:
                            turn_max(i + 2, s)
                        if g == 1 and n < 5:
                            pv(i, s, n - 1)
                        if g == 1 and n == 5 and next1:
                            pv(i + 1, s + 1, 0)
                        m = 2 * (n - 2) + g - 2
                        if g >= 2 and (next3 if m >= 4 else next2):
                            if m == 4:
                                pe.wait_ge(qk_in[s3], LOADS * (turn3 + 1))
                            pe.wait_ge(max_taken, 8 * (i + 2) + m + 3)
                            max_tile((s + 2) % RING if m < 4 else s3, (m + 4) % 8)
                if not a.by_tokens:
                    pick(i, s, next2)

            quads(pe, body)

        @block.scalar
        def _(act):
            def exps(i, s, k):
                act.wait_ge(pv_step, 4 * i + k - 2 + 1 + CREDITS)
                for g in range(4):
                    act.wait_ge(scores, 16 * i + 4 * k + g + 1)
                    nc.scalar.activation(prob[:, k % 2, g, :], score_bank[g % 2], ACT.Exp, scale=a.scale).then_inc(probs, 1)

            def rows(i, s):
                act.wait_ge(max_turned, i + 1)
                nc.scalar.activation(max_row[0:48, s % 2, :], turn_bank, ACT.Copy).then_inc(max_rows, 1)

            act.sem_inc(probs, CREDITS)
            act.sem_inc(max_rows, 1)
            rows(0, 0)
            exps(0, 0, 0)
            rows(1, 1)
            exps(0, 0, 1)

            def body(i, s, turn, next1, next2, next3):
                exps(i, s, 2)
                exps(i, s, 3)
                if next1:
                    exps(i + 1, s + 1, 0)
                if next2:
                    rows(i + 2, s)
                if next1:
                    exps(i + 1, s + 1, 1)

            quads(act, body)

        @block.vector
        def _(dve):
            def take(i, s, m):
                dve.wait_ge(max_scores, 8 * i + m + 1)
                col = max_column(m // 2, 2 * (m % 2))
                nc.vector.tensor_reduce(neg_max[:, s % 2, col:col + 2],
                                        max_bank[m % 2].rearrange("p (h t) -> p h t", h=2),
                                        axis=AX.X, op=ALU.max, negate=True).then_inc(max_taken, 1)

            def out(i, s):
                dve.wait_ge(pv_step, 4 * i + 4 + CREDITS)
                dve.wait_ge(o_done, i + 1)
                if a.by_tokens:
                    nc.vector.transpose(o_quad[:, s % 2, :], out_bank).then_inc(out_taken, 1)
                else:
                    nc.vector.tensor_copy(o_quad[:, s % 2, :], out_bank).then_inc(out_taken, 1)

            def normalise(i, s, turn):
                if a.by_tokens:
                    dve.wait_ge(out_taken, i + 2)
                    o = o_quad[:, s % 2, :].rearrange("p (j r) -> p j r", r=32)
                    nc.vector.reciprocal(recip[:, s % 2, :], o[:, :, HD]).then_inc(recip_done, 1)
                    dve.wait_ge(recip_done, i + 1)
                    nc.vector.tensor_tensor(c.o[:, bass.ds(i, 1), :].rearrange("p o (j d) -> p (o j) d", d=HD), o[:, :, 0:HD],
                                            recip[:, s % 2, :].unsqueeze(2).to_broadcast([128, HEADS, HD]),
                                            ALU.mult).then_inc(o_done, 1)
                else:
                    dve.wait_ge(picked, i + 1)
                    o = pick_bank.rearrange("p (t r) -> p t r", r=36)
                    r = recip[:, s % 2, :].rearrange("p (t g) -> p t g", t=4)
                    nc.vector.reciprocal(r, o[:, :, 32:36]).then_inc(recip_done, 1)
                    dve.wait_ge(recip_done, i + 1)
                    nc.vector.tensor_tensor(c.o[:, bass.ds(turn * TPB, TPB), 32 * s:32 * s + 32].rearrange("p t (g d) -> p t g d", g=4),
                                            o[:, :, 0:32].rearrange("p t (g d) -> p t g d", g=4),
                                            r.unsqueeze(3).to_broadcast([128, TPB, 4, HD]), ALU.mult).then_inc(o_done, 1)

            dve.sem_inc(out_taken, 1)
            dve.sem_inc(o_done, 1)
            for m in range(20):
                if m == 16:
                    dve.wait_ge(max_split, 2)
                take(m // 8, m // 8, m % 8)

            def body(i, s, turn, next1, next2, next3):
                if next2:
                    for m in range(4, 8):
                        take(i + 2, s, m)
                if next3:
                    dve.wait_ge(max_split, i + 3)
                out(i, s)
                if next3:
                    for m in range(4):
                        take(i + 3, s + 1, m)
                normalise(i, s, turn)

            quads(dve, body)


def channel_mix(c, d):
    nc = c.nc
    sem = lambda name: c.sem(f"mix_{name}")
    mu_in, mu_done = sem("mu_in"), sem("mu_done")
    part_done, mixed = sem("part_done"), sem("mixed")
    k_made, k_relu, k_sq = sem("k_made"), sem("k_relu"), sem("k_sq")
    r_made, r_sig, v_made, o_done = sem("r_made"), sem("r_sig"), sem("v_made"), sem("o_done")
    mu = c.take(4)
    SLOTS = 3
    ring = lambda: c.take(SLOTS * S).rearrange("p (s t) -> p s t", s=SLOTS)
    prev, x_r, x_k, k_pos, k_act, gate = ring(), ring(), ring(), ring(), ring(), ring()
    k_bank, r_bank, v_bank = ([c.bank(n), c.bank(n + 1)] for n in (0, 2, 4))

    with nc.Block() as block:
        @block.sync
        def _(sp):
            for n, name in enumerate(("L0_ffn_mu_r", "L0_ffn_mu_k")):
                sp.dma_start(mu[:, n:n + 1], d[name].rearrange("(c o) -> c o", o=1)).then_inc(mu_in, 16)
            sp.wait_ge(mu_in, 32)

        @block.vector
        def _(dve):
            def output(b):
                dve.wait_ge(v_made, b + 1)
                dve.wait_ge(r_sig, b + 1)
                nc.vector.tensor_tensor(c.o[:, TPB * b:TPB * b + TPB, :].rearrange("p t c -> p (t c)"), v_bank[b % 2],
                                        gate[:, b % SLOTS, :], ALU.mult).then_inc(o_done, 1)

            dve.wait_ge(mu_in, 32)
            nc.vector.tensor_scalar(mu[:, 2:4], mu[:, 0:2], -1.0, 1.0, ALU.mult, ALU.add).then_inc(mu_done, 1)
            dve.wait_ge(mu_done, 1)

            def mix(b):
                now, before = c.nT[:, b, 1:S + 1], c.nT[:, b, 0:S]
                for n, x_mix in enumerate((x_r, x_k)):
                    if b or n:
                        dve.wait_ge(mixed, 2 * b + n)
                    if b >= SLOTS:
                        dve.wait_ge(r_made, b - SLOTS + 1)
                        dve.wait_ge(k_made, b - SLOTS + 1)
                    nc.vector.tensor_scalar(prev[:, n, :], before, mu[:, 2 + n:3 + n], None, ALU.mult).then_inc(part_done, 1)
                    dve.wait_ge(part_done, 2 * b + n + 1)
                    nc.vector.scalar_tensor_tensor(x_mix[:, b % SLOTS, :], now, mu[:, n:n + 1], prev[:, n, :],
                                                   op0=ALU.mult, op1=ALU.add).then_inc(mixed, 1)

            mix(0)
            for b in range(B + 2):
                if b + 1 < B:
                    mix(b + 1)
                if b >= 2:
                    output(b - 2)

        @block.tensor
        def _(pe):
            def values(b):
                pe.wait_ge(k_sq, b + 1)
                if b >= 2:
                    pe.wait_ge(o_done, b - 1)
                for k in range(TPB):
                    last = nc.tensor.matmul(v_bank[b % 2][:, 128 * k:128 * k + 128], k_act[:, b % SLOTS, 128 * k:128 * k + 128],
                                            c.wT[:, W_V, :], start=True, stop=True)
                last.then_inc(v_made, 1)

            def project(b):
                pe.wait_ge(mixed, 2 * b + 2)
                if b >= 2:
                    pe.wait_ge(k_relu, b - 1)
                    pe.wait_ge(r_sig, b - 1)
                nc.tensor.matmul(k_bank[b % 2], c.wT[:, W_K, :], x_k[:, b % SLOTS, :], start=True, stop=True).then_inc(k_made, 1)
                for k in range(TPB):
                    last = nc.tensor.matmul(r_bank[b % 2][:, 128 * k:128 * k + 128], x_r[:, b % SLOTS, 128 * k:128 * k + 128],
                                            c.wT[:, W_R, :], start=True, stop=True)
                last.then_inc(r_made, 1)

            for b in range(B + 2):
                if b < B:
                    project(b)
                if b >= 2:
                    values(b - 2)

        @block.scalar
        def _(act):
            for b in range(B):
                act.wait_ge(k_made, b + 1)
                if b >= SLOTS:
                    act.wait_ge(k_sq, b - SLOTS + 1)
                nc.scalar.activation(k_pos[:, b % SLOTS, :], k_bank[b % 2], ACT.Relu).then_inc(k_relu, 1)
                act.wait_ge(r_made, b + 1)
                if b >= SLOTS:
                    act.wait_ge(o_done, b - SLOTS + 1)
                nc.scalar.activation(gate[:, b % SLOTS, :], r_bank[b % 2], ACT.Sigmoid).then_inc(r_sig, 1)

        @block.gpsimd
        def _(pool):
            for b in range(B):
                pool.wait_ge(k_relu, b + 1)
                if b >= SLOTS:
                    pool.wait_ge(v_made, b - SLOTS + 1)
                nc.gpsimd.tensor_tensor(k_act[:, b % SLOTS, :], k_pos[:, b % SLOTS, :], k_pos[:, b % SLOTS, :], ALU.mult).then_inc(k_sq, 1)


HID = 32
STEP = 1e-3 * 2.0 / (S * D)
TINY = 1e-6


def test_time_learner(c, d):
    nc = c.nc
    sem = lambda name: c.sem(f"ttl_{name}")
    flat = lambda v: v.rearrange("p t c -> p (t c)")
    tokens = lambda: c.take(TILES * D).rearrange("p (b s) -> p b s", b=B)
    z_nat, z_T, zy_nat, zy_T, q_T = tokens(), tokens(), tokens(), tokens(), tokens()
    t_diff = c.take(128)
    w1_nat, w1T, w2, w2T = c.take(128), c.take(HID), c.take(HID), c.take(128)
    b1, b1_col = c.take(HID), c.take(1)

    w_in, turned, w_ready = sem("w_in"), sem("turned"), sem("w_ready")
    diff_done = sem("diff_done")
    with nc.Block() as block:
        @block.sync
        def _(sp):
            sp.dma_start(w1_nat[0:HID, :], d["L1_attn_W1"]).then_inc(w_in, 16)
            sp.dma_start(w2, d["L1_attn_W2"]).then_inc(w_in, 16)
            sp.dma_start(b1, d["L1_attn_b1"].partition_broadcast(128)).then_inc(w_in, 16)
            sp.dma_start(b1_col[0:HID, :], d["L1_attn_b1"].rearrange("(c o) -> c o", o=1)).then_inc(w_in, 16)
            sp.dma_start(w2T[HID:HID + 1, :], d["L1_attn_b2"].rearrange("(o c) -> o c", o=1)).then_inc(w_in, 16)
            sp.wait_ge(w_in, 80)

        @block.tensor
        def _(pe):
            pe.wait_ge(w_in, 80)
            nc.tensor.transpose(c.bank(6)[:, 0:HID], w1_nat[0:HID, :], c.ident[0:HID, 0:HID])
            nc.tensor.transpose(c.bank(6)[0:HID, 128:256], w2, c.ident).then_inc(turned, 1)

        @block.scalar
        def _(act):
            act.wait_ge(turned, 1)
            nc.scalar.activation(w1T, c.bank(6)[:, 0:HID], ACT.Copy).then_inc(w_ready, 1)
            nc.scalar.activation(w2T[0:HID, :], c.bank(6)[0:HID, 128:256], ACT.Copy).then_inc(w_ready, 1)

        @block.vector
        def _(dve):
            nc.vector.tensor_tensor(t_diff, c.wT[:, T_K, :], c.wT[:, T_V, :], ALU.subtract).then_inc(diff_done, 1)

    small = lambda: c.take(128)
    a, a_sq, a_off, a_safe, gel, th, inv, phi, low, high, dens, slope, d_a = (small() for _ in range(13))
    h_one = c.take(TPB * (HID + 1)).rearrange("p (k h) -> p k h", k=TPB)
    hT, hqT = c.take(S), c.take(S)
    r_nat, r_T = c.take(S), c.take(S)
    tiles = lambda v: v.rearrange("p (k h) -> p k h", k=TPB)

    a_made, aT_made, r_made, rT_made, dh_made = (sem(s) for s in ("a_made", "aT_made", "r_made", "rT_made", "dh_made"))
    grad1, grad2, q_made, o_made = sem("grad1"), sem("grad2"), sem("q_made"), sem("o_made")
    a_ready, safe_ready, gel_done, hT_done, hq_done = (sem(s) for s in ("a_ready", "safe_ready", "gel_done", "hT_done", "hq_done"))
    step, h_ready, r_done, da_done, moved, o_done = (sem(s) for s in ("step", "h_ready", "r_done", "da_done", "moved", "o_done"))
    ones_set = sem("ones_set")
    d_sum = c.take(HID)
    pd, paT, pr, prT, p_new, pq, po, pg = (c.bank(n) for n in range(8))
    pa = pd[:, 352:480]
    products = [(c.wT[:, T_K, :], False, z_nat), (c.wT[:, T_K, :], True, z_T), (t_diff, False, zy_nat), (t_diff, True, zy_T),
                (c.wT[:, T_Q, :], False, c.o.rearrange("p (b t) c -> p b (t c)", b=B)), (c.wT[:, T_Q, :], True, q_T)]
    NEW = len(products)
    new_made, new_out = sem("new_made"), sem("new_out")
    g_w1, g_b1, g_b1_col, g_w2, g_w2T = pd[:, 256:288], pd[:, 288:320], pd[0:HID, 320:321], pg[:, 64:96], pg[0:HID + 1, 128:256]

    with nc.Block() as block:
        @block.tensor
        def _(pe):
            def hidden_T(out, x, b):
                return nc.tensor.matmul(out[0:HID, :], w1T, x[:, b, :], start=True, stop=True)

            def output(b):
                hidden_T(pq, q_T, b).then_inc(q_made, 1)
                pe.wait_ge(hq_done, b + 1)
                if b >= 1:
                    pe.wait_ge(o_done, b)
                for k in range(TPB):
                    last = nc.tensor.matmul(po[:, 128 * k:128 * k + 128], hqT[0:HID + 1, 128 * k:128 * k + 128],
                                            w2T[0:HID + 1, :], start=True, stop=True)
                last.then_inc(o_made, 1)

            def prepare(n):
                b, (w, turned, _) = n // NEW, products[n % NEW]
                if b < B:
                    if n >= 1:
                        pe.wait_ge(new_out, n)
                    x = c.nT[:, b, 1:S + 1]
                    if turned:
                        last = nc.tensor.matmul(p_new, w, x, start=True, stop=True)
                    else:
                        for k in range(TPB):
                            last = nc.tensor.matmul(p_new[:, 128 * k:128 * k + 128], x[:, 128 * k:128 * k + 128], w, start=True, stop=True)
                    last.then_inc(new_made, 1)

            pe.wait_ge(ones_set, 3)
            for n in range(NEW):
                prepare(n)
            for b in range(B):
                pe.wait_ge(new_out, NEW * (b + 1))
                if b >= 1:
                    pe.wait_ge(moved, 5 * b)
                hidden_T(paT, z_T, b).then_inc(aT_made, 1)
                for k in range(TPB):
                    last = nc.tensor.matmul(pa[:, 32 * k:32 * k + 32], z_T[:, b, 128 * k:128 * k + 128], w1T, start=True, stop=True)
                last.then_inc(a_made, 1)
                prepare(NEW * (b + 1))
                pe.wait_ge(hT_done, b + 1)
                nc.tensor.matmul(prT, w2T[0:HID + 1, :], hT[0:HID + 1, :], start=True, stop=True).then_inc(rT_made, 1)
                for k in range(TPB):
                    last = nc.tensor.matmul(pr[:, 128 * k:128 * k + 128], hT[0:HID + 1, 128 * k:128 * k + 128],
                                            w2T[0:HID + 1, :], start=True, stop=True)
                last.then_inc(r_made, 1)
                prepare(NEW * (b + 1) + 1)
                if b >= 1:
                    output(b - 1)
                prepare(NEW * (b + 1) + 2)
                pe.wait_ge(r_done, 2 * b + 1)
                for k in range(TPB):
                    last = nc.tensor.matmul(pd[:, 32 * k:32 * k + 32], r_T[:, 128 * k:128 * k + 128], w2, start=True, stop=True)
                last.then_inc(dh_made, 1)
                prepare(NEW * (b + 1) + 3)
                pe.wait_ge(r_done, 2 * b + 2)
                pe.wait_ge(h_ready, b + 1)
                for k in range(TPB):
                    nc.tensor.matmul(g_w2, r_nat[:, 128 * k:128 * k + 128], h_one[:, k, 0:HID], start=(k == 0), stop=(k == TPB - 1))
                for k in range(TPB):
                    last = nc.tensor.matmul(g_w2T, h_one[:, k, :], r_nat[:, 128 * k:128 * k + 128], start=(k == 0), stop=(k == TPB - 1))
                last.then_inc(grad2, 1)
                prepare(NEW * (b + 1) + 4)
                pe.wait_ge(da_done, 2 * b + 1)
                for k in range(TPB):
                    last = nc.tensor.matmul(g_w1, z_nat[:, b, 128 * k:128 * k + 128], d_a[:, 32 * k:32 * k + 32],
                                     start=(k == 0), stop=(k == TPB - 1))
                pe.wait_ge(da_done, 2 * b + 2)
                nc.tensor.matmul(g_b1, c.ones, d_sum, start=True, stop=True)
                last = nc.tensor.matmul(g_b1_col, d_sum, c.ones[:, 0:1], start=True, stop=True)
                last.then_inc(grad1, 1)
                prepare(NEW * (b + 1) + 5)
            pe.wait_ge(moved, 5 * B)
            output(B - 1)

        @block.scalar
        def _(act):
            def query(b):
                act.wait_ge(q_made, b + 1)
                if b >= 1:
                    act.wait_ge(o_made, b)
                nc.scalar.activation(hqT[0:HID, :], pq[0:HID, :], ACT.Gelu, bias=b1_col[0:HID, :]).then_inc(hq_done, 1)

            def copy(n):
                b, (_, _, out) = n // NEW, products[n % NEW]
                if b < B:
                    act.wait_ge(new_made, n + 1)
                    nc.scalar.activation(out[:, b, :], p_new, ACT.Copy).then_inc(new_out, 1)

            for n in range(NEW):
                copy(n)
            for b in range(B):
                act.wait_ge(aT_made, b + 1)
                if b >= 1:
                    act.wait_ge(r_made, b)
                nc.scalar.activation(hT[0:HID, :], paT[0:HID, :], ACT.Gelu, bias=b1_col[0:HID, :]).then_inc(hT_done, 1)
                copy(NEW * (b + 1))
                act.wait_ge(safe_ready, b + 1)
                nc.scalar.activation(gel, a_safe, ACT.Gelu).then_inc(gel_done, 1)
                nc.scalar.activation(th, a_sq, ACT.Tanh, scale=0.25).then_inc(gel_done, 1)
                copy(NEW * (b + 1) + 1)
                if b >= 1:
                    query(b - 1)
                for n in range(2, NEW):
                    copy(NEW * (b + 1) + n)
            query(B - 1)

        @block.vector
        def _(dve):
            nc.vector.memset(hT[HID:HID + 1, :], 1.0).then_inc(ones_set, 1)
            nc.vector.memset(hqT[HID:HID + 1, :], 1.0).then_inc(ones_set, 1)
            nc.vector.memset(h_one[:, :, HID:HID + 1], 1.0).then_inc(ones_set, 1)
            ch = Chain(dve, step)
            tt, ts, stt = nc.vector.tensor_tensor, nc.vector.tensor_scalar, nc.vector.scalar_tensor_tensor

            def output(b):
                dve.wait_ge(o_made, b + 1)
                o = flat(c.o[:, TPB * b:TPB * b + TPB, :])
                tt(o, o, po, ALU.add).then_inc(o_done, 1)

            for b in range(B):
                dve.wait_ge(new_out, NEW * (b + 1))
                dve.wait_ge(a_made, b + 1)
                ch.next(tt(tiles(a), tiles(pa), b1.unsqueeze(1).to_broadcast([128, TPB, HID]), ALU.add))
                ch.next(tt(a_sq, a, a, ALU.mult))
                ch.next(ts(a_off, a_sq, TINY * TINY, 4 * TINY, ALU.is_lt, ALU.mult))
                tt(a_safe, a, a_off, ALU.add).then_inc(safe_ready, 1)
                dve.wait_ge(safe_ready, b + 1)
                nc.vector.reciprocal(inv, a_safe).then_inc(step, 1)
                ch.at += 1
                dve.wait_ge(gel_done, 2 * b + 1)
                ch.wait()
                ch.next(tt(phi, gel, inv, ALU.mult))
                tt(h_one[:, :, 0:HID], tiles(a), tiles(phi), ALU.mult).then_inc(h_ready, 1)
                dve.wait_ge(rT_made, b + 1)
                tt(r_T, zy_T[:, b, :], prT, ALU.add).then_inc(r_done, 1)
                dve.wait_ge(r_made, b + 1)
                tt(r_nat, zy_nat[:, b, :], pr, ALU.add).then_inc(r_done, 1)
                dve.wait_ge(gel_done, 2 * b + 2)
                ch.next(ts(high, th, 1.0, None, ALU.add))
                ch.next(nc.vector.reciprocal(dens, high))
                ch.next(ts(low, th, -1.0, 1.0, ALU.mult, ALU.add))
                ch.next(tt(dens, dens, low, ALU.mult))
                ch.next(stt(slope, dens, 0.3989422804014327, a, op0=ALU.mult, op1=ALU.mult))
                ch.next(tt(slope, slope, phi, ALU.add))
                dve.wait_ge(dh_made, b + 1)
                tt(d_a, pd[:, 0:128], slope, ALU.mult).then_inc(da_done, 1)
                dve.wait_ge(da_done, 2 * b + 1)
                nc.vector.tensor_reduce(d_sum, d_a.rearrange("p (k h) -> p h k", k=TPB), axis=AX.X, op=ALU.add).then_inc(da_done, 1)
                if b >= 1:
                    output(b - 1)
                dve.wait_ge(grad2, b + 1)
                stt(w2, g_w2, -STEP, w2, op0=ALU.mult, op1=ALU.add).then_inc(moved, 1)
                stt(w2T[0:HID + 1, :], g_w2T, -STEP, w2T[0:HID + 1, :], op0=ALU.mult, op1=ALU.add).then_inc(moved, 1)
                dve.wait_ge(grad1, b + 1)
                stt(w1T, g_w1, -STEP, w1T, op0=ALU.mult, op1=ALU.add).then_inc(moved, 1)
                stt(b1, g_b1, -STEP, b1, op0=ALU.mult, op1=ALU.add).then_inc(moved, 1)
                stt(b1_col[0:HID, :], g_b1_col, -STEP, b1_col[0:HID, :], op0=ALU.mult, op1=ALU.add).then_inc(moved, 1)
                dve.wait_ge(moved, 5 * b + 5)
            output(B - 1)


EXPERTS, FFN = 8, 512
CHUNKS = FFN // 128
CAPACITY = TOK // EXPERTS // 2
SLOTS = EXPERTS * CAPACITY
FAR = 1 << 20


class Counting:

    def __init__(self, c):
        self.upto = c.take(64).bitcast(BF16)
        self.all = c.take(64).bitcast(BF16)
        self.goes_on = c.take(EXPERTS * TILES)
        self.row = c.take(TILES).bitcast(I32)
        self.expert = c.take(EXPERTS)
        self.built = c.sem("counting_built")

    def build(self, c, pool):
        nc = c.nc
        nc.gpsimd.memset(self.all, 1.0).then_inc(self.built, 1)
        nc.gpsimd.memset(self.goes_on, 1.0).then_inc(self.built, 1)
        pool.wait_ge(self.built, 2)
        nc.gpsimd.affine_select(out=self.upto, in_=self.all, compare_op=ALU.is_ge, fill=0.0, base=0,
                                pattern=[[1, 128]], channel_multiplier=-1).then_inc(self.built, 1)
        nc.gpsimd.memset(self.goes_on.rearrange("p (e t) -> p e t", e=EXPERTS)[:, :, 0:1], 0.0).then_inc(self.built, 1)
        nc.gpsimd.iota(self.expert, pattern=[[1, EXPERTS]], base=0, channel_multiplier=0,
                       allow_small_or_imprecise_dtypes=True).then_inc(self.built, 1)


def by_expert(v):
    return v.rearrange("p (e t) -> p e t", e=EXPERTS)


def over_tiles(v):
    return v.unsqueeze(2).to_broadcast([128, EXPERTS, TILES])


def switch_layer(c, d, n_count):
    nc = c.nc
    sem = lambda name: c.sem(f"sw_{name}")
    rows_in = nc.dram_tensor("sw_rows_in", (SLOTS, D), F32).ap()
    rows_out = nc.dram_tensor("sw_rows_out", (SLOTS, D), F32).ap()
    b_sw = c.take(EXPERTS)
    w1 = c.take(EXPERTS * FFN).rearrange("p (e f) -> p e f", e=EXPERTS)
    w2 = c.take(EXPERTS * FFN).rearrange("p (e k c) -> p e k c", e=EXPERTS, k=CHUNKS)
    b1_nat, b1T, b2 = c.take(128), c.take(EXPERTS * CHUNKS), c.take(EXPERTS * D)
    row = n_count.row
    keep = c.used
    wide = lambda: c.take(EXPERTS * TILES)
    logit, tie, pick, total, upto, slot = (wide() for _ in range(6))
    chosen = c.take(EXPERTS * TILES // 2).bitcast(BF16)
    best, row_f = c.take(TILES), c.take(TILES)
    zeros = c.take(SLOTS)
    small_in, w_in, made, counted = sem("small_in"), sem("w_in"), sem("made"), sem("counted")
    chosen_done, step, zero_set, zero_out, row_done = sem("chosen_done"), sem("step"), sem("zero_set"), sem("zero_out"), sem("row_done")
    sent, b1_turned = sem("sent"), sem("b1_turned")
    tiles_last = lambda v: v.rearrange("p (e t) -> p t e", e=EXPERTS)
    per_tile = lambda v: v.unsqueeze(2).to_broadcast([128, TILES, EXPERTS])
    per_expert = lambda v: v.unsqueeze(1).to_broadcast([128, TILES, EXPERTS])

    with nc.Block() as block:
        @block.sync
        def _(sp):
            sp.dma_start(b_sw, d["L1_ffn_b_switch"].partition_broadcast(128)).then_inc(small_in, 16)
            sp.dma_start(b1_nat[0:EXPERTS * CHUNKS, :], d["L1_ffn_b1"].rearrange("e (k p) -> (e k) p", p=128)).then_inc(small_in, 16)
            sp.dma_start(b2[0:1, :], d["L1_ffn_b2"].rearrange("(o e) c -> o (e c)", o=1)).then_inc(small_in, 16)
            sp.wait_ge(zero_set, 1)
            sp.dma_start(rows_in.rearrange("(p s) c -> p (s c)", p=128), zeros).then_inc(zero_out, 16)
            sp.dma_start(w1, d["L1_ffn_w1"].rearrange("e p f -> p e f")).then_inc(w_in, 16)
            sp.dma_start(w2, d["L1_ffn_w2"].rearrange("e (k p) c -> p e k c", p=128)).then_inc(w_in, 16)
            sp.wait_ge(small_in, 48)
            sp.wait_ge(w_in, 32)

        @block.tensor
        def _(pe):
            pe.wait_ge(small_in, 48)
            nc.tensor.transpose(c.bank(3)[:, 0:EXPERTS * CHUNKS], b1_nat[0:EXPERTS * CHUNKS, :],
                                c.ident[0:EXPERTS * CHUNKS, 0:EXPERTS * CHUNKS]).then_inc(made, 1)
            pe.wait_ge(chosen_done, 1)
            pe.wait_ge(n_count.built, 5)
            nc.tensor.matmul(c.bank(1)[:, 0:256], n_count.upto, chosen, start=True, stop=True)
            nc.tensor.matmul(c.bank(2)[:, 0:256], n_count.all, chosen, start=True, stop=True).then_inc(counted, 1)

        @block.scalar
        def _(act):
            act.wait_ge(made, 1)
            nc.scalar.activation(b1T, c.bank(3)[:, 0:EXPERTS * CHUNKS], ACT.Copy).then_inc(b1_turned, 1)

        @block.vector
        def _(dve):
            ch = Chain(dve, step)
            tt, ts = nc.vector.tensor_tensor, nc.vector.tensor_scalar
            nc.vector.memset(zeros, 0.0).then_inc(zero_set, 1)
            dve.wait_ge(n_count.built, 5)
            dve.wait_ge(small_in, 48)
            ch.next(tt(tiles_last(logit), c.gated[:, 0:256].rearrange("p (t e) -> p t e", e=EXPERTS), per_expert(b_sw), ALU.add))
            ch.next(nc.vector.tensor_reduce(best, tiles_last(logit), axis=AX.X, op=ALU.max))
            ch.next(tt(tiles_last(tie), tiles_last(logit), per_tile(best), ALU.is_equal))
            ch.next(ts(slot[:, 0:EXPERTS], n_count.expert, -1.0, float(EXPERTS), ALU.mult, ALU.add))
            ch.next(tt(tiles_last(tie), tiles_last(tie), per_expert(slot[:, 0:EXPERTS]), ALU.mult))
            ch.next(nc.vector.tensor_reduce(best, tiles_last(tie), axis=AX.X, op=ALU.max))
            ch.next(tt(tiles_last(pick), tiles_last(tie), per_tile(best), ALU.is_equal))
            nc.vector.tensor_copy(chosen, pick).then_inc(chosen_done, 1)
            dve.wait_ge(counted, 1)
            ch.next(nc.vector.tensor_copy(total, c.bank(2)[:, 0:256]))
            ch.next(nc.vector.tensor_tensor_scan(upto, n_count.goes_on, total, 0.0, op0=ALU.mult, op1=ALU.add))
            ch.next(tt(upto, upto, total, ALU.subtract))
            ch.next(tt(upto, upto, c.bank(1)[:, 0:256], ALU.add))
            ch.next(ts(tie, upto, float(CAPACITY), float(FAR), ALU.is_gt, ALU.mult))
            ch.next(ts(slot[:, 0:EXPERTS], n_count.expert, float(CAPACITY), -1.0, ALU.mult, ALU.add))
            ch.next(tt(by_expert(upto), by_expert(upto), over_tiles(slot[:, 0:EXPERTS]), ALU.add))
            ch.next(tt(upto, upto, tie, ALU.add))
            ch.next(tt(upto, upto, pick, ALU.mult))
            ch.next(nc.vector.tensor_reduce(row_f, tiles_last(upto), axis=AX.X, op=ALU.add))
            nc.vector.tensor_copy(row, row_f).then_inc(row_done, 1)

        @block.gpsimd
        def _(pool):
            pool.wait_ge(zero_out, 16)
            pool.wait_ge(row_done, 1)
            for t in range(TILES):
                pool.indirect_dma_start(rows_in, bass.IndirectOffsetOnAxis(ap=row[:, t:t + 1], axis=0), c.n[:, t, :], None,
                                        bounds_check=SLOTS - 1, oob_is_err=False).then_inc(sent, 16)
            pool.wait_ge(sent, 16 * TILES)

    c.used = keep
    PER = CAPACITY // 128
    x_nat = c.take(SLOTS).rearrange("p (s c) -> p s c", c=D)
    y_nat = c.take(SLOTS).rearrange("p (s c) -> p s c", c=D)
    xT = c.take(2 * CAPACITY).rearrange("p (r s) -> p r s", r=2)
    hT = c.take(2 * CHUNKS * CAPACITY).rearrange("p (r k s) -> p r k s", r=2, k=CHUNKS)
    x_in, x_turned, xT_done, h_made, h_done = (sem(s) for s in ("x_in", "x_turned", "xT_done", "h_made", "h_done"))
    y_made, y_done, y_out, passed = (sem(s) for s in ("y_made", "y_done", "y_out", "passed"))
    with nc.Block() as block:
        @block.sync
        def _(sp):
            sp.dma_start(x_nat, rows_in.rearrange("(s p) c -> p s c", p=128)).then_inc(x_in, 16)
            for e in range(EXPERTS):
                sp.wait_ge(y_done, e + 1)
                sp.dma_start(rows_out[CAPACITY * e:CAPACITY * (e + 1), :].rearrange("(s p) c -> p s c", p=128),
                             y_nat[:, PER * e:PER * (e + 1), :]).then_inc(y_out, 16)
            sp.wait_ge(y_out, 16 * EXPERTS)

        @block.tensor
        def _(pe):
            def turn(e):
                if e >= 2:
                    pe.wait_ge(xT_done, e - 1)
                for s in range(PER):
                    last = nc.tensor.transpose(c.bank(e % 2)[:, 128 * s:128 * s + 128], x_nat[:, PER * e + s, :], c.ident)
                last.then_inc(x_turned, 1)

            def up(e):
                pe.wait_ge(xT_done, e + 1)
                for k in range(CHUNKS):
                    if k % 2 == 0 and e >= 1:
                        pe.wait_ge(h_done, CHUNKS * (e - 1) + k + 2)
                    last = nc.tensor.matmul(c.bank(2 + k // 2)[:, CAPACITY * (k % 2):CAPACITY * (k % 2) + CAPACITY],
                                            w1[:, e, 128 * k:128 * k + 128], xT[:, e % 2, :], start=True, stop=True)
                    if k % 2:
                        last.then_inc(h_made, 1)

            def down(e):
                pe.wait_ge(h_done, CHUNKS * e + CHUNKS)
                if e >= 2:
                    pe.wait_ge(y_done, e - 1)
                for s in range(PER):
                    out = c.bank(4 + e % 2)[:, 128 * s:128 * s + 128]
                    for k in range(CHUNKS):
                        nc.tensor.matmul(out, hT[:, e % 2, k, 128 * s:128 * s + 128], w2[:, e, k, :], start=(k == 0), stop=False)
                    last = nc.tensor.matmul(out, c.ones[0:1, :], b2[0:1, D * e:D * e + D], start=False, stop=True)
                last.then_inc(y_made, 1)

            pe.wait_ge(x_in, 16)
            turn(0)
            for e in range(EXPERTS):
                if e + 1 < EXPERTS:
                    turn(e + 1)
                up(e)
                if e >= 1:
                    down(e - 1)
            down(EXPERTS - 1)

        @block.scalar
        def _(act):
            for e in range(EXPERTS):
                act.wait_ge(x_turned, e + 1)
                if e >= 2:
                    act.wait_ge(h_made, 2 * (e - 1))
                nc.scalar.activation(xT[:, e % 2, :], c.bank(e % 2)[:, 0:CAPACITY], ACT.Copy).then_inc(xT_done, 1)
                for k in range(CHUNKS):
                    act.wait_ge(h_made, 2 * e + k // 2 + 1)
                    if e >= 2:
                        act.wait_ge(y_made, e - 1)
                    nc.scalar.activation(hT[:, e % 2, k, :], c.bank(2 + k // 2)[:, CAPACITY * (k % 2):CAPACITY * (k % 2) + CAPACITY],
                                         ACT.Relu, bias=b1T[:, CHUNKS * e + k:CHUNKS * e + k + 1]).then_inc(h_done, 1)

        @block.vector
        def _(dve):
            nc.vector.tensor_copy(c.o, c.n).then_inc(passed, 1)
            for e in range(EXPERTS):
                dve.wait_ge(y_made, e + 1)
                nc.vector.tensor_copy(y_nat[:, PER * e:PER * (e + 1), :].rearrange("p s c -> p (s c)"),
                                      c.bank(4 + e % 2)[:, 0:PER * 128]).then_inc(y_done, 1)

        @block.gpsimd
        def _(pool):
            pool.wait_ge(passed, 1)
            pool.wait_ge(y_out, 16 * EXPERTS)

    def fetch(pool, b, signal):
        for t in range(TPB * b, TPB * b + TPB):
            pool.indirect_dma_start(c.o[:, t, :], None, rows_out, bass.IndirectOffsetOnAxis(ap=row[:, t:t + 1], axis=0),
                                    bounds_check=SLOTS - 1, oob_is_err=False).then_inc(signal, 16)

    return fetch


def linear_attention(c, d):
    nc = c.nc
    sem = lambda name: c.sem(f"lin_{name}")
    QK = 2 * D
    SLOTS = 3
    ring = lambda n: c.take(SLOTS * TPB * n).rearrange("p (s t c) -> p s t c", s=SLOTS, t=TPB)
    qk, sq, v_one = ring(QK), ring(QK), ring(D + 2)
    norm = c.take(SLOTS * TPB * 32).rearrange("p (s h) -> p s h", s=SLOTS)
    qT = c.take(2 * S).rearrange("p (s t) -> p s t", s=2)
    kv = c.take(2 * (D + HEADS)).rearrange("p (s c) -> p s c", s=2)
    k_sum, head_mask, block_mask = c.take(2), c.take(HEADS), c.take(D)
    recip = c.take(2 * TPB * HEADS).rearrange("p (s h) -> p s h", s=2)
    made, qk_out, v_out, sq_done, ss_done, bounded, logs, inv_done, unit = (sem(s) for s in (
        "made", "qk_out", "v_out", "sq_done", "ss_done", "bounded", "logs", "inv_done", "unit"))
    expd, soft, kv_made, kv_done, qT_made, qT_done, o_made, o_done = (sem(s) for s in (
        "expd", "soft", "kv_made", "kv_done", "qT_made", "qT_done", "o_made", "o_done"))
    masks, step = sem("masks"), sem("step")
    heads = lambda v: v.rearrange("p t (h d) -> p (t h) d", d=HD)
    OW = D + HEADS

    with nc.Block() as block:
        @block.gpsimd
        def _(pool):
            nc.gpsimd.memset(head_mask, 1.0).then_inc(masks, 1)
            pool.wait_ge(masks, 1)
            nc.gpsimd.affine_select(out=head_mask, in_=head_mask, compare_op=ALU.is_ge, fill=0.0, base=0,
                                    pattern=[[-HD, HEADS]], channel_multiplier=1).then_inc(masks, 1)
            pool.wait_ge(masks, 2)
            nc.gpsimd.affine_select(out=head_mask, in_=head_mask, compare_op=ALU.is_ge, fill=0.0, base=HD - 1,
                                    pattern=[[HD, HEADS]], channel_multiplier=-1).then_inc(masks, 1)
            pool.wait_ge(masks, 3)
            nc.gpsimd.tensor_copy(block_mask.rearrange("p (h d) -> p h d", d=HD),
                                  head_mask.unsqueeze(2).to_broadcast([128, HEADS, HD])).then_inc(masks, 1)

        @block.tensor
        def _(pe):
            def project(b):
                for k in range(TPB):
                    n = TPB * b + k
                    if n >= 3:
                        pe.wait_ge(qk_out, n - 2)
                        pe.wait_ge(v_out, n - 2)
                    nc.tensor.matmul(c.bank(n % 3)[:, 0:3 * D], c.nT[:, b, 1 + 128 * k:129 + 128 * k],
                                     c.wT[:, W_QKV2:W_QKV2 + 3, :].rearrange("p w c -> p (w c)"), start=True, stop=True).then_inc(made, 1)

            def sums(b):
                pe.wait_ge(soft, b + 1)
                if b >= 1:
                    pe.wait_ge(kv_done, b)
                    pe.wait_ge(qT_done, b)
                for k in range(TPB):
                    last = nc.tensor.matmul(c.bank(3)[:, 0:D + 1], qk[:, b % SLOTS, k, D:QK], v_one[:, b % SLOTS, k, 0:D + 1],
                                            start=(k == 0), stop=(k == TPB - 1))
                last.then_inc(kv_made, 1)
                for k in range(TPB):
                    last = nc.tensor.transpose(c.bank(4)[:, 128 * k:128 * k + 128], qk[:, b % SLOTS, k, 0:D], c.ident)
                last.then_inc(qT_made, 1)

            def output(b):
                pe.wait_ge(kv_done, b + 1)
                pe.wait_ge(qT_done, b + 1)
                if b >= 1:
                    pe.wait_ge(o_done, b)
                for k in range(TPB):
                    last = nc.tensor.matmul(c.bank(5 + k // 2)[:, OW * (k % 2):OW * (k % 2) + OW], qT[:, b % 2, 128 * k:128 * k + 128],
                                            kv[:, b % 2, :], start=True, stop=True)
                last.then_inc(o_made, 1)

            for b in range(B + 3):
                if b < B:
                    project(b)
                if 2 <= b < B + 2:
                    sums(b - 2)
                if b >= 3:
                    output(b - 3)

        @block.scalar
        def _(act):
            def soften(b):
                act.wait_ge(unit, b + 1)
                nc.scalar.activation(sq[:, b % SLOTS], qk[:, b % SLOTS], ACT.Exp).then_inc(expd, 1)
                act.wait_ge(expd, b + 1)
                nc.scalar.activation(qk[:, b % SLOTS], sq[:, b % SLOTS], ACT.Ln, bias=1.0).then_inc(soft, 1)

            def turn(b):
                act.wait_ge(qT_made, b + 1)
                if b >= 2:
                    act.wait_ge(o_made, b - 1)
                nc.scalar.activation(qT[:, b % 2, :], c.bank(4), ACT.Copy).then_inc(qT_done, 1)

            def copy(b):
                for k in range(TPB):
                    n = TPB * b + k
                    act.wait_ge(made, n + 1)
                    if b >= SLOTS and k == 0:
                        act.wait_ge(qT_made, b - SLOTS + 1)
                    nc.scalar.activation(qk[:, b % SLOTS, k, :], c.bank(n % 3)[:, 0:QK], ACT.Copy).then_inc(qk_out, 1)
                act.wait_ge(qk_out, TPB * (b + 1))
                nc.scalar.activation(sq[:, b % SLOTS], qk[:, b % SLOTS], ACT.Square).then_inc(sq_done, 1)

            def invert(b):
                act.wait_ge(bounded, b + 1)
                nc.scalar.activation(norm[:, b % SLOTS, :], norm[:, b % SLOTS, :], ACT.Ln).then_inc(logs, 1)
                act.wait_ge(logs, b + 1)
                nc.scalar.activation(norm[:, b % SLOTS, :], norm[:, b % SLOTS, :], ACT.Exp, scale=-0.5).then_inc(inv_done, 1)

            for b in range(B + 2):
                if b < B:
                    copy(b)
                if b >= 2:
                    soften(b - 2)
                if 1 <= b < B + 1:
                    invert(b - 1)
                if b >= 2:
                    turn(b - 2)

        @block.vector
        def _(dve):
            ch = Chain(dve, step)
            nc.vector.memset(v_one[:, :, :, D:D + 1], 1.0).then_inc(step, 1)
            ch.at += 1
            dve.wait_ge(masks, 4)

            def mask(b):
                dve.wait_ge(kv_made, b + 1)
                if b >= 2:
                    dve.wait_ge(o_made, b - 1)
                ch.next(nc.vector.tensor_scalar(k_sum[:, 0:1], c.bank(3)[:, D:D + 1], 1e-6, None, ALU.add))
                ch.next(nc.vector.scalar_tensor_tensor(kv[:, b % 2, 0:D], c.bank(3)[:, 0:D], float(HD) ** -0.5, block_mask,
                                                       op0=ALU.mult, op1=ALU.mult))
                nc.vector.tensor_scalar(kv[:, b % 2, D:OW], head_mask, k_sum[:, 0:1], None, ALU.mult).then_inc(kv_done, 1)

            def output(b):
                dve.wait_ge(o_made, b + 1)
                for k in range(2):
                    o = c.bank(5 + k)[:, 0:2 * OW].rearrange("p (t c) -> p t c", t=2)
                    r = recip[:, k, 0:2 * HEADS].rearrange("p (t h) -> p t h", t=2)
                    ch.next(nc.vector.reciprocal(r, o[:, :, D:OW]))
                    t = TPB * b + 2 * k
                    last = nc.vector.tensor_tensor(c.o[:, t:t + 2, :].rearrange("p t (h d) -> p t h d", d=HD),
                                                   o[:, :, 0:D].rearrange("p t (h d) -> p t h d", d=HD),
                                                   r.unsqueeze(3).to_broadcast([128, 2, HEADS, HD]), ALU.mult)
                    if k == 0:
                        ch.mark(last)
                ch.wait()
                last.then_inc(o_done, 1)

            def sums(b):
                for k in range(TPB):
                    n = TPB * b + k
                    dve.wait_ge(made, n + 1)
                    dve.wait_ge(qk_out, n + 1)
                    if b >= SLOTS and k == 0:
                        dve.wait_ge(kv_made, b - SLOTS + 1)
                    nc.vector.tensor_copy(v_one[:, b % SLOTS, k, 0:D], c.bank(n % 3)[:, QK:3 * D]).then_inc(v_out, 1)
                dve.wait_ge(sq_done, b + 1)
                if b >= SLOTS:
                    dve.wait_ge(unit, b - SLOTS + 1)
                nc.vector.tensor_reduce(norm[:, b % SLOTS, :], heads(sq[:, b % SLOTS]), axis=AX.X, op=ALU.add).then_inc(ss_done, 1)
                dve.wait_ge(ss_done, b + 1)
                nc.vector.tensor_scalar(norm[:, b % SLOTS, :], norm[:, b % SLOTS, :], 1e-24, None, ALU.max).then_inc(bounded, 1)

            def scale(b):
                dve.wait_ge(inv_done, b + 1)
                nc.vector.tensor_tensor(heads(qk[:, b % SLOTS]), heads(qk[:, b % SLOTS]),
                                        norm[:, b % SLOTS, :].unsqueeze(2).to_broadcast([128, TPB * 32, HD]), ALU.mult).then_inc(unit, 1)

            for b in range(B + 3):
                if b < B:
                    sums(b)
                if 2 <= b < B + 2:
                    mask(b - 2)
                if 1 <= b < B + 1:
                    scale(b - 1)
                if b >= 3:
                    output(b - 3)


BITS = 30
STEP_BITS = 2
ROUNDS, TRIALS = BITS // STEP_BITS, (1 << STEP_BITS) - 1
SHARE = 128 // EXPERTS
KEPT = TOK // EXPERTS
PICKS = TOK // 128
PER_EXPERT = KEPT // 128


def expert_choice(c, d, n_count):
    nc = c.nc
    sem = lambda name: c.sem(f"ec_{name}")
    idx = c.take(PICKS).bitcast(I32)
    weight = c.take(PICKS)
    lnw, lnb = c.take(1), c.take(1)
    b1_nat, b1T, b2 = c.take(128), c.take(EXPERTS * CHUNKS), c.take(EXPERTS * D)
    fc1 = c.take(EXPERTS * FFN).rearrange("p (e k c) -> p e k c", e=EXPERTS, k=CHUNKS)
    fc2 = c.take(EXPERTS * FFN).rearrange("p (e f) -> p e f", e=EXPERTS)
    normed = nc.dram_tensor("ec_normed", (TOK, D), F32).ap()
    result = nc.dram_tensor("ec_result", (TOK, D), F32).ap()
    keep = c.used
    wide = lambda: c.take(EXPERTS * TILES)
    half_wide = lambda: c.take(EXPERTS * TILES // 2).bitcast(BF16)
    score, above, equal, total, place, chosen, work = (wide() for _ in range(7))
    mask_a, mask_b = half_wide(), half_wide()
    best = c.take(TILES)
    limit = c.take(EXPERTS)
    flat = c.take(EXPERTS * TILES)
    reach = c.take(TRIALS * EXPERTS * TILES // 2).bitcast(BF16).rearrange("p (k t) -> p k t", k=TRIALS)
    trial = c.take(TRIALS + 1)
    steps = c.take(ROUNDS * TRIALS).bitcast(I32).rearrange("p (r k) -> p r k", r=ROUNDS)
    cand = c.take(TRIALS)
    count_bf = c.take(2).bitcast(BF16)
    member, member_bf, first = c.take(EXPERTS), c.take(64).bitcast(BF16), c.take(EXPERTS)
    chosen_limit = c.take(EXPERTS)
    count, need = c.take(EXPERTS), c.take(EXPERTS)
    lane, slot_tile = wide(), wide()
    whole, cand_wide = wide().bitcast(I32), wide().bitcast(I32)
    iota128, iota4, p_id, t_id = c.take(128), c.take(4), c.take(1), c.take(TILES)
    one_hot = c.take(2 * TILES * 64).bitcast(BF16).rearrange("p (s t a) -> p s t a", s=2, t=TILES)
    VALS = 5
    vals = c.take(2 * TILES * 4 * VALS // 2).bitcast(BF16).rearrange("p (s t v b) -> p s t v b", s=2, t=TILES, v=VALS)
    here = c.take(EXPERTS * TILES * 4).rearrange("p (e b) -> p e b", b=4)
    first_tile = wide()
    w_part = c.take(3 * EXPERTS * TILES // 2).bitcast(BF16).rearrange("p (v e) -> p v e", v=3)
    w_left = wide()
    found = c.take(EXPERTS * 4 * VALS).rearrange("p (e v b) -> p e v b", e=EXPERTS, v=VALS)
    small_in, turned, step, expd = (sem(s) for s in ("small_in", "turned", "step", "expd"))
    counted, counts, spread, grouped, limits = (sem(s) for s in ("counted", "counts", "spread", "grouped", "limits"))
    probs_ready, w_in = sem("probs_ready"), sem("w_in")
    slots, val_step, vals_ready = sem("slots"), sem("val_step"), sem("vals_ready")
    ids, tallied, mask_done, hot, hot_used, xf_out, idx_done = (sem(s) for s in (
        "ids", "tallied", "mask_done", "hot", "hot_used", "xf_out", "idx_done"))
    y_stats, y_mv, y_rstd, y_step, yn_done = (sem(s) for s in ("y_stats", "y_mv", "y_rstd", "y_step", "yn_done"))
    tiles_last = lambda v: v.rearrange("p (e t) -> p t e", e=EXPERTS)
    per_tile = lambda v: v.unsqueeze(2).to_broadcast([128, TILES, EXPERTS])

    GROUPED = 6 + ROUNDS * TRIALS
    with nc.Block() as block:
        @block.sync
        def _(sp):
            sp.dma_start(b1_nat[0:EXPERTS * CHUNKS, :], d["L2_ffn_b1s"].rearrange("e (k p) -> (e k) p", p=128)).then_inc(small_in, 16)
            sp.dma_start(b2[0:1, :], d["L2_ffn_b2s"].rearrange("(o e) c -> o (e c)", o=1)).then_inc(small_in, 16)
            sp.dma_start(lnw, d["L2_ffn_ln_w"].rearrange("(c o) -> c o", o=1)).then_inc(small_in, 16)
            sp.dma_start(lnb, d["L2_ffn_ln_b"].rearrange("(c o) -> c o", o=1)).then_inc(small_in, 16)
            sp.wait_ge(probs_ready, 1)
            for e in range(EXPERTS):
                sp.dma_start(flat[SHARE * e:SHARE * e + SHARE, :], score[:, TILES * e:TILES * e + TILES]).then_inc(spread, 16)
            sp.dma_start(result.rearrange("(t p) c -> p t c", p=128), c.n).then_inc(xf_out, 16)
            sp.dma_start(fc1, d["L2_ffn_fc1s"].rearrange("e (k p) c -> p e k c", p=128)).then_inc(w_in, 16)
            sp.dma_start(fc2, d["L2_ffn_fc2s"].rearrange("e c f -> c e f")).then_inc(w_in, 16)
            sp.wait_ge(yn_done, TILES)
            sp.dma_start(normed.rearrange("(t p) c -> p t c", p=128), c.o).then_inc(xf_out, 16)
            sp.wait_ge(small_in, 64)
            sp.wait_ge(xf_out, 32)
            sp.wait_ge(w_in, 32)

        @block.gpsimd
        def _(pool):
            io = dict(allow_small_or_imprecise_dtypes=True)
            nc.gpsimd.iota(iota128, pattern=[[1, 128]], base=0, channel_multiplier=0, **io).then_inc(ids, 1)
            nc.gpsimd.iota(iota4, pattern=[[1, 4]], base=0, channel_multiplier=0, **io).then_inc(ids, 1)
            nc.gpsimd.iota(p_id, pattern=[[0, 1]], base=0, channel_multiplier=1, **io).then_inc(ids, 1)
            nc.gpsimd.iota(t_id, pattern=[[1, TILES]], base=0, channel_multiplier=0, **io).then_inc(ids, 1)
            nc.gpsimd.iota(first_tile, pattern=[[PER_EXPERT, EXPERTS], [0, TILES]], base=0, channel_multiplier=0, **io).then_inc(ids, 1)
            nc.gpsimd.memset(member, 1.0).then_inc(grouped, 1)
            nc.gpsimd.memset(first, 0.0).then_inc(grouped, 1)
            pool.wait_ge(grouped, 2)
            nc.gpsimd.affine_select(out=member, in_=member, compare_op=ALU.is_ge, fill=0.0, base=0,
                                    pattern=[[-SHARE, EXPERTS]], channel_multiplier=1).then_inc(grouped, 1)
            nc.gpsimd.affine_select(out=first, in_=first, compare_op=ALU.not_equal, fill=1.0, base=0,
                                    pattern=[[-SHARE, EXPERTS]], channel_multiplier=1).then_inc(grouped, 1)
            pool.wait_ge(grouped, 4)
            nc.gpsimd.affine_select(out=member, in_=member, compare_op=ALU.is_ge, fill=0.0, base=SHARE - 1,
                                    pattern=[[SHARE, EXPERTS]], channel_multiplier=-1).then_inc(grouped, 1)
            pool.wait_ge(grouped, 5)
            nc.gpsimd.tensor_copy(member_bf.rearrange("p (e j) -> p e j", e=EXPERTS),
                                  member.unsqueeze(2).to_broadcast([128, EXPERTS, SHARE])).then_inc(grouped, 1)
            for r in range(ROUNDS):
                for k in range(TRIALS):
                    nc.gpsimd.memset(steps[:, r, k:k + 1], (k + 1) << (BITS - STEP_BITS * (r + 1))).then_inc(grouped, 1)
            pool.wait_ge(y_mv, TILES)
            nc.gpsimd.tensor_scalar(c.var_eps, c.mv[:, :, 1], LN_EPS, None, ALU.add).then_inc(y_step, 1)
            pool.wait_ge(y_step, 1)
            nc.gpsimd.tensor_tensor(c.rstd, c.var_eps, c.minus_half, ALU.pow).then_inc(y_rstd, 1)
            ch = Chain(pool, val_step)
            pool.wait_ge(probs_ready, 1)
            ch.next(nc.gpsimd.tensor_copy(w_part[:, 0, :], score))
            ch.next(nc.gpsimd.tensor_tensor(w_left, score, w_part[:, 0, :], ALU.subtract))
            ch.next(nc.gpsimd.tensor_copy(w_part[:, 1, :], w_left))
            ch.next(nc.gpsimd.tensor_tensor(w_part[:, 2, :], w_left, w_part[:, 1, :], ALU.subtract))
            pool.wait_ge(ids, 5)
            pool.wait_ge(slots, 1)
            four = lambda v: v.unsqueeze(2).to_broadcast([128, TILES, 4])
            for e in range(EXPERTS):
                at = slice(TILES * e, TILES * e + TILES)
                s = e % 2
                if e >= 2:
                    pool.wait_ge(hot_used, e - 1)
                ch.mark(nc.gpsimd.tensor_tensor(vals[:, s, :, 0, :], here[:, at, :], p_id.unsqueeze(2).to_broadcast([128, TILES, 4]), ALU.mult))
                ch.mark(nc.gpsimd.tensor_tensor(vals[:, s, :, 1, :], here[:, at, :], four(t_id), ALU.mult))
                for v in range(2):
                    ch.mark(nc.gpsimd.tensor_tensor(vals[:, s, :, 2 + v, :], here[:, at, :], four(w_part[:, v, at]), ALU.mult))
                ch.wait()
                nc.gpsimd.tensor_tensor(vals[:, s, :, 4, :], here[:, at, :], four(w_part[:, 2, at]), ALU.mult).then_inc(vals_ready, 1)

        @block.tensor
        def _(pe):
            pe.wait_ge(small_in, 64)
            nc.tensor.transpose(c.bank(7)[:, 32:64], b1_nat[0:EXPERTS * CHUNKS, :],
                                c.ident[0:EXPERTS * CHUNKS, 0:EXPERTS * CHUNKS]).then_inc(turned, 1)
            pe.wait_ge(grouped, GROUPED)
            for n in range(ROUNDS):
                pe.wait_ge(counts, n + 1)
                nc.tensor.matmul(c.bank(1)[:, 0:TRIALS], member_bf, count_bf[:, 0:TRIALS], start=True, stop=True).then_inc(counted, 1)
            pe.wait_ge(limits, 1)
            nc.tensor.matmul(c.bank(1)[:, 64:64 + EXPERTS], c.ones, chosen_limit, start=True, stop=True).then_inc(counted, 1)
            pe.wait_ge(mask_done, 2)
            nc.tensor.matmul(c.bank(2)[:, 0:256], n_count.all, mask_a, start=True, stop=True)
            nc.tensor.matmul(c.bank(3)[:, 0:256], n_count.all, mask_b, start=True, stop=True)
            nc.tensor.matmul(c.bank(4)[:, 0:256], n_count.upto, mask_b, start=True, stop=True).then_inc(tallied, 1)
            pe.wait_ge(mask_done, 3)
            nc.tensor.matmul(c.bank(2)[:, 0:256], n_count.all, mask_a, start=True, stop=True)
            nc.tensor.matmul(c.bank(3)[:, 0:256], n_count.upto, mask_a, start=True, stop=True).then_inc(tallied, 1)
            for e in range(EXPERTS):
                pe.wait_ge(hot, e + 1)
                pe.wait_ge(vals_ready, e + 1)
                for t in range(TILES):
                    last = nc.tensor.matmul(c.bank(5)[:, 20 * e:20 * e + 20], one_hot[:, e % 2, t, :],
                                            vals[:, e % 2, t].rearrange("p v b -> p (v b)"), start=(t == 0), stop=(t == TILES - 1))
                last.then_inc(hot_used, 1)

        @block.scalar
        def _(act):
            act.wait_ge(turned, 1)
            act.wait_ge(step, 2)
            nc.scalar.activation(score, work, ACT.Exp).then_inc(expd, 1)
            act.wait_ge(turned, 1)
            nc.scalar.activation(b1T, c.bank(7)[:, 32:64], ACT.Copy)

        @block.vector
        def _(dve):
            ch = Chain(dve, step)
            tt, ts = nc.vector.tensor_tensor, nc.vector.tensor_scalar
            logits = c.gated[:, 0:256].rearrange("p (t e) -> p t e", e=EXPERTS)
            ch.next(nc.vector.tensor_reduce(best, logits, axis=AX.X, op=ALU.max))
            ch.next(tt(tiles_last(work), logits, per_tile(best), ALU.subtract))
            dve.wait_ge(expd, 1)
            ch.next(nc.vector.tensor_reduce(best, tiles_last(score), axis=AX.X, op=ALU.add))
            ch.next(nc.vector.reciprocal(best, best))
            tt(tiles_last(score), tiles_last(score), per_tile(best), ALU.mult).then_inc(probs_ready, 1)
            for t in range(TILES):
                nc.vector.bn_stats(c.stats[:, t, :], c.n[:, t, :]).then_inc(y_stats, 1)
            dve.wait_ge(y_stats, TILES)
            for t in range(TILES):
                nc.vector.bn_aggr(c.mv[:, t, :], c.stats[:, t, :]).then_inc(y_mv, 1)
            now = trial[:, 0:1]
            ch.next(nc.vector.memset(now, 0.0))
            dve.wait_ge(grouped, GROUPED)
            dve.wait_ge(spread, 16 * EXPERTS)
            for n in range(ROUNDS):
                ch.next(tt(cand.bitcast(I32), steps[:, n, :], now.bitcast(I32).to_broadcast([128, TRIALS]), ALU.bitwise_or))
                ch.next(tt(reach, flat.unsqueeze(1).to_broadcast([128, TRIALS, EXPERTS * TILES]),
                           cand.unsqueeze(2).to_broadcast([128, TRIALS, EXPERTS * TILES]), ALU.is_ge))
                with nc.allow_low_precision(reason="whole numbers up to 256"):
                    nc.vector.tensor_reduce(count_bf[:, 0:TRIALS], reach, axis=AX.X, op=ALU.add).then_inc(counts, 1)
                dve.wait_ge(counted, n + 1)
                ch.next(nc.vector.scalar_tensor_tensor(trial[:, 1:TRIALS + 1], c.bank(1)[:, 0:TRIALS], float(KEPT), cand,
                                                       op0=ALU.is_ge, op1=ALU.mult))
                ch.next(nc.vector.tensor_reduce(now, trial, axis=AX.X, op=ALU.max))
            nc.vector.tensor_scalar(chosen_limit, first, now, None, ALU.mult).then_inc(limits, 1)
            dve.wait_ge(y_rstd, 1)
            for t in range(TILES):
                ts(c.o[:, t, :], c.n[:, t, :], c.mv[:, t, 0:1], c.rstd[:, t:t + 1], ALU.subtract, ALU.mult).then_inc(yn_done, 1)
            dve.wait_ge(counted, ROUNDS + 1)
            ch.next(nc.vector.tensor_copy(limit, c.bank(1)[:, 64:64 + EXPERTS]))
            lim = over_tiles(limit)
            ch.next(tt(by_expert(above), by_expert(score), lim, ALU.is_gt))
            ch.next(tt(by_expert(equal), by_expert(score), lim, ALU.is_equal))
            nc.vector.tensor_copy(mask_a, above).then_inc(mask_done, 1)
            nc.vector.tensor_copy(mask_b, equal).then_inc(mask_done, 1)
            dve.wait_ge(tallied, 1)
            ch.next(nc.vector.tensor_reduce(count, by_expert(c.bank(2)[:, 0:256]), axis=AX.X, op=ALU.add))
            ch.next(ts(need, count, -1.0, float(KEPT), ALU.mult, ALU.add))
            ch.next(nc.vector.tensor_copy(total, c.bank(3)[:, 0:256]))
            ch.next(nc.vector.tensor_tensor_scan(place, n_count.goes_on, total, 0.0, op0=ALU.mult, op1=ALU.add))
            ch.next(tt(place, place, total, ALU.subtract))
            ch.next(tt(place, place, c.bank(4)[:, 0:256], ALU.add))
            ch.next(tt(by_expert(work), by_expert(place), over_tiles(need), ALU.is_le))
            ch.next(tt(work, work, equal, ALU.mult))
            ch.next(tt(chosen, work, above, ALU.add))
            nc.vector.tensor_copy(mask_a, chosen).then_inc(mask_done, 1)
            dve.wait_ge(tallied, 2)
            ch.next(nc.vector.tensor_copy(total, c.bank(2)[:, 0:256]))
            ch.next(nc.vector.memset(work, 1.0))
            ch.next(nc.vector.tensor_tensor_scan(place, work, total, 0.0, op0=ALU.mult, op1=ALU.add))
            ch.next(tt(place, place, total, ALU.subtract))
            ch.next(tt(place, place, c.bank(3)[:, 0:256], ALU.add))
            ch.next(tt(place, place, chosen, ALU.subtract))
            ch.next(nc.vector.tensor_copy(whole, place))
            ch.next(ts(cand_wide, whole, 127, None, ALU.bitwise_and))
            ch.next(nc.vector.tensor_copy(lane, cand_wide))
            ch.next(ts(whole, whole, 7, None, ALU.logical_shift_right))
            ch.next(nc.vector.tensor_copy(slot_tile, whole))
            dve.wait_ge(ids, 5)
            ch.next(tt(slot_tile, slot_tile, first_tile, ALU.subtract))
            tt(here, slot_tile.unsqueeze(2).to_broadcast([128, EXPERTS * TILES, 4]),
               iota4.unsqueeze(1).to_broadcast([128, EXPERTS * TILES, 4]), ALU.is_equal).then_inc(slots, 1)
            ch.next(ts(lane, lane, 1.0, None, ALU.add))
            ch.next(tt(lane, lane, chosen, ALU.mult))
            ch.next(ts(lane, lane, -1.0, None, ALU.add))
            for e in range(EXPERTS):
                at = slice(TILES * e, TILES * e + TILES)
                if e >= 2:
                    dve.wait_ge(hot_used, e - 1)
                tt(one_hot[:, e % 2], lane[:, at].unsqueeze(2).to_broadcast([128, TILES, 128]),
                   iota128.unsqueeze(1).to_broadcast([128, TILES, 128]), ALU.is_equal).then_inc(hot, 1)
            dve.wait_ge(hot_used, EXPERTS)
            ch.next(nc.vector.tensor_copy(found.rearrange("p e v b -> p (e v b)"), c.bank(5)[:, 0:20 * EXPERTS]))
            by_slot = lambda v: v.rearrange("p (e b) -> p e b", e=EXPERTS)
            ch.next(nc.vector.scalar_tensor_tensor(by_slot(work[:, 0:PICKS]), found[:, :, 1, :], 128.0, found[:, :, 0, :],
                                                   op0=ALU.mult, op1=ALU.add))
            ch.next(nc.vector.tensor_copy(idx, work[:, 0:PICKS]))
            ch.next(tt(by_slot(weight), found[:, :, 2, :], found[:, :, 3, :], ALU.add))
            ch.next(tt(by_slot(weight), by_slot(weight), found[:, :, 4, :], ALU.add))

    c.used = keep
    rows = c.take(TOK).rearrange("p (s c) -> p s c", c=D)
    fc1T = c.take(2 * FFN).rearrange("p (r f) -> p r f", r=2)
    fc2T = c.take(3 * FFN).rearrange("p (r k c) -> p r k c", r=3, k=CHUNKS)
    yT = c.take(2 * KEPT).rearrange("p (r s) -> p r s", r=2)
    hT = c.take(2 * CHUNKS * KEPT).rearrange("p (r k s) -> p r k s", r=2, k=CHUNKS)
    out = c.take(2 * KEPT).rearrange("p (r s c) -> p r s c", r=2, c=D)
    got = [sem(f"got{e}") for e in range(EXPERTS)]
    w1_turned, w2_turned, w1_done, w2_done, y_turned, yT_done = (sem(s) for s in (
        "w1_turned", "w2_turned", "w1_done", "w2_done", "y_turned", "yT_done"))
    h_made, h_done, o_made, o_done, added = (sem(s) for s in ("h_made", "h_done", "o_made", "o_done", "added"))
    with nc.Block() as block:
        @block.gpsimd
        def _(pool):
            for s in range(PICKS):
                pool.indirect_dma_start(rows[:, s, :], None, normed, bass.IndirectOffsetOnAxis(ap=idx[:, s:s + 1], axis=0),
                                        bounds_check=TOK - 1, oob_is_err=False).then_inc(got[s // PER_EXPERT], 16)
            for e in range(EXPERTS):
                pool.wait_ge(o_done, PER_EXPERT * (e + 1))
                if e >= 1:
                    pool.wait_ge(added, 16 * PER_EXPERT * e)
                for s in range(PER_EXPERT):
                    n = PER_EXPERT * e + s
                    pool.indirect_dma_start(result, bass.IndirectOffsetOnAxis(ap=idx[:, n:n + 1], axis=0), out[:, e % 2, s, :], None,
                                            bounds_check=TOK - 1, oob_is_err=True, compute_op=ALU.add).then_inc(added, 16)
            pool.wait_ge(added, 16 * PICKS)

        @block.tensor
        def _(pe):
            def prepare(e):
                if e >= 1:
                    pe.wait_ge(w1_done, e)
                    pe.wait_ge(w2_done, e)
                    pe.wait_ge(yT_done, e)
                for k in range(CHUNKS):
                    last = nc.tensor.transpose(c.bank(0)[:, 128 * k:128 * k + 128], fc1[:, e, k, :], c.ident)
                last.then_inc(w1_turned, 1)
                for k in range(CHUNKS):
                    last = nc.tensor.transpose(c.bank(1)[:, 128 * k:128 * k + 128], fc2[:, e, 128 * k:128 * k + 128], c.ident)
                last.then_inc(w2_turned, 1)
                pe.wait_ge(got[e], 16 * PER_EXPERT)
                for s in range(PER_EXPERT):
                    last = nc.tensor.transpose(c.bank(2)[:, 128 * s:128 * s + 128], rows[:, PER_EXPERT * e + s, :], c.ident)
                last.then_inc(y_turned, 1)

            def up(e):
                pe.wait_ge(w1_done, e + 1)
                pe.wait_ge(yT_done, e + 1)
                for k in range(CHUNKS):
                    n = CHUNKS * e + k
                    if n >= 3:
                        pe.wait_ge(h_done, n - 2)
                    nc.tensor.matmul(c.bank(3 + n % 3), fc1T[:, e % 2, 128 * k:128 * k + 128], yT[:, e % 2, :],
                                     start=True, stop=True).then_inc(h_made, 1)

            def down(e):
                pe.wait_ge(h_done, CHUNKS * e + CHUNKS)
                pe.wait_ge(w2_done, e + 1)
                if e >= 2:
                    pe.wait_ge(o_done, PER_EXPERT * (e - 1))
                for s in range(PER_EXPERT):
                    o = c.bank(6 + e % 2)[:, 128 * s:128 * s + 128]
                    for k in range(CHUNKS):
                        nc.tensor.matmul(o, hT[:, e % 2, k, 128 * s:128 * s + 128], fc2T[:, e % 3, k, :], start=(k == 0), stop=False)
                    last = nc.tensor.matmul(o, c.ones[0:1, :], b2[0:1, D * e:D * e + D], start=False, stop=True)
                last.then_inc(o_made, 1)

            prepare(0)
            for e in range(EXPERTS):
                if e + 1 < EXPERTS:
                    prepare(e + 1)
                up(e)
                if e >= 1:
                    down(e - 1)
            down(EXPERTS - 1)

        @block.scalar
        def _(act):
            def tokens(e):
                act.wait_ge(y_turned, e + 1)
                if e >= 2:
                    act.wait_ge(h_made, CHUNKS * (e - 1))
                nc.scalar.activation(yT[:, e % 2, :], c.bank(2), ACT.Identity, bias=lnb, scale=lnw).then_inc(yT_done, 1)

            tokens(0)
            for e in range(EXPERTS):
                if e + 1 < EXPERTS:
                    tokens(e + 1)
                for k in range(CHUNKS):
                    n = CHUNKS * e + k
                    act.wait_ge(h_made, n + 1)
                    if e >= 2:
                        act.wait_ge(o_made, e - 1)
                    nc.scalar.activation(hT[:, e % 2, k, :], c.bank(3 + n % 3), ACT.Gelu_apprx_tanh,
                                         bias=b1T[:, n:n + 1]).then_inc(h_done, 1)

        @block.vector
        def _(dve):
            def weights(e):
                dve.wait_ge(w1_turned, e + 1)
                if e >= 2:
                    dve.wait_ge(h_made, CHUNKS * (e - 1))
                nc.vector.tensor_copy(fc1T[:, e % 2, :], c.bank(0)).then_inc(w1_done, 1)
                dve.wait_ge(w2_turned, e + 1)
                if e >= 3:
                    dve.wait_ge(o_made, e - 2)
                nc.vector.tensor_copy(fc2T[:, e % 3].rearrange("p k c -> p (k c)"), c.bank(1)).then_inc(w2_done, 1)

            def output(e):
                dve.wait_ge(o_made, e + 1)
                if e >= 2:
                    dve.wait_ge(added, 16 * PER_EXPERT * (e - 1))
                for s in range(PER_EXPERT):
                    n = PER_EXPERT * e + s
                    nc.vector.tensor_scalar(out[:, e % 2, s, :], c.bank(6 + e % 2)[:, 128 * s:128 * s + 128],
                                            weight[:, n:n + 1], None, ALU.mult).then_inc(o_done, 1)

            weights(0)
            for e in range(EXPERTS):
                if e + 1 < EXPERTS:
                    weights(e + 1)
                if e >= 1:
                    output(e - 1)
            output(EXPERTS - 1)
    return result.rearrange("(t p) c -> p t c", p=128)


def project_heads(c, d):
    nc = c.nc
    sem = lambda name: c.sem(f"out_{name}")
    bias_in, turned, oT_done, made, added = (sem(s) for s in ("bias_in", "turned", "oT_done", "made", "added"))
    bias = c.take(D)
    oT = c.take(2 * S).rearrange("p (s t) -> p s t", s=2)
    with nc.Block() as block:
        @block.sync
        def _(sp):
            sp.dma_start(bias, d["L3_attn_bout"].partition_broadcast(128)).then_inc(bias_in, 16)

        @block.tensor
        def _(pe):
            def turn(b):
                if b >= 2:
                    pe.wait_ge(oT_done, b - 1)
                for k in range(TPB):
                    last = nc.tensor.transpose(c.bank(b % 2)[:, 128 * k:128 * k + 128], c.o[:, TPB * b + k, :], c.ident)
                last.then_inc(turned, 1)

            turn(0)
            for b in range(B):
                if b + 1 < B:
                    turn(b + 1)
                pe.wait_ge(oT_done, b + 1)
                if b >= 2:
                    pe.wait_ge(added, b - 1)
                for k in range(TPB):
                    last = nc.tensor.matmul(c.bank(2 + b % 2)[:, 128 * k:128 * k + 128], oT[:, b % 2, 128 * k:128 * k + 128],
                                            c.wT[:, W_OUT, :], start=True, stop=True)
                last.then_inc(made, 1)

        @block.scalar
        def _(act):
            for b in range(B):
                act.wait_ge(turned, b + 1)
                if b >= 2:
                    act.wait_ge(made, b - 1)
                nc.scalar.activation(oT[:, b % 2, :], c.bank(b % 2), ACT.Copy).then_inc(oT_done, 1)

        @block.vector
        def _(dve):
            dve.wait_ge(bias_in, 16)
            for b in range(B):
                dve.wait_ge(made, b + 1)
                nc.vector.tensor_tensor(c.o[:, TPB * b:TPB * b + TPB, :], c.bank(2 + b % 2).rearrange("p (t c) -> p t c", t=TPB),
                                        bias.unsqueeze(1).to_broadcast([128, TPB, D]), ALU.add).then_inc(added, 1)


MIX = 4


class MixtureInputs:

    def __init__(self, c):
        self.b1, self.b2 = c.take(128), c.take(MIX * D)
        self.wu, self.bu = c.take(1), c.take(1)
        self.w_switch, self.w_choice = c.take(EXPERTS), c.take(EXPERTS)
        self.below, self.share = c.take(MIX), c.take(MIX)
        self.loads = 8

    def load(self, eng, d, signal):
        eng.dma_start(self.w_switch, d["L1_ffn_w_switch"]).then_inc(signal, 16)
        eng.dma_start(self.w_choice, d["choice_gate"]).then_inc(signal, 16)
        eng.dma_start(self.wu, d["L3_ffn_Wu"]).then_inc(signal, 16)
        eng.dma_start(self.bu, d["L3_ffn_bu"].partition_broadcast(128)).then_inc(signal, 16)
        eng.dma_start(self.below, d["expert_below"]).then_inc(signal, 16)
        eng.dma_start(self.share, d["expert_share"]).then_inc(signal, 16)
        eng.dma_start(self.b2, d["L3_ffn_b2"].rearrange("e c -> (e c)").partition_broadcast(128)).then_inc(signal, 16)
        eng.dma_start(self.b1[0:MIX * CHUNKS, :], d["L3_ffn_b1"].rearrange("e (k p) -> (e k) p", p=128)).then_inc(signal, 16)


def elastic_mixture(c, d, small):
    nc = c.nc
    sem = lambda name: c.sem(f"mix_{name}")
    w1 = c.take(MIX * FFN).rearrange("p (e f) -> p e f", e=MIX)
    w2 = c.take(MIX * FFN).rearrange("p (e k c) -> p e k c", e=MIX, k=CHUNKS)
    b1T = c.take(MIX * CHUNKS)
    b1_nat, b2, bu, below, share = small.b1, small.b2, small.bu, small.below, small.share
    u, u4 = c.take(TILES), c.take(TILES)
    w = c.take(TILES * MIX).rearrange("p (t e) -> p t e", e=MIX)
    taken = c.take(TILES * MIX).rearrange("p (t e) -> p t e", e=MIX)
    hT = c.take(2 * CHUNKS * S).rearrange("p (s k t) -> p s k t", s=2, k=CHUNKS)
    w_now = c.take(2 * TPB * MIX).rearrange("p (s t e) -> p s t e", s=2, e=MIX)
    w1_in, w2_in = sem("w1_in"), sem("w2_in")
    u_done, step, b1_turned = sem("u_done"), sem("step"), sem("b1_turned")
    with nc.Block() as block:
        @block.sync
        def _(sp):
            sp.dma_start(w1, d["L3_ffn_W1"].rearrange("e c f -> c e f")).then_inc(w1_in, 16)
            sp.dma_start(w2, d["L3_ffn_W2"].rearrange("e (k p) c -> p e k c", p=128)).then_inc(w2_in, 16)
            sp.wait_ge(w1_in, 16)
            sp.wait_ge(w2_in, 16)

        @block.tensor
        def _(pe):
            nc.tensor.transpose(c.bank(1)[:, 0:MIX * CHUNKS], b1_nat[0:MIX * CHUNKS, :],
                                c.ident[0:MIX * CHUNKS, 0:MIX * CHUNKS]).then_inc(b1_turned, 1)

        @block.scalar
        def _(act):
            nc.scalar.activation(u, c.gated[:, 0:TILES], ACT.Sigmoid, bias=bu).then_inc(u_done, 1)
            act.wait_ge(b1_turned, 1)
            nc.scalar.activation(b1T, c.bank(1)[:, 0:MIX * CHUNKS], ACT.Copy)

        @block.vector
        def _(dve):
            ch = Chain(dve, step)
            dve.wait_ge(u_done, 1)
            wide = lambda v: v.unsqueeze(2).to_broadcast([128, TILES, MIX])
            each = lambda v: v.unsqueeze(1).to_broadcast([128, TILES, MIX])
            ch.next(nc.vector.tensor_scalar(u4, u, float(MIX), None, ALU.mult))
            ch.next(nc.vector.tensor_tensor(taken, wide(u4), each(below), ALU.is_gt))
            ch.next(nc.vector.tensor_tensor(w, wide(u), each(share), ALU.mult))
            ch.next(nc.vector.tensor_tensor(w, w, taken, ALU.mult))

    h_made, h_done, y_made, y_done, w_there, started = (sem(s) for s in ("h_made", "h_done", "y_made", "y_done", "w_there", "started"))
    H0, Y0, OUT0 = CHUNKS, 2, 2 * TPB
    with nc.Block() as block:
        def batches(eng, body):
            with eng.Fori(0, B - 1) as b:
                body(b, True)
            body(B - 1, False)

        @block.tensor
        def _(pe):
            def up(b, e, batch):
                for k in range(CHUNKS):
                    pe.wait_ge(h_done, 16 * b + 4 * e + k + 1 - CHUNKS + H0)
                    nc.tensor.matmul(c.bank(k), w1[:, e, 128 * k:128 * k + 128], batch, start=True, stop=True).then_inc(h_made, 1)

            def down(b, e):
                pe.wait_ge(h_done, 16 * b + 4 * e + CHUNKS + H0)
                pe.wait_ge(y_done, TPB * (4 * b + e - 1) + OUT0)
                for t in range(TPB):
                    for k in range(CHUNKS):
                        last = nc.tensor.matmul(c.bank(4 + e % 2)[:, 128 * t:128 * t + 128], hT[:, e % 2, k, 128 * t:128 * t + 128],
                                                w2[:, e, k, :], start=(k == 0), stop=(k == CHUNKS - 1))
                last.then_inc(y_made, 1)

            pe.sem_inc(y_made, Y0)
            up(0, 0, c.nT[:, 0, 1:S + 1])

            def body(b, more):
                now = c.nT[:, bass.ds(b, 1), 1:S + 1].rearrange("p o s -> p (o s)")
                for e in range(1, MIX):
                    up(b, e, now)
                    down(b, e - 1)
                if more:
                    up(b + 1, 0, c.nT[:, bass.ds(b + 1, 1), 1:S + 1].rearrange("p o s -> p (o s)"))
                down(b, MIX - 1)

            batches(pe, body)

        @block.scalar
        def _(act):
            act.sem_inc(h_done, H0)

            def body(b, more):
                for e in range(MIX):
                    act.wait_ge(y_made, 4 * b + e - 1 + Y0)
                    for k in range(CHUNKS):
                        act.wait_ge(h_made, 16 * b + 4 * e + k + 1)
                        nc.scalar.activation(hT[:, e % 2, k, :], c.bank(k), ACT.Relu,
                                             bias=b1T[:, CHUNKS * e + k:CHUNKS * e + k + 1]).then_inc(h_done, 1)

            batches(act, body)

        @block.vector
        def _(dve):
            dve.sem_inc(y_done, OUT0)

            def body(b, more):
                dve.wait_ge(y_done, 16 * b + OUT0)
                nc.vector.tensor_copy(w_now[:, 0], w[:, bass.ds(b * TPB, TPB), :]).then_inc(w_there, 1)
                dve.wait_ge(w_there, b + 1)
                tile = lambda t: c.o[:, bass.ds(b * TPB + t, 1), :].rearrange("p o c -> p (o c)")
                for e in range(MIX):
                    bias = b2[:, D * e:D * e + D]
                    if e >= 1:
                        dve.wait_ge(started, 16 * b + 4 * e)
                    for t in range(TPB):
                        if e == 0:
                            ins = nc.vector.tensor_scalar(tile(t), bias, w_now[:, 0, t, 0:1], None, ALU.mult)
                        else:
                            ins = nc.vector.scalar_tensor_tensor(tile(t), bias, w_now[:, 0, t, e:e + 1], tile(t),
                                                                 op0=ALU.mult, op1=ALU.add)
                        ins.then_inc(started, 1)
                dve.wait_ge(started, 16 * b + 16)
                for e in range(MIX):
                    dve.wait_ge(y_made, 4 * b + e + 1 + Y0)
                    dve.wait_ge(y_done, 16 * b + 4 * e + OUT0)
                    for t in range(TPB):
                        nc.vector.scalar_tensor_tensor(tile(t), c.bank(4 + e % 2)[:, 128 * t:128 * t + 128], w_now[:, 0, t, e:e + 1], tile(t),
                                                       op0=ALU.mult, op1=ALU.add).then_inc(y_done, 1)

            batches(dve, body)


def shape_constants():
    import numpy as np
    half = HD // 2
    freq = (1.0 / np.float32(10000.0) ** (np.arange(0, HD, 2, dtype=np.float32) / np.float32(HD))).astype(np.float32)
    angle = np.outer(np.arange(S, dtype=np.float32), freq)
    row = np.arange(128)
    width = row // 4 % HD
    sign = np.where(width < half, -1.0, 1.0).astype(np.float32)
    select = np.zeros((128, 36), np.float32)
    for g in range(4):
        for r in range(HD):
            select[32 * g + r, HD * g + r] = 1.0
        select[32 * g + HD, 4 * HD + g] = 1.0
    number = (np.arange(4)[None, :] - row[:, None]) % 4 + 1
    return {"rope_cos": np.cos(angle).astype(np.float32).T[width % half].copy(),
            "rope_sin": (np.sin(angle).astype(np.float32).T[width % half] * sign[:, None]).astype(np.float32),
            "select_rows": select,
            "expert_below": np.where(number == 1, -1.0, number - 1.0).astype(np.float32),
            "expert_share": (1.0 / number).astype(np.float32)}


def laid_out(inputs):
    import numpy as np
    bias = np.asarray(inputs["L3_attn_bqkv"])[0:2 * D].reshape(2, 4, 4, 2, HD // 2)
    columns = [b.transpose(0, 1, 3, 4, 2).reshape(2, D) for b in (bias, bias[:, :, :, ::-1, :])]
    return {"qk_bias": np.concatenate(columns).T, "choice_gate": np.asarray(inputs["L2_ffn_gate_w"]).T}


class RotaryTables:

    def __init__(self, c):
        self.qk_bias = c.take(4)
        self.v_bias = c.take(D)
        self.cos, self.sin = c.take(S), c.take(S)
        self.select = c.take(36)
        self.loads = 5

    def load(self, eng, d, signal):
        eng.dma_start(self.qk_bias, d["qk_bias"]).then_inc(signal, 16)
        eng.dma_start(self.v_bias, d["L3_attn_bqkv"][2 * D:3 * D].partition_broadcast(128)).then_inc(signal, 16)
        eng.dma_start(self.cos, d["rope_cos"]).then_inc(signal, 16)
        eng.dma_start(self.sin, d["rope_sin"]).then_inc(signal, 16)
        eng.dma_start(self.select, d["select_rows"]).then_inc(signal, 16)


def rotary_attention(c, d, tables):
    a = Attention(c, "L3", by_tokens=False, scale=float(HD) ** -0.5)
    keep = c.used
    attention_operands(c, a, W_QKV3, tables)
    c.used = keep
    attention(c, a, tables.select)
    c.free_work()
    project_heads(c, d)


def reshaped_attention(c):
    a = Attention(c, "L0", by_tokens=True, scale=1.0)
    keep = c.used
    attention_operands(c, a, W_Q0)
    c.used = keep
    attention(c, a)


MANY = 80


def program(nc, d, out):
    with ExitStack() as ctx:
        c = Core(nc, ctx)
        counting, rotary, mixture = Counting(c), RotaryTables(c), MixtureInputs(c)
        c.base = c.used

        def stage(run, *args, **kw):
            c.free_work()
            result = run(c, *args, **kw)
            if len(c.sems) > MANY:
                c.end_stage()
            return result

        stage(setup, d, counting, (rotary, mixture))
        stage(norms, "norm0", after_layer=False)
        stage(reshaped_attention)
        stage(norms, "norm1", after_layer=True, scale_of_batch=True)
        stage(channel_mix, d)
        stage(norms, "norm2", after_layer=True)
        stage(test_time_learner, d)
        stage(norms, "norm3", after_layer=True, gate=mixture.w_switch)
        fetch = stage(switch_layer, d, counting)
        stage(norms, "norm4", after_layer=True, fetch=fetch)
        stage(linear_attention, d)
        stage(norms, "norm5", after_layer=True, gate=mixture.w_choice)
        chosen_sums = stage(expert_choice, d, counting)
        stage(norms, "norm6", after_layer=True, reload=chosen_sums)
        stage(rotary_attention, d, rotary)
        stage(norms, "norm7", after_layer=True, gate=mixture.wu)
        stage(elastic_mixture, d, mixture)
        stage(norms, "norm8", after_layer=True, x_norm=False, out=out)


def kernel(**inputs):
    import numpy as _np
    import concourse.bacc as _bacc
    from concourse import mybir as _mybir
    from concourse.bass_utils import run_bass_kernel_spmd as _run

    nc = _bacc.Bacc("TRN2", target_bir_lowering=False, num_devices=1)
    arrays, d = {}, {}
    for name, a in list(inputs.items()) + list(laid_out(inputs).items()) + list(shape_constants().items()):
        a = _np.ascontiguousarray(a)
        arrays[f"in_{name}"] = a
        d[name] = nc.dram_tensor(f"in_{name}", a.shape, _mybir.dt.from_np(a.dtype), kind="ExternalInput").ap()
    out = nc.dram_tensor("out_0", (B, S, D), F32, kind="ExternalOutput").ap()
    program(nc, d, out)
    return _run(nc, [arrays], core_ids=[0]).results[0]["out_0"]
```
